# Optimizing a Trainium2 kernel written in Bass

```python
import numpy as np
import jax
import jax.numpy as jnp

def _softmax(x, axis=-1):
    return jax.nn.softmax(x, axis=axis)

def _gelu(x):
    return jax.nn.gelu(x, approximate=True)

def _silu(x):
    return jax.nn.silu(x)

def _sigmoid(x):
    return jax.nn.sigmoid(x)

def _layernorm(x, axis=-1, eps=1e-05):
    m = jnp.mean(x, axis=axis, keepdims=True)
    v = jnp.var(x, axis=axis, keepdims=True)
    return (x - m) / jnp.sqrt(v + eps)

def _scatter_add(tgt, idx, src, axis=0):
    return tgt.at[idx].add(src)

def _segment_sum(src, seg, n):
    return jax.ops.segment_sum(src, seg, n)
kernel_name = 'mk_audio_tower_d1_tok_audfeat1024_r4_dab1db'

def setup_inputs(seed: int=0):
    np.random.seed(seed)
    _w = jnp.asarray

    def _rec_inputs():
        import jax
        import jax.numpy as jnp
        _rk = jax.random.key(seed)
        x = -0.000125008 + 0.999885 * jax.random.normal(jax.random.fold_in(_rk, 1), (16, 128, 750), jnp.float32)
        return x
    x = _rec_inputs()

    def _L0_tok_setup():
        import jax, jax.numpy as jnp
        import numpy as np
        from jax import lax
        ALPHA = 0.1
        B, C_IN, T, D_MODEL = (32, 128, 512, 256)

        def _ewma_scan(xt):

            def step(carry, xi):
                carry = ALPHA * xi + (1.0 - ALPHA) * carry
                return (carry, carry)
            _, ys = lax.scan(step, xt[0], xt[1:])
            return jnp.concatenate([xt[:1], ys], axis=0)
        key = jax.random.key(seed)
        k_x, k_w, k_b = jax.random.split(key, 3)
        x = jax.random.normal(k_x, (B, C_IN, T), dtype=jnp.float32)
        bound = 1.0 / np.sqrt(C_IN)
        W = jax.random.uniform(k_w, (D_MODEL, C_IN), dtype=jnp.float32, minval=-bound, maxval=bound)
        b = jax.random.uniform(k_b, (D_MODEL,), dtype=jnp.float32, minval=-bound, maxval=bound)
        return {'x': x, 'W': W, 'b': b}
    _L0_tok_all = _L0_tok_setup()
    _L0_tok_in = {k: v for k, v in _L0_tok_all.items() if k in ('W', 'b')}
    del _L0_tok_all

    def _L0_attn_setup():
        import jax, jax.numpy as jnp
        import numpy as np
        DEPTH = 2
        DIM = 256
        SDIM = 64
        B = 64
        S = 64
        EPS = 1e-05

        def _run_selective_scan(x, Wd, bd, Wi, bi, A_log, Wo, bo):
            delta = jax.nn.softplus(jnp.einsum('bsd,dn->bsn', x, Wd) + bd)
            u = jnp.einsum('bsd,dn->bsn', x, Wi) + bi
            decay = jnp.exp(-delta * jax.nn.softplus(A_log))
            drive = delta * u

            def step(h, t):
                d, g = t
                h = d * h + g
                return (h, h)
            h0 = jnp.zeros((x.shape[0], Wd.shape[1]), x.dtype)
            final, hs = jax.lax.scan(step, h0, (decay.swapaxes(0, 1), drive.swapaxes(0, 1)))
            hs = hs.swapaxes(0, 1)
            y = jnp.einsum('bsn,nd->bsd', hs, Wo) + bo
            return (y, final)

        def _reference_tuple_inner(shot_embeddings, Wd, bd, Wi, bi, A_log, Wo, bo, Ws, bs, gamma, beta):
            hidden = shot_embeddings
            class_state = None
            for l in range(Wd.shape[0]):
                hidden, state = _run_selective_scan(hidden, Wd[l], bd[l], Wi[l], bi[l], A_log[l], Wo[l], bo[l])
                class_state = jnp.einsum('bn,nd->bd', state, Ws[l]) + bs[l]
                hidden = hidden + class_state[:, None, :]
            pooled = class_state + hidden.mean(axis=1)
            mu = pooled.mean(axis=-1, keepdims=True)
            var = pooled.var(axis=-1, keepdims=True)
            class_repr = (pooled - mu) / jnp.sqrt(var + EPS) * gamma + beta
            return (class_repr, hidden)
        key = jax.random.key(seed)
        ks = jax.random.split(key, 10)
        sc = 0.02
        return {'shot_embeddings': jax.random.normal(ks[0], (B, S, DIM), jnp.float32), 'Wd': jax.random.normal(ks[1], (DEPTH, DIM, SDIM), jnp.float32) * sc, 'bd': jnp.zeros((DEPTH, SDIM), jnp.float32), 'Wi': jax.random.normal(ks[2], (DEPTH, DIM, SDIM), jnp.float32) * sc, 'bi': jnp.zeros((DEPTH, SDIM), jnp.float32), 'A_log': jax.random.normal(ks[3], (DEPTH, SDIM), jnp.float32), 'Wo': jax.random.normal(ks[4], (DEPTH, SDIM, DIM), jnp.float32) * sc, 'bo': jnp.zeros((DEPTH, DIM), jnp.float32), 'Ws': jax.random.normal(ks[5], (DEPTH, SDIM, DIM), jnp.float32) * sc, 'bs': jnp.zeros((DEPTH, DIM), jnp.float32), 'gamma': jnp.ones((DIM,), jnp.float32), 'beta': jnp.zeros((DIM,), jnp.float32)}
    _L0_attn_all = _L0_attn_setup()
    _L0_attn_in = {k: v for k, v in _L0_attn_all.items() if k in ('Wd', 'bd', 'Wi', 'bi', 'A_log', 'Wo', 'bo', 'Ws', 'bs', 'gamma', 'beta')}
    del _L0_attn_all

    def _L0_ffn_setup():
        import jax, jax.numpy as jnp
        import numpy as np
        E = 16
        G = 4
        EPG = E // G
        K = 4
        TOPK_GROUP = 2
        PER_GROUP_K = K // TOPK_GROUP

        def _route(xf, router_w, correction_bias):
            S = xf.shape[0]
            logits = xf @ router_w.T
            scores = jax.nn.sigmoid(logits)
            sb = scores + correction_bias
            grp_top = jax.lax.top_k(sb.reshape(S, G, EPG), PER_GROUP_K)[0]
            group_scores = grp_top.sum(axis=-1)
            _, group_idx = jax.lax.top_k(group_scores, TOPK_GROUP)
            group_mask = jnp.zeros((S, G), sb.dtype).at[jnp.arange(S)[:, None], group_idx].set(1.0)
            score_mask = jnp.broadcast_to(group_mask[:, :, None], (S, G, EPG)).reshape(S, E)
            masked = jnp.where(score_mask > 0, sb, -jnp.inf)
            _, topk_idx = jax.lax.top_k(masked, K)
            w = jnp.take_along_axis(scores, topk_idx, axis=1)
            w = w / (w.sum(axis=-1, keepdims=True) + 1e-20)
            return (topk_idx, w, scores)
        key = jax.random.key(seed)
        ks = jax.random.split(key, 9)
        B, T, C, H, HS = (2, 256, 256, 64, 512)
        std = 0.02
        return {'x': jax.random.normal(ks[0], (B, T, C), jnp.float32), 'router_w': jax.random.normal(ks[1], (E, C), jnp.float32) * std, 'correction_bias': jnp.zeros((E,), jnp.float32), 'gate_w': jax.random.normal(ks[2], (E, C, H), jnp.float32) * std, 'up_w': jax.random.normal(ks[3], (E, C, H), jnp.float32) * std, 'down_w': jax.random.normal(ks[4], (E, H, C), jnp.float32) * std, 'shared_gate_w': jax.random.normal(ks[5], (HS, C), jnp.float32) * std, 'shared_up_w': jax.random.normal(ks[6], (HS, C), jnp.float32) * std, 'shared_down_w': jax.random.normal(ks[7], (C, HS), jnp.float32) * std}
    _L0_ffn_all = _L0_ffn_setup()
    _L0_ffn_in = {k: v for k, v in _L0_ffn_all.items() if k in ('router_w', 'correction_bias', 'gate_w', 'up_w', 'down_w', 'shared_gate_w', 'shared_up_w', 'shared_down_w')}
    del _L0_ffn_all
    return {'x': x, 'L0_tok_W': _L0_tok_in['W'], 'L0_tok_b': _L0_tok_in['b'], 'L0_attn_Wd': _L0_attn_in['Wd'], 'L0_attn_bd': _L0_attn_in['bd'], 'L0_attn_Wi': _L0_attn_in['Wi'], 'L0_attn_bi': _L0_attn_in['bi'], 'L0_attn_A_log': _L0_attn_in['A_log'], 'L0_attn_Wo': _L0_attn_in['Wo'], 'L0_attn_bo': _L0_attn_in['bo'], 'L0_attn_Ws': _L0_attn_in['Ws'], 'L0_attn_bs': _L0_attn_in['bs'], 'L0_attn_gamma': _L0_attn_in['gamma'], 'L0_attn_beta': _L0_attn_in['beta'], 'L0_ffn_router_w': _L0_ffn_in['router_w'], 'L0_ffn_correction_bias': _L0_ffn_in['correction_bias'], 'L0_ffn_gate_w': _L0_ffn_in['gate_w'], 'L0_ffn_up_w': _L0_ffn_in['up_w'], 'L0_ffn_down_w': _L0_ffn_in['down_w'], 'L0_ffn_shared_gate_w': _L0_ffn_in['shared_gate_w'], 'L0_ffn_shared_up_w': _L0_ffn_in['shared_up_w'], 'L0_ffn_shared_down_w': _L0_ffn_in['shared_down_w']}

def reference(x, L0_tok_W, L0_tok_b, L0_attn_Wd, L0_attn_bd, L0_attn_Wi, L0_attn_bi, L0_attn_A_log, L0_attn_Wo, L0_attn_bo, L0_attn_Ws, L0_attn_bs, L0_attn_gamma, L0_attn_beta, L0_ffn_router_w, L0_ffn_correction_bias, L0_ffn_gate_w, L0_ffn_up_w, L0_ffn_down_w, L0_ffn_shared_gate_w, L0_ffn_shared_up_w, L0_ffn_shared_down_w):
    import jax
    import jax.numpy as jnp

    def _L0_tok_ref(x, W, b):
        import jax, jax.numpy as jnp
        import numpy as np
        from jax import lax
        ALPHA = 0.1
        B, C_IN, T, D_MODEL = (32, 128, 512, 256)

        def _ewma_scan(xt):

            def step(carry, xi):
                carry = ALPHA * xi + (1.0 - ALPHA) * carry
                return (carry, carry)
            _, ys = lax.scan(step, xt[0], xt[1:])
            return jnp.concatenate([xt[:1], ys], axis=0)
        xp = jnp.transpose(x, (0, 2, 1))
        xt = jnp.moveaxis(xp, 1, 0)
        fwd = _ewma_scan(xt)
        bwd = _ewma_scan(xt[::-1])[::-1]
        ewma = jnp.moveaxis((fwd + bwd) * 0.5, 0, 1)
        return jnp.einsum('btc,dc->btd', ewma, W) + b

    def _L0_attn_ref(shot_embeddings, Wd, bd, Wi, bi, A_log, Wo, bo, Ws, bs, gamma, beta):
        import jax, jax.numpy as jnp
        import numpy as np
        DEPTH = 2
        DIM = 256
        SDIM = 64
        B = 64
        S = 64
        EPS = 1e-05

        def _run_selective_scan(x, Wd, bd, Wi, bi, A_log, Wo, bo):
            delta = jax.nn.softplus(jnp.einsum('bsd,dn->bsn', x, Wd) + bd)
            u = jnp.einsum('bsd,dn->bsn', x, Wi) + bi
            decay = jnp.exp(-delta * jax.nn.softplus(A_log))
            drive = delta * u

            def step(h, t):
                d, g = t
                h = d * h + g
                return (h, h)
            h0 = jnp.zeros((x.shape[0], Wd.shape[1]), x.dtype)
            final, hs = jax.lax.scan(step, h0, (decay.swapaxes(0, 1), drive.swapaxes(0, 1)))
            hs = hs.swapaxes(0, 1)
            y = jnp.einsum('bsn,nd->bsd', hs, Wo) + bo
            return (y, final)

        def _reference_tuple_inner(shot_embeddings, Wd, bd, Wi, bi, A_log, Wo, bo, Ws, bs, gamma, beta):
            hidden = shot_embeddings
            class_state = None
            for l in range(Wd.shape[0]):
                hidden, state = _run_selective_scan(hidden, Wd[l], bd[l], Wi[l], bi[l], A_log[l], Wo[l], bo[l])
                class_state = jnp.einsum('bn,nd->bd', state, Ws[l]) + bs[l]
                hidden = hidden + class_state[:, None, :]
            pooled = class_state + hidden.mean(axis=1)
            mu = pooled.mean(axis=-1, keepdims=True)
            var = pooled.var(axis=-1, keepdims=True)
            class_repr = (pooled - mu) / jnp.sqrt(var + EPS) * gamma + beta
            return (class_repr, hidden)
        return _reference_tuple_inner(shot_embeddings, Wd, bd, Wi, bi, A_log, Wo, bo, Ws, bs, gamma, beta)[1]

    def _L0_ffn_ref(x, router_w, correction_bias, gate_w, up_w, down_w, shared_gate_w, shared_up_w, shared_down_w):
        import jax, jax.numpy as jnp
        import numpy as np
        E = 16
        G = 4
        EPG = E // G
        K = 4
        TOPK_GROUP = 2
        PER_GROUP_K = K // TOPK_GROUP

        def _route(xf, router_w, correction_bias):
            S = xf.shape[0]
            logits = xf @ router_w.T
            scores = jax.nn.sigmoid(logits)
            sb = scores + correction_bias
            grp_top = jax.lax.top_k(sb.reshape(S, G, EPG), PER_GROUP_K)[0]
            group_scores = grp_top.sum(axis=-1)
            _, group_idx = jax.lax.top_k(group_scores, TOPK_GROUP)
            group_mask = jnp.zeros((S, G), sb.dtype).at[jnp.arange(S)[:, None], group_idx].set(1.0)
            score_mask = jnp.broadcast_to(group_mask[:, :, None], (S, G, EPG)).reshape(S, E)
            masked = jnp.where(score_mask > 0, sb, -jnp.inf)
            _, topk_idx = jax.lax.top_k(masked, K)
            w = jnp.take_along_axis(scores, topk_idx, axis=1)
            w = w / (w.sum(axis=-1, keepdims=True) + 1e-20)
            return (topk_idx, w, scores)
        B, T, C = x.shape
        S = B * T
        xf = x.reshape(S, C)
        sg = xf @ shared_gate_w.T
        su = xf @ shared_up_w.T
        shared_out = jax.nn.silu(sg) * su @ shared_down_w.T
        topk_idx, w, _scores = _route(xf, router_w, correction_bias)
        combine = jnp.zeros((S, E), xf.dtype).at[jnp.arange(S)[:, None], topk_idx].add(w)
        g = jnp.einsum('sc,ech->esh', xf, gate_w)
        u = jnp.einsum('sc,ech->esh', xf, up_w)
        h = jax.nn.silu(g) * u
        hw = h * combine.T[:, :, None]
        routed = jnp.einsum('esh,ehc->sc', hw, down_w)
        return (shared_out + routed).reshape(B, T, C)
    h = _L0_tok_ref(x, L0_tok_W, L0_tok_b)
    h = h + _L0_attn_ref(_layernorm(h, axis=-1), L0_attn_Wd, L0_attn_bd, L0_attn_Wi, L0_attn_bi, L0_attn_A_log, L0_attn_Wo, L0_attn_bo, L0_attn_Ws, L0_attn_bs, L0_attn_gamma, L0_attn_beta)
    h = h + _L0_ffn_ref(_layernorm(h, axis=-1), L0_ffn_router_w, L0_ffn_correction_bias, L0_ffn_gate_w, L0_ffn_up_w, L0_ffn_down_w, L0_ffn_shared_gate_w, L0_ffn_shared_up_w, L0_ffn_shared_down_w)
    return h

_drawn_inputs = setup_inputs


def setup_inputs(seed=0):
    import zlib

    import numpy as np

    out = dict(_drawn_inputs(seed))
    spreads = {'L0_attn_bd': (0.0, 0.8),
     'L0_attn_bi': (0.0, 0.1),
     'L0_attn_bo': (0.0, 0.1),
     'L0_attn_bs': (0.0, 0.1),
     'L0_attn_gamma': (1.0, 0.2),
     'L0_attn_beta': (0.0, 0.1),
     'L0_ffn_correction_bias': (0.0, 0.376)}
    factors = {'L0_ffn_router_w': 3.581, 'L0_ffn_up_w': 2.707, 'L0_ffn_down_w': 2.709}
    for name, (base, spread) in spreads.items():
        noise = np.random.default_rng([zlib.crc32(name.encode()), seed]).standard_normal(out[name].shape)
        drawn = base * np.exp(spread * noise) if base else spread * noise
        out[name] = jnp.asarray(drawn.astype(out[name].dtype))
    for name, factor in factors.items():
        out[name] = (out[name] * factor).astype(out[name].dtype)
    return out
```

```python
from contextlib import ExitStack

import concourse.bass as bass
from concourse import mybir

F32 = mybir.dt.float32
F32R = mybir.dt.float32r
ALU = mybir.AluOpType
ACT = mybir.ActivationFunctionType
AX = mybir.AxisListType

CHAIN = {
    0.0: [(0, "y", (1, 0))],
    0.5: [(0, "y", (1, 1)), (1, "ewma", 0)],
    1.0: [(0, "ln2_stats", 1)],
    1.5: [(1, "ewma", 1)],
    2.0: [(0, "ln2_norm", 1), (1, "tok", 0)],
    2.5: [(1, "tok", 1)],
    3.0: [(0, "x2t", (1, 0))],
    3.5: [(0, "x2t", (1, 1)), (1, "ln1_stats", 0)],
    4.0: [(0, "logit", 1)],
    4.5: [(0, "logit_t", 1)],
    5.0: [(0, "route_scores", 1), (1, "tok", 2)],
    5.5: [(1, "tok", 3), (1, "ln1_norm", 0)],
    6.0: [(0, "route_groups", 1), (0, "y", (2, 0))],
    6.5: [(0, "y", (2, 1))],
    7.0: [(0, "route_pick", 1), (1, "x1t", (0, 0))],
    7.5: [(1, "x1t", (0, 1)), (1, "ln1_stats", 1)],
    8.0: [(0, "route_weights", 1), (1, "tok", 4)],
    8.5: [(1, "ln1_norm", 1), (1, "tok", 5)],
    9.0: [(0, "comb_t", 1)],
    9.5: [(1, "pre", (0, 0))],
    10.0: [(1, "x1t", (1, 0)), (1, "ln1_stats", 2)],
    10.5: [(1, "x1t", (1, 1))],
    11.0: [(1, "ln1_norm", 2)],
    11.5: [(1, "pre", (0, 1))],

    12.0: [(0, "ln2_stats", 2)],
    12.5: [(1, "x1t", (2, 0))],
    13.0: [(1, "x1t", (2, 1)), (0, "ln2_norm", 2)],
    13.5: [(1, "pre", (0, 2))],
    14.0: [(0, "x2t", (2, 0)), (1, "ssm_log", 0)],
    14.5: [(0, "x2t", (2, 1))],
    15.0: [(0, "logit", 2)],
    15.5: [(0, "logit_t", 2)],
    16.0: [(1, "ssm_decay", 0)],
    16.5: [(0, "route_scores", 2)],
    17.0: [(1, "ssm_scan", 0)],
    18.0: [(1, "carry", 0), (0, "route_groups", 2)],
    18.5: [(1, "pre", (1, 0))],
    19.0: [(1, "pre", (1, 1))],
    19.5: [(1, "pre", (1, 2))],
    20.0: [(0, "route_pick", 2), (1, "ssm_log", 1)],
    21.0: [(0, "route_weights", 2)],
    21.5: [(0, "comb_t", 2)],
    22.0: [(1, "ssm_decay", 1)],
    23.0: [(1, "ssm_scan", 1)],
    23.5: [(1, "last_state", 0)],

    24.0: [(1, "class_row", 0)],
    24.5: [(1, "residual", 0)],
    25.0: [(1, "residual", 1)],
    25.5: [(1, "residual", 2)],
    26.0: [(1, "y", (0, 0)), (1, "residual", 3)],
    26.5: [(1, "y", (0, 1))],
    27.0: [(1, "ln2_stats", 0), (1, "residual", 4)],
    28.0: [(1, "ln2_norm", 0), (1, "residual", 5)],
    29.0: [(1, "x2t", (0, 0))],
    29.5: [(1, "x2t", (0, 1))],
    30.0: [(1, "logit", 0)],
    30.5: [(1, "logit_t", 0)],
    31.0: [(1, "route_scores", 0)],
    32.0: [(1, "route_groups", 0)],
    33.0: [(1, "route_pick", 0)],
    34.0: [(1, "route_weights", 0)],
    35.0: [(1, "comb_t", 0)],
}


def audio_tower_kernel(nc, x, tok_w, tok_b, wd, bd, wi, bi, a_log, wo, bo, ws, bs, router_w, corr_bias,
                       gate_w, up_w, down_w, sh_gate_w, sh_up_w, sh_down_w, out):
    B, C, T = x.shape
    D = tok_w.shape[0]
    N = wd.shape[2]
    E, _, H = gate_w.shape
    HS = sh_gate_w.shape[0]
    P = 128
    NP = B // 2
    TT = 500
    NT = 2 * T // TT
    TP = 125
    SUB = TT // TP
    NJ = NT * SUB
    KD = D // P
    MS = HS // P
    MR = E * H // P
    M = MS + MR
    NG, EG = 4, E // 4
    SLOTS = NT * M
    ALPHA = 0.1
    EPS = 1e-5
    BIG = 3e38
    assert C == P and D == 2 * P and 2 * N == P and 2 * H == P and 2 * T == NT * TT and M == 12

    with ExitStack() as ctx:
        def sb(name, shape, dt=F32):
            return ctx.enter_context(nc.sbuf_tensor(name, shape, dt))

        def ps(name, shape):
            return ctx.enter_context(nc.psum_tensor(name, shape, F32))

        def sem(name):
            return ctx.enter_context(nc.semaphore(name))

        gate_hi, gate_lo = (sb(f"gate_{s}", [P, KD, M * P], F32R) for s in ("hi", "lo"))
        up_hi, up_lo = (sb(f"up_{s}", [P, KD, M * P], F32R) for s in ("hi", "lo"))
        down_hi, down_lo = (sb(f"down_{s}", [P, M, D], F32R) for s in ("hi", "lo"))
        stage = sb("stage", [P, 2 * NJ * D])
        h_tok = stage[0:TP, 0:NJ * D].rearrange("p (j d) -> p j d", d=D)
        h2 = stage[0:TP, NJ * D:2 * NJ * D].rearrange("p (j d) -> p j d", d=D)
        x_in = sb("x_in", [P, 2, T])
        ew = sb("ew", [P, 2, T])
        ends10 = sb("ends10", [P, 2, 2])
        xn1 = sb("xn1", [TP, SUB, D])
        xn2 = sb("xn2", [TP, SUB, D])
        x1T = sb("x1T", [P, KD, TT])
        x2T = sb("x2T", [P, KD, TT])
        x_hi = sb("x_hi", [P, NT, KD, TT], F32R)
        x_lo = sb("x_lo", [P, NT, KD, TT], F32R)
        zt = sb("zt", [P, T])
        ut = sb("ut", [P, T])
        t1 = sb("t1", [P, T])
        t2 = sb("t2", [P, T])
        hs1 = sb("hs1", [P, T])
        blocks = sb("blocks", [P, 4, TT])
        sg, hid = blocks[:, 0:2, :], blocks[:, 2:4, :]
        hid_hi = sb("hid_hi", [P, 2, TT], F32R)
        hid_lo = sb("hid_lo", [P, 2, TT], F32R)
        combT = sb("combT", [P, NT, TT], F32R)
        ident = sb("ident", [P, P])
        sel = sb("sel", [P, MR, P], F32R)
        tokwT = sb("tokwT", [P, D])
        wdi0 = sb("wdi0", [P, 2, KD, P])
        g1 = sb("g1", [P, 2, P])
        sbd = sb("sbd", [P, 2, P])
        wo1 = sb("wo1", [P, 2, D])
        ws1 = sb("ws1", [P, 2, D])
        tokb_bc = sb("tokb_bc", [TP, D])
        brow = sb("brow", [TP, 2, D])
        rows = sb("rows", [TP, 2, D])
        last_bc = sb("last_bc", [P, TP])
        rw_hi = sb("rw_hi", [P, KD, E], F32R)
        rw_lo = sb("rw_lo", [P, KD, E], F32R)
        corr_bc = sb("corr_bc", [TP, E])
        vecs = sb("vecs", [P, 6])
        nspa = sb("nspa", [P, 2])
        spt = sb("spt", [P, 4])
        bias1 = sb("bias1", [P, 2])
        bias1s = sb("bias1s", [P, 2])
        c09 = sb("c09", [P, 1])
        mhalf = sb("mhalf", [TP, SUB])
        stats = [sb(f"stats{n}", [TP, SUB, 6]) for n in (1, 2)]
        halves = [sb(f"halves{n}", [TP, SUB, 2]) for n in (1, 2)]
        mv = [sb(f"mv{n}", [TP, SUB, 2]) for n in (1, 2)]
        rstd = [sb(f"rstd{n}", [TP, SUB]) for n in (1, 2)]
        logT = sb("logT", [P, TT])
        sc = sb("sc", [TP, SUB * E])
        sbias = sb("sbias", [TP, SUB * E])
        pairs6 = sb("pairs6", [TP, SUB * NG, 6])
        gs = sb("gs", [TP, SUB, NG])
        ge1 = sb("ge1", [TP, SUB, NG])
        ge2 = sb("ge2", [TP, SUB, 2])
        ge3 = sb("ge3", [TP, SUB, 1])
        winit = sb("winit", [TP, SUB, NG])
        wins = sb("wins", [TP, SUB, NG])
        gmask = sb("gmask", [TP, SUB * NG])
        gpen = sb("gpen", [TP, SUB * NG])
        masked = sbias
        top8 = sb("top8", [TP, SUB, 8])
        marks = sb("marks", [TP, SUB, 8])
        gscore = pairs6[:, :, :].rearrange("p g n -> p (g n)")[:, 0:SUB * E]
        marked = sb("marked", [TP, SUB * E])
        wsel = sb("wsel", [TP, SUB * E])
        wsum = sb("wsum", [TP, SUB])
        comb2 = sb("comb2", [TP, SUB, 2, E], F32R)
        wraw = zt[:, 0:2 * P].rearrange("p (k c) -> p k c", k=KD)
        rraw = zt[0:E, 2 * P:4 * P]
        wos = ut[:, 0:2 * D].rearrange("p (o d) -> p o d", o=2)
        wosT = t1[:, 0:4 * P].rearrange("p (o k n) -> p o k n", o=2, k=KD)
        wdi1 = t2[:, 0:2 * P].rearrange("p (k n) -> p k n", k=KD)
        wdup = hs1[:, 0:4 * P].rearrange("p (s k n) -> p s k n", s=2, k=KD)
        bcol = sb("bcol", [P, KD, 2])
        bsum = sb("bsum", [P, KD])
        self32 = ew[:, :, :].rearrange("p b t -> p (b t)")[:, 0:MR * P]
        up_stage = stage[:, 0:KD * E * H].rearrange("p (k n) -> p k n", k=KD)
        gate_stage = stage[:, 2 * E * H:2 * E * H + KD * E * H].rearrange("p (k n) -> p k n", k=KD)
        down_stage = stage[:, 4 * E * H:4 * E * H + MR * D].rearrange("p (m d) -> p m d", m=MR)
        sh_raw = blocks[:, :, :].rearrange("p a n -> p (a n)")[:, 0:MS * D].rearrange("p (m d) -> p m d", m=MS)

        g_ps = ps("g_ps", [P, 2, 512])
        u_ps = ps("u_ps", [P, 2, 512])
        c_ps = ps("c_ps", [P, 512])
        ch_ps = ps("ch_ps", [P, 512])
        d_ps = ps("d_ps", [P, SUB, D])

        S = {name: sem(name) for name in (
            "x_in", "zeroed", "w_chain", "w_ffn", "w_shared", "ident_done", "const_done", "setup_mm", "setup_ev",
            "setup_act", "setup_dve", "shared_mm", "shared_ev", "staged_used",
            "ends_done", "scan_done", "ew_done", "tok_mm", "tok_ev", "st1", "aggr1", "rstd1", "xn1",
            "x1t_mm", "x1t_ev", "pre_mm", "z_ev", "u_ev", "abs_done", "relu_done", "exp_done", "ln_done",
            "delta_done", "decay_done", "drive_done", "ssm_done", "carry_mm", "carry_ev", "last_done",
            "row_mm", "row_ev", "res_done", "y_mm", "y_ev", "st2", "aggr2", "rstd2", "xn2", "x2t_mm", "x2t_ev",
            "xhi_done", "xlo_done", "logit_mm", "logit_ev", "logt_mm", "score_exp", "route", "comb_mm", "comb_ev",
            "gate_mm", "up_mm", "c_mm", "down_mm", "silu_done", "t_done", "hid_done", "hi_done",
            "lo_done", "fin_done", "out0", "out1", "out2")}
        OUT = [S["out0"], S["out1"], S["out2"]]

        def nth(pair, per_pair, n):
            return pair * per_pair + n

        def wait(eng, name, value):
            if not (isinstance(value, int) and value <= 0):
                eng.wait_ge(S[name], value)

        def inc(ins, name):
            return ins.then_inc(S[name], 1)

        ZU = [1, 3, 4]
        ROUTE = {"scores": 0, "groups": 10, "pick": 18, "weights": 26}
        NROUTE = 32
        NAGGR = 7

        def reads_of(step, arg, pair):
            if step == "tok":
                return [("tok_ev", nth(pair, 6, arg + 1))]
            if step == "x1t":
                return [("x1t_ev", nth(pair, 6, 2 * arg[0] + arg[1] + 1))]
            if step == "pre":
                v = nth(pair, 8, 4 * arg[0] + ZU[arg[1]])
                return [("z_ev", v), ("u_ev", v)]
            if step == "carry":
                return [("carry_ev", nth(pair, 1, 1))]
            if step == "class_row":
                return [("row_ev", nth(pair, 1, 1))]
            if step == "y":
                return [("y_ev", nth(pair, 6, 2 * arg[0] + arg[1] + 1))]
            if step == "x2t":
                return [("x2t_ev", nth(pair, 6, 2 * arg[0] + arg[1] + 1))]
            if step == "logit":
                return [("logit_ev", nth(pair, 3, arg + 1))]
            if step == "logit_t":
                return [("score_exp", nth(pair, 3, arg + 1))]
            if step == "comb_t":
                return [("comb_ev", nth(pair, 3, arg + 1))]
            return None

        PE_STEPS = ("tok", "x1t", "pre", "carry", "class_row", "y", "x2t", "logit", "logit_t", "comb_t")
        last_pe = [None]

        def chain_at(at, pair, have_next, have_this=True):
            for which, step, arg in CHAIN.get(at, ()):
                if which == 1 and have_next:
                    yield step, arg, pair + 1
                if which == 0 and have_this:
                    yield step, arg, pair

        def pieces(s):
            got = []
            for b in range(2):
                lo, hi = max(s * TT, b * T), min((s + 1) * TT, (b + 1) * T)
                if lo < hi:
                    got.append((b, lo - b * T, hi - lo, lo - s * TT))
            return got

        def cols(j):
            return j // (NJ // 2), (j % (NJ // 2)) * TP

        block = ctx.enter_context(nc.Block())

        x_v = x.rearrange("(q b) c t -> q c b t", b=2)
        out_v = out.rearrange("(q b) t d -> q (b t) d", b=2).rearrange("q (t j p) d -> q t p j d", t=NT, p=TP)

        @block.sync
        def _(sp):
            sp.dma_start(x_in[:], x_v[0]).then_inc(S["x_in"], 16)
            sp.dma_start(wraw, tok_w.rearrange("(k p) c -> p k c", p=P)).then_inc(S["w_chain"], 16)
            for o, (a, b) in enumerate(((wo, ws), (ws, wo))):
                sp.dma_start(wos[0:N, o, :], a[0]).then_inc(S["w_chain"], 16)
                sp.dma_start(wos[N:P, o, :], b[0]).then_inc(S["w_chain"], 16)
            for o, (a, b) in enumerate(((wd, wi), (wi, wd))):
                sp.dma_start(wdi0[:, o, :, 0:N], a[0].rearrange("(k p) n -> p k n", p=P)).then_inc(S["w_chain"], 16)
                sp.dma_start(wdi0[:, o, :, N:P], b[0].rearrange("(k p) n -> p k n", p=P)).then_inc(S["w_chain"], 16)
            for o, a in enumerate((wd, wi)):
                a1 = a[1].rearrange("(k p) n -> p k n", p=P)
                sp.dma_start(wdi1[:, :, o * N:(o + 1) * N], a1).then_inc(S["w_chain"], 16)
                for half in range(2):
                    sp.dma_start(wdup[:, o, :, half * N:(half + 1) * N], a1).then_inc(S["w_chain"], 16)
            sp.wait_ge(S["zeroed"], 2)
            for b in range(2):
                sp.dma_start(wo1[b * N:(b + 1) * N, b, :], wo[1]).then_inc(S["w_chain"], 16)
                sp.dma_start(ws1[b * N:(b + 1) * N, b, :], ws[1]).then_inc(S["w_chain"], 16)
            for dst, src in ((gate_stage, gate_w), (up_stage, up_w)):
                for k in range(KD):
                    sp.dma_start(dst[:, k, :].rearrange("p (e h) -> p e h", e=E),
                                 src[:, k * P:(k + 1) * P, :].rearrange("e p h -> p e h")).then_inc(S["w_ffn"], 16)
            sp.dma_start(down_stage, down_w.rearrange("e h d -> (e h) d").rearrange("(m p) d -> p m d", p=P)
                         ).then_inc(S["w_ffn"], 16)
            sp.dma_start(sh_raw, sh_gate_w.rearrange("(m p) c -> p m c", p=P)).then_inc(S["w_shared"], 16)
            sp.wait_ge(S["shared_mm"], MS)
            sp.dma_start(sh_raw, sh_up_w.rearrange("(m p) c -> p m c", p=P)).then_inc(S["w_shared"], 16)
            sp.wait_ge(S["shared_mm"], 2 * MS)
            sp.dma_start(sh_raw[:, :, :].rearrange("p m c -> p (m c)").rearrange("p (k n) -> p k n", k=KD),
                         sh_down_w.rearrange("(k p) n -> p k n", p=P)).then_inc(S["w_shared"], 16)

            def load_x(pair):
                wait(sp, "ew_done", nth(pair - 1, 2, 2))
                sp.dma_start(x_in[:], x_v[pair]).then_inc(S["x_in"], 16)

            def store(pair, t):
                wait(sp, "fin_done", nth(pair, 2 * NT, 2 * t + 2))
                sp.dma_start(out_v[pair, t], h2[:, t * SUB:(t + 1) * SUB, :]).then_inc(OUT[t], 16)

            load_x(1)
            store(0, 0)
            store(0, 1)
            with sp.Fori(1, NP - 1) as i:
                load_x(i + 1)
                store(i - 1, NT - 1)
                store(i, 0)
                store(i, 1)
            store(NP - 2, NT - 1)
            for t in range(NT):
                store(NP - 1, t)
            for t in range(NT):
                sp.wait_ge(OUT[t], 16 * NP)

        @block.gpsimd
        def _(pool):
            pool.memset(ident[:], 0.0).then_inc(S["ident_done"], 1)
            pool.memset(self32, 0.0).then_inc(S["ident_done"], 1)
            pool.wait_ge(S["ident_done"], 2)
            pool.affine_select(out=ident[:], in_=ident[:], compare_op=ALU.not_equal, fill=1.0, base=0,
                               pattern=[[-1, P]], channel_multiplier=1).then_inc(S["ident_done"], 1)
            sv = self32.rearrange("p (m a c) -> p m a c", m=MR, a=2)
            for part in range(2):
                pool.affine_select(out=sv, in_=sv, compare_op=ALU.not_equal, fill=1.0, base=-part * E,
                                   pattern=[[-2, MR], [-1, 2], [0, H]], channel_multiplier=1
                                   ).then_inc(S["ident_done"], 1)
                pool.wait_ge(S["ident_done"], 4 + part)

            def chain(step, arg, pair):
                if step == "ewma":
                    wait(pool, "scan_done", nth(pair, 4, 2 * arg + 2))
                    inc(pool.tensor_tensor(ew[:, arg, :], ew[:, arg, :], x_in[:, arg, :], ALU.add), "ew_done")
                elif step in ("ln1_stats", "ln2_stats"):
                    n = int(step[2]) - 1
                    wait(pool, f"aggr{n + 1}", nth(pair, NT * NAGGR, NAGGR * (arg + 1)))
                    wait(pool, f"xn{n + 1}", nth(pair, 3, arg))
                    inc(pool.tensor_tensor(rstd[n][:], mv[n][:, :, 1], mhalf[:], ALU.pow), f"rstd{n + 1}")
                elif step == "residual":
                    wait(pool, "row_ev", nth(pair, 1, 1))
                    wait(pool, "xn1", nth(pair, 3, 3))
                    hv = h_tok[:, 2 * arg:2 * arg + 2, :]
                    row = rows[:, arg // 3, :].unsqueeze(1).broadcast_to([TP, 2, D])
                    inc(pool.tensor_tensor(hv, hv, row, ALU.add), "res_done")
                elif step == "x2t":
                    t, k = arg
                    wait(pool, "xhi_done", nth(pair, 6, 2 * t + k + 1))
                    inc(pool.tensor_tensor(x_lo[:, t, k, :], x2T[:, k, :], x_hi[:, t, k, :].bitcast(F32),
                                           ALU.subtract), "xlo_done")

            def ffn(pair, idx):
                wait(pool, "hi_done", nth(pair, SLOTS, idx + 1))
                wait(pool, "down_mm", nth(pair, SLOTS, idx - 1))
                inc(pool.tensor_tensor(hid_lo[:, idx % 2, :], hid[:, idx % 2, :],
                                       hid_hi[:, idx % 2, :].bitcast(F32), ALU.subtract), "lo_done")

            def iteration(pair, have_next):
                for idx in range(SLOTS):
                    for half in (0.0, 0.5):
                        for step, arg, of in chain_at(idx + half, pair, have_next):
                            chain(step, arg, of)
                    ffn(pair, idx)

            pool.wait_ge(S["const_done"], 2)
            for at in sorted(CHAIN):
                for step, arg, of in chain_at(at, -1, True, have_this=False):
                    chain(step, arg, of)
            iteration(0, True)
            with pool.Fori(1, NP - 1) as i:
                iteration(i, True)
            iteration(NP - 1, False)

        @block.scalar
        def _(act):
            for half in (vecs[0:N, :], vecs[N:P, :]):
                for n, a in enumerate((bd, bi, a_log)):
                    act.dma_start(half[:, 2 * n:2 * n + 2], a.rearrange("l n -> n l"),
                                   allow_slow_non_contiguous=True).then_inc(S["w_chain"], 16)
            for n, a in enumerate((bo, bs)):
                act.dma_start(bcol[:, :, n:n + 1], a[0].rearrange("(k p a) -> p k a", p=P, a=1),
                               allow_slow_non_contiguous=True).then_inc(S["w_chain"], 16)
                act.dma_start(brow[:, n, :], a[1].partition_broadcast(TP)).then_inc(S["w_chain"], 16)
            act.dma_start(tokb_bc[:], tok_b.partition_broadcast(TP)).then_inc(S["w_chain"], 16)
            act.dma_start(corr_bc[:], corr_bias.partition_broadcast(TP)).then_inc(S["w_chain"], 16)
            act.dma_start(rraw, router_w[:, :]).then_inc(S["w_chain"], 16)
            act.wait_ge(S["w_chain"], 16 * W_CHAIN)
            inc(act.activation(spt[:, 0:2], vecs[:, 4:6], ACT.Abs), "setup_act")
            act.wait_ge(S["setup_act"], 1)
            inc(act.activation(spt[:, 2:4], spt[:, 0:2], ACT.Exp, scale=-1.0), "setup_act")
            act.wait_ge(S["setup_act"], 2)
            inc(act.activation(spt[:, 0:2], spt[:, 2:4], ACT.Ln, bias=1.0), "setup_act")

            def chain(step, arg, pair):
                if step == "x1t":
                    t, k = arg
                    wait(act, "x1t_mm", nth(pair, 6, 2 * t + k + 1))
                    if k == 0:
                        wait(act, "pre_mm", nth(pair, 6, t) if t else nth(pair - 1, 6, 3))
                    inc(act.activation(x1T[:, k, :], ch_ps[:, 0:TT], ACT.Copy), "x1t_ev")
                elif step == "pre":
                    layer, s = arg
                    wait(act, "pre_mm", nth(pair, 6, 3 * layer + s + 1))
                    wait(act, "ssm_done", nth(pair, 2, layer))
                    for b, c0, n, at in pieces(s):
                        src = ch_ps[0:N, at:at + n] if b == 0 else ch_ps[N:P, at:at + n]
                        inc(act.activation(zt[b * N:(b + 1) * N, c0:c0 + n], src, ACT.Copy), "z_ev")
                elif step == "ssm_log":
                    bz = vecs[:, 0:1] if arg == 0 else bias1s[:, 0:1]
                    wait(act, "z_ev", nth(pair, 8, 4 * arg + 4))
                    if arg == 0:
                        wait(act, "delta_done", nth(pair - 1, 2, 2))
                    else:
                        wait(act, "pre_mm", nth(pair, 6, 6))
                        wait(act, "carry_ev", nth(pair, 1, 1))
                    inc(act.activation(t1[:], zt[:], ACT.Abs, bias=bz), "abs_done")
                    wait(act, "abs_done", nth(pair, 2, arg + 1))
                    inc(act.activation(t1[:], t1[:], ACT.Exp, scale=-1.0), "exp_done")
                    wait(act, "exp_done", nth(pair, 2, arg + 1))
                    inc(act.activation(t1[:], t1[:], ACT.Ln, bias=1.0), "ln_done")
                elif step == "ssm_decay":
                    wait(act, "delta_done", nth(pair, 2, arg + 1))
                    inc(act.activation(zt[:], t2[:], ACT.Exp, scale=nspa[:, arg:arg + 1]), "decay_done")
                elif step == "x2t":
                    t, k = arg
                    wait(act, "x2t_mm", nth(pair, 6, 2 * t + k + 1))
                    wait(act, "xlo_done", nth(pair, 6, 2 * t + k - 1))
                    inc(act.activation(x2T[:, k, :], ch_ps[:, 0:TT], ACT.Copy), "x2t_ev")
                elif step == "logit":
                    wait(act, "logit_mm", nth(pair, 3, arg + 1))
                    wait(act, "logt_mm", nth(pair, 3, arg))
                    inc(act.activation(logT[0:E, :], ch_ps[0:E, 0:TT], ACT.Copy), "logit_ev")
                elif step == "logit_t":
                    wait(act, "logt_mm", nth(pair, 3, arg + 1))
                    wait(act, "route", nth(pair, 3 * NROUTE, NROUTE * arg))
                    inc(act.activation(sc[:, :].rearrange("p (j e) -> p j e", e=E),
                                       ch_ps[0:TP, :].rearrange("p (j e) -> p j e", j=SUB)[:, :, 0:E],
                                       ACT.Exp, scale=-1.0), "score_exp")
                elif step == "comb_t":
                    wait(act, "comb_mm", nth(pair, 3, arg + 1))
                    wait(act, "down_mm", nth(pair - 1, SLOTS, M * (arg + 1)))
                    inc(act.activation(combT[0:2 * E, arg, :], ch_ps[0:2 * E, 0:TT], ACT.Copy), "comb_ev")

            def ffn(pair, idx):
                wait(act, "gate_mm", nth(pair, SLOTS, idx + 1))
                wait(act, "hid_done", nth(pair, SLOTS, idx - 1))
                inc(act.activation(sg[:, idx % 2, :], g_ps[:, idx % 2, 0:TT], ACT.Silu), "silu_done")

            def ffn_hi(pair, idx):
                wait(act, "hid_done", nth(pair, SLOTS, idx + 1))
                wait(act, "down_mm", nth(pair, SLOTS, idx - 1))
                inc(act.activation(hid_hi[:, idx % 2, :], hid[:, idx % 2, :], ACT.Copy), "hi_done")

            def iteration(pair, have_next):
                for idx in range(SLOTS):
                    for step, arg, of in chain_at(idx + 0.0, pair, have_next):
                        chain(step, arg, of)
                    ffn(pair, idx)
                    for step, arg, of in chain_at(idx + 0.5, pair, have_next):
                        chain(step, arg, of)
                    ffn_hi(pair, idx)

            for at in sorted(CHAIN):
                for step, arg, of in chain_at(at, -1, True, have_this=False):
                    chain(step, arg, of)
            iteration(0, True)
            with act.Fori(1, NP - 1) as i:
                iteration(i, True)
            iteration(NP - 1, False)

        @block.vector
        def _(dve):
            inc(dve.memset(wo1[:], 0.0), "zeroed")
            inc(dve.memset(ws1[:], 0.0), "zeroed")
            inc(dve.memset(g1[:], 0.0), "zeroed")
            inc(dve.memset(sbd[:], 0.0), "zeroed")
            inc(dve.memset(combT[:, :, :].bitcast(F32), 0.0), "zeroed")
            inc(dve.memset(ge1[:], 0.0), "zeroed")
            inc(dve.memset(logT[:], 0.0), "zeroed")
            for g in range(NG):
                dve.memset(winit[:, :, g:g + 1], float(g))
            inc(dve.memset(c09[:], 1.0 - ALPHA), "const_done")
            inc(dve.memset(mhalf[:], -0.5), "const_done")
            dve.wait_ge(S["const_done"], 2)
            dve.wait_ge(S["ident_done"], 5)
            dve.tensor_copy(sel[:, :, :].rearrange("p m c -> p (m c)"), self32)

            dve.wait_ge(S["w_chain"], 16 * W_CHAIN)
            inc(dve.tensor_tensor(bsum[:], bcol[:, :, 0], bcol[:, :, 1], ALU.add), "setup_ev")
            inc(dve.tensor_tensor(brow[:, 0, :], brow[:, 0, :], brow[:, 1, :], ALU.add), "setup_ev")
            dve.wait_ge(S["setup_mm"], 1)
            inc(dve.tensor_scalar(tokwT[:], ch_ps[:, 0:D], 0.5 * ALPHA, None, ALU.mult), "setup_ev")
            dve.wait_ge(S["setup_mm"], 2)
            inc(dve.tensor_copy(wosT, ch_ps[:, :].rearrange("p (o k n) -> p o k n", o=2, k=KD)), "setup_ev")
            dve.wait_ge(S["setup_mm"], 3)
            dve.wait_ge(S["zeroed"], 4)
            lo_, hi_ = slice(0, N), slice(N, P)
            p0, p1 = ch_ps[:, 0:P], ch_ps[:, P:2 * P]
            for dst, src in (
                (g1[lo_, 0, :], p0[lo_, :]),
                (g1[hi_, 1, lo_], p1[hi_, hi_]), (g1[hi_, 1, hi_], p1[hi_, lo_]),
                (sbd[lo_, 0, lo_], p1[lo_, lo_]), (sbd[hi_, 0, hi_], p0[hi_, lo_]),
                (sbd[lo_, 1, lo_], p1[lo_, hi_]), (sbd[hi_, 1, hi_], p0[hi_, hi_]),
            ):
                last = dve.tensor_copy(dst, src)
            inc(last, "setup_ev")
            dve.wait_ge(S["setup_mm"], 4)
            for s in range(2):
                last = dve.tensor_tensor(bias1[:, s:s + 1], ch_ps[:, s:s + 1], vecs[:, 2 * s + 1:2 * s + 2], ALU.add)
            inc(last, "setup_ev")
            dve.wait_ge(S["setup_mm"], 5)
            rwT_ps = ch_ps[:, 0:KD * E].rearrange("p (k e) -> p k e", k=KD)
            inc(dve.tensor_copy(rw_hi[:], rwT_ps), "setup_dve")
            dve.wait_ge(S["setup_dve"], 1)
            inc(dve.tensor_tensor(rw_lo[:], rwT_ps, rw_hi[:, :, :].bitcast(F32), ALU.subtract), "setup_ev")
            dve.wait_ge(S["setup_act"], 3)
            inc(dve.tensor_scalar(spt[:, 2:4], vecs[:, 4:6], 0.0, None, ALU.max), "setup_dve")
            dve.wait_ge(S["setup_dve"], 2)
            inc(dve.tensor_tensor(spt[:, 2:4], spt[:, 2:4], spt[:, 0:2], ALU.add), "setup_dve")
            dve.wait_ge(S["setup_dve"], 3)
            inc(dve.tensor_scalar(nspa[:], spt[:, 2:4], -1.0, None, ALU.mult), "setup_ev")
            dve.wait_ge(S["w_ffn"], 16 * 5)
            nd = 3
            for hi_t, lo_t, src in (
                (gate_hi[:, :, HS:], gate_lo[:, :, HS:], gate_stage), (up_hi[:, :, HS:], up_lo[:, :, HS:], up_stage),
                (down_hi[:, MS:, :], down_lo[:, MS:, :], down_stage),
            ):
                inc(dve.tensor_copy(hi_t, src), "setup_dve")
                nd += 1
                dve.wait_ge(S["setup_dve"], nd)
                inc(dve.tensor_tensor(lo_t, src, hi_t.bitcast(F32), ALU.subtract), "staged_used")
            for n, (hi_t, lo_t) in enumerate(((gate_hi, gate_lo), (up_hi, up_lo))):
                for m in range(MS):
                    dve.wait_ge(S["shared_mm"], n * MS + m + 1)
                    src = ch_ps[:, 0:D].rearrange("p (k c) -> p k c", k=KD)
                    hv, lv = hi_t[:, :, m * P:(m + 1) * P], lo_t[:, :, m * P:(m + 1) * P]
                    inc(dve.tensor_copy(hv, src), "setup_dve")
                    nd += 1
                    dve.wait_ge(S["setup_dve"], nd)
                    inc(dve.tensor_tensor(lv, src, hv.bitcast(F32), ALU.subtract), "shared_ev")
            for m in range(MS):
                dve.wait_ge(S["shared_mm"], 2 * MS + m + 1)
                inc(dve.tensor_copy(down_hi[:, m, :], ch_ps[:, 0:D]), "setup_dve")
                nd += 1
                dve.wait_ge(S["setup_dve"], nd)
                inc(dve.tensor_tensor(down_lo[:, m, :], ch_ps[:, 0:D], down_hi[:, m, :].bitcast(F32),
                                      ALU.subtract), "shared_ev")
            dve.wait_ge(S["shared_ev"], 3 * MS)
            dve.wait_ge(S["staged_used"], 3)

            def routed(ins, pair, tile, n):
                inc(ins, "route")
                wait(dve, "route", nth(pair, 3 * NROUTE, NROUTE * tile + n))

            def chain(step, arg, pair):
                if step == "ewma":
                    b = arg
                    if b == 0:
                        wait(dve, "x_in", nth(pair, 16, 16))
                        inc(dve.tensor_scalar(ends10[:], x_in[:, :, 0:T:T - 1], 1.0 / ALPHA, None, ALU.mult),
                            "ends_done")
                    wait(dve, "ends_done", nth(pair, 1, 1))
                    wait(dve, "tok_mm", nth(pair - 1, 6, 3 * (b + 1)))
                    decay = c09[:, 0:1].broadcast_to([P, T])
                    inc(dve.tensor_tensor_scan(ew[:, b, :], decay, x_in[:, b, :], ends10[:, b, 0:1],
                                               ALU.mult, ALU.add), "scan_done")
                    wait(dve, "scan_done", nth(pair, 4, 2 * b + 1))
                    inc(dve.tensor_tensor_scan(x_in[:, b, T - 1::-1], decay, x_in[:, b, T - 1::-1],
                                               ends10[:, b, 1:2], ALU.mult, ALU.add), "scan_done")
                elif step == "tok":
                    wait(dve, "tok_mm", nth(pair, 6, arg + 1))
                    wait(dve, "y_ev", nth(pair - 1, 6, arg + 1))
                    hv = h_tok[:, 2 * arg:2 * arg + 2, :]
                    inc(dve.tensor_tensor(hv, ch_ps[0:TP, :].rearrange("p (j d) -> p j d", d=D),
                                          tokb_bc[:, :].unsqueeze(1).broadcast_to([TP, 2, D]), ALU.add), "tok_ev")
                    wait(dve, "tok_ev", nth(pair, 6, arg + 1))
                    for j in range(2):
                        inc(dve.bn_stats(stats[0][:, (2 * arg + j) % SUB, :], hv[:, j, :]), "st1")
                elif step in ("ln1_stats", "ln2_stats"):
                    n = int(step[2]) - 1
                    wait(dve, f"st{n + 1}", nth(pair, NJ, SUB * (arg + 1)))
                    wait(dve, f"xn{n + 1}", nth(pair, 3, arg))
                    st, sq, a = stats[n], halves[n], f"aggr{n + 1}"
                    v0 = NAGGR * arg
                    inc(dve.tensor_tensor(mv[n][:, :, 0], st[:, :, 1], st[:, :, 4], ALU.add), a)
                    inc(dve.tensor_tensor(sq[:, :, 0], st[:, :, 1], st[:, :, 4], ALU.subtract), a)
                    inc(dve.tensor_tensor(sq[:, :, 1], st[:, :, 2], st[:, :, 5], ALU.add), a)
                    wait(dve, a, nth(pair, NT * NAGGR, v0 + 3))
                    inc(dve.tensor_scalar(mv[n][:, :, 0], mv[n][:, :, 0], 0.5, None, ALU.mult), a)
                    inc(dve.scalar_tensor_tensor(sq[:, :, 0], sq[:, :, 0], 0.25, sq[:, :, 0], ALU.mult, ALU.mult), a)
                    inc(dve.tensor_scalar(sq[:, :, 1], sq[:, :, 1], 1.0 / D, EPS, ALU.mult, ALU.add), a)
                    wait(dve, a, nth(pair, NT * NAGGR, v0 + 6))
                    inc(dve.tensor_tensor(mv[n][:, :, 1], sq[:, :, 1], sq[:, :, 0], ALU.add), a)
                elif step in ("ln1_norm", "ln2_norm"):
                    n = int(step[2]) - 1
                    src, dst = (h_tok, xn1) if n == 0 else (h2, xn2)
                    wait(dve, f"rstd{n + 1}", nth(pair, 3, arg + 1))
                    wait(dve, f"x{n + 1}t_mm", nth(pair, 6, 2 * arg))
                    for j in range(SUB):
                        last = dve.tensor_scalar(dst[:, j, :], src[:, arg * SUB + j, :], mv[n][:, j, 0:1],
                                                 rstd[n][:, j:j + 1], ALU.subtract, ALU.mult)
                    inc(last, f"xn{n + 1}")
                elif step == "pre":
                    layer, s = arg
                    wait(dve, "pre_mm", nth(pair, 6, 3 * layer + s + 1))
                    wait(dve, "ssm_done", nth(pair, 2, layer))
                    if len(pieces(s)) > 1:
                        wait(dve, "z_ev", nth(pair, 8, 4 * layer + ZU[s]))
                    for b, c0, n, at in pieces(s):
                        src = ch_ps[N:P, at:at + n] if b == 0 else ch_ps[0:N, at:at + n]
                        inc(dve.tensor_copy(ut[b * N:(b + 1) * N, c0:c0 + n], src), "u_ev")
                elif step == "ssm_log":
                    bz = vecs[:, 0:1] if arg == 0 else bias1s[:, 0:1]
                    wait(dve, "z_ev", nth(pair, 8, 4 * arg + 4))
                    if arg == 1:
                        wait(dve, "carry_ev", nth(pair, 1, 1))
                    inc(dve.tensor_scalar(t2[:], zt[:], bz, 0.0, ALU.add, ALU.max), "relu_done")
                elif step == "ssm_decay":
                    wait(dve, "ln_done", nth(pair, 2, arg + 1))
                    wait(dve, "relu_done", nth(pair, 2, arg + 1))
                    inc(dve.tensor_tensor(t2[:], t1[:], t2[:], ALU.add), "delta_done")
                    bu = vecs[:, 2:3] if arg == 0 else bias1s[:, 1:2]
                    wait(dve, "delta_done", nth(pair, 2, arg + 1))
                    wait(dve, "u_ev", nth(pair, 8, 4 * arg + 4))
                    inc(dve.scalar_tensor_tensor(ut[:], ut[:], bu, t2[:], ALU.add, ALU.mult), "drive_done")
                elif step == "ssm_scan":
                    wait(dve, "decay_done", nth(pair, 2, arg + 1))
                    wait(dve, "drive_done", nth(pair, 2, arg + 1))
                    if arg == 1:
                        wait(dve, "y_mm", nth(pair - 1, 6, 6))
                    inc(dve.tensor_tensor_scan(t1[:] if arg == 0 else hs1[:], zt[:], ut[:], 0.0,
                                               ALU.mult, ALU.add), "ssm_done")
                elif step == "carry":
                    wait(dve, "carry_mm", nth(pair, 1, 1))
                    inc(dve.tensor_tensor(bias1s[:], ch_ps[:, 0:2], bias1[:], ALU.add), "carry_ev")
                elif step == "last_state":
                    wait(dve, "ssm_done", nth(pair, 2, 2))
                    wait(dve, "row_mm", nth(pair - 1, 1, 1))
                    inc(dve.tensor_copy(last_bc[:], hs1[:, T - 1:T].broadcast_to([P, TP])), "last_done")
                elif step == "class_row":
                    wait(dve, "row_mm", nth(pair, 1, 1))
                    wait(dve, "res_done", nth(pair - 1, 6, 6))
                    inc(dve.tensor_tensor(rows[:], ch_ps[0:TP, :].rearrange("p (b d) -> p b d", b=2),
                                          brow[:, 0, :].unsqueeze(1).broadcast_to([TP, 2, D]), ALU.add), "row_ev")
                elif step == "y":
                    t, q = arg
                    j = t * SUB + 2 * q
                    wait(dve, "y_mm", nth(pair, 6, 2 * t + q + 1))
                    wait(dve, "res_done", nth(pair, 6, 2 * t + q + 1))
                    if not (isinstance(pair, int) and pair == 0):
                        dve.wait_ge(OUT[t], nth(pair, 16, 0))
                    hv = h2[:, j:j + 2, :]
                    inc(dve.tensor_tensor(hv, ch_ps[0:TP, :].rearrange("p (j d) -> p j d", d=D),
                                          h_tok[:, j:j + 2, :], ALU.add), "y_ev")
                    wait(dve, "y_ev", nth(pair, 6, 2 * t + q + 1))
                    if q == 0:
                        wait(dve, "aggr2", nth(pair, NT * NAGGR, NAGGR * t))
                    for n in range(2):
                        inc(dve.bn_stats(stats[1][:, 2 * q + n, :], hv[:, n, :]), "st2")
                elif step == "x2t":
                    t, k = arg
                    wait(dve, "x2t_ev", nth(pair, 6, 2 * t + k + 1))
                    if k == 0:
                        wait(dve, "up_mm", nth(pair - 1, SLOTS, M * (t + 1)))
                    inc(dve.tensor_copy(x_hi[:, t, k, :], x2T[:, k, :]), "xhi_done")
                elif step == "route_scores":
                    base = ROUTE["scores"]
                    wait(dve, "score_exp", nth(pair, 3, arg + 1))
                    routed(dve.tensor_scalar(sc[:], sc[:], 1.0, None, ALU.add), pair, arg, base + 1)
                    routed(dve.reciprocal(sc[:], sc[:]), pair, arg, base + 2)
                    routed(dve.tensor_tensor(sbias[:, :].rearrange("p (j e) -> p j e", e=E),
                                             sc[:, :].rearrange("p (j e) -> p j e", e=E),
                                             corr_bc[:, :].unsqueeze(1).broadcast_to([TP, SUB, E]), ALU.add),
                           pair, arg, base + 3)
                    s4 = sbias[:, :].rearrange("p (g e) -> p g e", e=EG)
                    n0 = 0
                    for d in range(1, EG):
                        inc(dve.tensor_tensor(pairs6[:, :, n0:n0 + EG - d], s4[:, :, 0:EG - d], s4[:, :, d:EG],
                                              ALU.add), "route")
                        n0 += EG - d
                    wait(dve, "route", nth(pair, 3 * NROUTE, NROUTE * arg + base + 6))
                    routed(dve.tensor_reduce(gs[:, :, :].rearrange("p j g -> p (j g)"), pairs6[:], AX.X, ALU.max),
                           pair, arg, base + 7)
                    inc(dve.tensor_tensor(ge1[:, :, 0:3], gs[:, :, 0:3], gs[:, :, 1:4], ALU.is_ge), "route")
                    inc(dve.tensor_tensor(ge2[:], gs[:, :, 0:2], gs[:, :, 2:4], ALU.is_ge), "route")
                    inc(dve.tensor_tensor(ge3[:], gs[:, :, 0:1], gs[:, :, 3:4], ALU.is_ge), "route")
                elif step == "route_groups":
                    base = ROUTE["groups"]
                    wait(dve, "route", nth(pair, 3 * NROUTE, NROUTE * arg + base))
                    steps = ((slice(0, 4), winit[:], ge1[:], ALU.add),
                             (slice(1, 4), None, ge1[:, :, 0:3], ALU.subtract), (slice(0, 2), None, ge2[:], ALU.add),
                             (slice(2, 4), None, ge2[:], ALU.subtract), (slice(0, 1), None, ge3[:], ALU.add),
                             (slice(3, 4), None, ge3[:], ALU.subtract))
                    for n, (s, a, b, op) in enumerate(steps):
                        routed(dve.tensor_tensor(wins[:, :, s], wins[:, :, s] if a is None else a, b, op),
                               pair, arg, base + n + 1)
                    routed(dve.tensor_scalar(gmask[:], wins[:, :, :].rearrange("p j g -> p (j g)"), 2.0, None,
                                             ALU.is_ge), pair, arg, base + 7)
                    routed(dve.tensor_scalar(gpen[:], gmask[:], 1.0, BIG, ALU.subtract, ALU.mult),
                           pair, arg, base + 8)
                elif step == "route_pick":
                    base = ROUTE["pick"]
                    gm = gmask[:, :].unsqueeze(2).broadcast_to([TP, SUB * NG, EG])
                    gp = gpen[:, :].unsqueeze(2).broadcast_to([TP, SUB * NG, EG])
                    m4 = masked[:, :].rearrange("p (g e) -> p g e", e=EG)
                    s4 = sbias[:, :].rearrange("p (g e) -> p g e", e=EG)
                    routed(dve.tensor_tensor(m4, s4, gm, ALU.mult), pair, arg, base + 1)
                    routed(dve.tensor_tensor(m4, m4, gp, ALU.add), pair, arg, base + 2)
                    inc(dve.memset(marks[:, :, 4:8], -BIG), "route")
                    for j in range(SUB):
                        last = dve.max(top8[:, j, :], masked[:, j * E:(j + 1) * E])
                    routed(last, pair, arg, base + 4)
                    routed(dve.tensor_copy(marks[:, :, 0:4], top8[:, :, 0:4]), pair, arg, base + 5)
                    inc(dve.tensor_tensor(gscore.rearrange("p (g e) -> p g e", e=EG),
                                          sc[:, :].rearrange("p (g e) -> p g e", e=EG), gm, ALU.mult), "route")
                    for j in range(SUB):
                        last = dve.match_replace(marked[:, j * E:(j + 1) * E], marks[:, j, :],
                                                 masked[:, j * E:(j + 1) * E], BIG)
                    routed(last, pair, arg, base + 7)
                    inc(dve.scalar_tensor_tensor(wsel[:], marked[:], BIG, gscore, ALU.is_equal, ALU.mult),
                        "route")
                elif step == "route_weights":
                    base = ROUTE["weights"]
                    w3 = wsel[:, :].rearrange("p (j e) -> p j e", e=E)
                    wait(dve, "comb_mm", nth(pair, 3, arg))
                    wait(dve, "route", nth(pair, 3 * NROUTE, NROUTE * arg + base))
                    routed(dve.tensor_reduce(wsum[:], w3, AX.X, ALU.add), pair, arg, base + 1)
                    routed(dve.tensor_scalar(wsum[:], wsum[:], 1e-20, None, ALU.add), pair, arg, base + 2)
                    routed(dve.reciprocal(wsum[:], wsum[:]), pair, arg, base + 3)
                    routed(dve.tensor_tensor(w3, w3, wsum[:, :].unsqueeze(2).broadcast_to([TP, SUB, E]), ALU.mult),
                           pair, arg, base + 4)
                    routed(dve.tensor_copy(comb2[:, :, 0, :], w3), pair, arg, base + 5)
                    inc(dve.tensor_tensor(comb2[:, :, 1, :], w3, comb2[:, :, 0, :].bitcast(F32), ALU.subtract),
                        "route")

            def ffn(pair, idx):
                t, m = divmod(idx, M)
                if m >= MS:
                    wait(dve, "c_mm", nth(pair, NT * MR, t * MR + m - MS + 1))
                    wait(dve, "silu_done", nth(pair, SLOTS, idx + 1))
                    inc(dve.tensor_tensor(sg[:, idx % 2, :], sg[:, idx % 2, :], c_ps[:, 0:TT], ALU.mult), "t_done")
                    wait(dve, "t_done", nth(pair, NT * MR, t * MR + m - MS + 1))
                else:
                    wait(dve, "silu_done", nth(pair, SLOTS, idx + 1))
                wait(dve, "up_mm", nth(pair, SLOTS, idx + 1))
                wait(dve, "lo_done", nth(pair, SLOTS, idx - 1))
                inc(dve.tensor_tensor(hid[:, idx % 2, :], sg[:, idx % 2, :], u_ps[:, idx % 2, 0:TT], ALU.mult),
                    "hid_done")

            def finish(pair, t):
                wait(dve, "down_mm", nth(pair, SLOTS, M * (t + 1)))
                for q in range(2):
                    hv = h2[:, t * SUB + 2 * q:t * SUB + 2 * q + 2, :]
                    inc(dve.tensor_tensor(hv, d_ps[0:TP, 2 * q:2 * q + 2, :], hv, ALU.add), "fin_done")

            def iteration(pair, have_next, first=False):
                for idx in range(SLOTS):
                    for half in (0.0, 0.5):
                        for step, arg, of in chain_at(idx + half, pair, have_next):
                            chain(step, arg, of)
                    ffn(pair, idx)
                    if idx % M == 0 and not (first and idx == 0):
                        if idx == 0:
                            finish(pair - 1, NT - 1)
                        else:
                            finish(pair, idx // M - 1)

            for at in sorted(CHAIN):
                for step, arg, of in chain_at(at, -1, True, have_this=False):
                    chain(step, arg, of)
            iteration(0, True, first=True)
            with dve.Fori(1, NP - 1) as i:
                iteration(i, True)
            iteration(NP - 1, False)
            finish(NP - 1, NT - 1)

        @block.tensor
        def _(pe):
            pe.wait_ge(S["ident_done"], 3)
            pe.wait_ge(S["w_chain"], 16 * W_CHAIN)
            for k in range(KD):
                last = pe.transpose(ch_ps[:, k * P:(k + 1) * P], wraw[:, k, :], ident[:])
            inc(last, "setup_mm")
            pe.wait_ge(S["setup_ev"], 3)
            for o in range(2):
                for k in range(KD):
                    last = pe.transpose(ch_ps[:, (2 * o + k) * P:(2 * o + k + 1) * P],
                                        wos[:, o, k * P:(k + 1) * P], ident[:])
            inc(last, "setup_mm")
            pe.wait_ge(S["setup_ev"], 4)
            for o in range(2):
                for k in range(KD):
                    last = pe.matmul(ch_ps[:, o * P:(o + 1) * P], wosT[:, o, k, :], wdi1[:, k, :],
                                     start=(k == 0), stop=(k == KD - 1))
            inc(last, "setup_mm")
            pe.wait_ge(S["setup_ev"], 5)
            for s in range(2):
                for k in range(KD):
                    last = pe.matmul(ch_ps[:, s:s + 1], wdup[:, s, k, :], bsum[:, k:k + 1],
                                     start=(k == 0), stop=(k == KD - 1))
            inc(last, "setup_mm")
            pe.wait_ge(S["setup_ev"], 6)
            for k in range(KD):
                last = pe.transpose(ch_ps[:, k * E:(k + 1) * E], rraw[:, k * P:(k + 1) * P], ident[0:E, 0:E])
            inc(last, "setup_mm")
            pe.wait_ge(S["setup_ev"], 7)
            for n in range(2):
                pe.wait_ge(S["w_shared"], 16 * (n + 1))
                for m in range(MS):
                    wait(pe, "shared_ev", n * MS + m)
                    for k in range(KD):
                        last = pe.transpose(ch_ps[:, k * P:(k + 1) * P], sh_raw[:, m, k * P:(k + 1) * P], ident[:])
                    inc(last, "shared_mm")
            pe.wait_ge(S["w_shared"], 48)
            sdn = sh_raw[:, :, :].rearrange("p m c -> p (m c)").rearrange("p (k n) -> p k n", k=KD)
            for m in range(MS):
                pe.wait_ge(S["shared_ev"], 2 * MS + m)
                for k in range(KD):
                    last = pe.transpose(ch_ps[:, k * P:(k + 1) * P], sdn[:, k, m * P:(m + 1) * P], ident[:])
                inc(last, "shared_mm")
            pe.wait_ge(S["shared_ev"], 3 * MS)

            def chain(step, arg, pair):
                if step not in PE_STEPS:
                    return
                if last_pe[0] is not None:
                    for name, value in reads_of(*last_pe[0]):
                        wait(pe, name, value)
                last_pe[0] = (step, arg, pair)
                if step == "tok":
                    if arg % 3 == 0:
                        wait(pe, "ew_done", nth(pair, 2, arg // 3 + 1))
                    for n in range(2):
                        b, c0 = cols(2 * arg + n)
                        last = pe.matmul(ch_ps[0:TP, n * D:(n + 1) * D], ew[:, b, c0:c0 + TP], tokwT[:],
                                         start=True, stop=True)
                    inc(last, "tok_mm")
                elif step in ("x1t", "x2t"):
                    t, k = arg
                    src = xn1 if step == "x1t" else xn2
                    wait(pe, f"xn{step[1]}", nth(pair, 3, t + 1))
                    for j in range(SUB):
                        last = pe.transpose(ch_ps[:, j * TP:(j + 1) * TP], src[:, j, k * P:(k + 1) * P],
                                            ident[0:TP, 0:TP])
                    inc(last, f"{step}_mm")
                elif step == "pre":
                    layer, s = arg
                    if layer == 0:
                        wait(pe, "x1t_ev", nth(pair, 6, 2 * s + 2))
                    else:
                        wait(pe, "ssm_done", nth(pair, 2, 1))
                    for b, c0, n, at in pieces(s):
                        if layer == 0:
                            for k in range(KD):
                                last = pe.matmul(ch_ps[:, at:at + n], wdi0[:, b, k, :], x1T[:, k, at:at + n],
                                                 start=(k == 0), stop=(k == KD - 1))
                        else:
                            last = pe.matmul(ch_ps[:, at:at + n], g1[:, b, :], t1[:, c0:c0 + n],
                                             start=True, stop=True)
                    inc(last, "pre_mm")
                elif step == "carry":
                    wait(pe, "ssm_done", nth(pair, 2, 1))
                    for s in range(2):
                        last = pe.matmul(ch_ps[:, s:s + 1], sbd[:, s, :], t1[:, T - 1:T], start=True, stop=True)
                    inc(last, "carry_mm")
                elif step == "class_row":
                    wait(pe, "last_done", nth(pair, 1, 1))
                    for b in range(2):
                        last = pe.matmul(ch_ps[0:TP, b * D:(b + 1) * D], last_bc[:], ws1[:, b, :],
                                         start=True, stop=True)
                    inc(last, "row_mm")
                elif step == "y":
                    t, q = arg
                    wait(pe, "ssm_done", nth(pair, 2, 2))
                    for n in range(2):
                        b, c0 = cols(t * SUB + 2 * q + n)
                        last = pe.matmul(ch_ps[0:TP, n * D:(n + 1) * D], hs1[:, c0:c0 + TP], wo1[:, b, :],
                                         start=True, stop=True)
                    inc(last, "y_mm")
                elif step == "logit":
                    wait(pe, "xlo_done", nth(pair, 6, 2 * arg + 2))
                    parts = [(w, xx, k) for k in range(KD) for w, xx in ((rw_hi, x_hi), (rw_lo, x_hi), (rw_hi, x_lo))]
                    for n, (w, xx, k) in enumerate(parts):
                        last = pe.matmul(ch_ps[0:E, 0:TT], w[:, k, :], xx[:, arg, k, :], start=(n == 0),
                                         stop=(n == len(parts) - 1))
                    inc(last, "logit_mm")
                elif step == "logit_t":
                    wait(pe, "logit_ev", nth(pair, 3, arg + 1))
                    for j in range(SUB):
                        last = pe.transpose(ch_ps[0:TP, j * P:(j + 1) * P], logT[:, j * TP:(j + 1) * TP], ident[:])
                    inc(last, "logt_mm")
                elif step == "comb_t":
                    wait(pe, "route", nth(pair, 3 * NROUTE, NROUTE * (arg + 1)))
                    c2 = comb2[:, :, :, :].bitcast(F32).rearrange("p j a e -> p j (a e)")
                    for j in range(SUB):
                        last = pe.transpose(ch_ps[0:2 * E, j * TP:(j + 1) * TP], c2[:, j, :], ident[0:TP, 0:TP])
                    inc(last, "comb_mm")

            def down(pair, idx):
                t, m = divmod(idx, M)
                wait(pe, "lo_done", nth(pair, SLOTS, idx + 1))
                if m == 0:
                    wait(pe, "fin_done", nth(pair, 2 * NT, 2 * t))
                hh, hl = hid_hi[:, idx % 2, :], hid_lo[:, idx % 2, :]
                for j in range(SUB):
                    tc = slice(j * TP, (j + 1) * TP)
                    for n, (a, w) in enumerate(((hh, down_hi), (hh, down_lo), (hl, down_hi))):
                        last = pe.matmul(d_ps[0:TP, j, :], a[:, tc], w[:, m, :],
                                         start=(m == 0 and n == 0 and j % 2 == 0),
                                         stop=(m == M - 1 and n == 2), skip_group_check=True)
                inc(last, "down_mm")

            def ffn(pair, idx, before):
                t, m = divmod(idx, M)

                def product(bank, hi_w, lo_w):
                    ms = slice(m * P, (m + 1) * P)
                    for k in range(KD):
                        for n, (w, xx) in enumerate(((hi_w, x_hi), (hi_w, x_lo), (lo_w, x_hi))):
                            last = pe.matmul(bank, w[:, k, ms], xx[:, t, k, :], start=(k == 0 and n == 0),
                                             stop=(k == KD - 1 and n == 2))
                    return last

                if m == 0:
                    wait(pe, "xlo_done", nth(pair, 6, 2 * t + 2))
                wait(pe, "silu_done", nth(pair, SLOTS, idx - 1))
                inc(product(g_ps[:, idx % 2, 0:TT], gate_hi, gate_lo), "gate_mm")
                for step, arg, of in before:
                    chain(step, arg, of)
                if m >= MS:
                    if m == MS:
                        wait(pe, "comb_ev", nth(pair, 3, t + 1))
                    wait(pe, "t_done", nth(pair, NT * MR, t * MR + m - MS))
                    inc(pe.matmul(c_ps[:, 0:TT], sel[:, m - MS, :], combT[:, t, :], start=True, stop=True), "c_mm")
                wait(pe, "hid_done", nth(pair, SLOTS, idx - 1))
                inc(product(u_ps[:, idx % 2, 0:TT], up_hi, up_lo), "up_mm")

            def iteration(pair, have_next, first=False):
                for idx in range(SLOTS):
                    for step, arg, of in chain_at(idx + 0.0, pair, have_next):
                        chain(step, arg, of)
                    ffn(pair, idx, list(chain_at(idx + 0.5, pair, have_next)))
                    if idx:
                        down(pair, idx - 1)
                    elif not first:
                        down(pair - 1, SLOTS - 1)

            for at in sorted(CHAIN):
                for step, arg, of in chain_at(at, -1, True, have_this=False):
                    chain(step, arg, of)
            iteration(0, True, first=True)
            with pe.Fori(1, NP - 1) as i:
                last_pe[0] = ("comb_t", 0, i)
                iteration(i, True)
            last_pe[0] = ("comb_t", 0, NP - 1)
            iteration(NP - 1, False)
            down(NP - 1, SLOTS - 1)


W_CHAIN = 1 + 4 + 4 + 6 + 4 + 6 + 4 + 2 + 1


_INS = ["x", "L0_tok_W", "L0_tok_b", "L0_attn_Wd", "L0_attn_bd", "L0_attn_Wi", "L0_attn_bi", "L0_attn_A_log",
        "L0_attn_Wo", "L0_attn_bo", "L0_attn_Ws", "L0_attn_bs", "L0_ffn_router_w", "L0_ffn_correction_bias",
        "L0_ffn_gate_w", "L0_ffn_up_w", "L0_ffn_down_w", "L0_ffn_shared_gate_w", "L0_ffn_shared_up_w",
        "L0_ffn_shared_down_w"]


def kernel(**inputs):
    import numpy as _np
    import concourse.bacc as _bacc
    from concourse import mybir as _mybir
    from concourse.bass_utils import run_bass_kernel_spmd as _run

    nc = _bacc.Bacc("TRN2", target_bir_lowering=False, num_devices=1)
    arrays, args = {}, []
    for name in _INS:
        a = _np.ascontiguousarray(inputs[name])
        arrays[f"in_{name}_dram"] = a
        args.append(nc.dram_tensor(f"in_{name}_dram", a.shape, _mybir.dt.from_np(a.dtype), kind="ExternalInput").ap())
    shape = (inputs["x"].shape[0], inputs["x"].shape[2], inputs["L0_tok_W"].shape[0])
    args.append(nc.dram_tensor("out_0_dram", shape, _mybir.dt.float32, kind="ExternalOutput").ap())
    audio_tower_kernel(nc, *args)
    r = _run(nc, [arrays], core_ids=[0])
    return r.results[0]["out_0_dram"]
```

```python
from contextlib import ExitStack

import concourse.bass as bass
from concourse import mybir

F32 = mybir.dt.float32
F32R = mybir.dt.float32r
ALU = mybir.AluOpType
ACT = mybir.ActivationFunctionType
AX = mybir.AxisListType

CHAIN = {
    0.0: [(0, "y", (1, 0))],
    0.5: [(0, "y", (1, 1))],
    1.0: [(0, "ln2_stats", 1)],
    1.5: [(1, "ewma", 0)],
    2.0: [(0, "ln2_norm", 1)],
    2.5: [(1, "ewma", 1)],
    3.0: [(0, "x2t", (1, 0))],
    3.5: [(0, "x2t", (1, 1)), (1, "tok", 0)],
    4.0: [(0, "logit", 1), (1, "tok", 1)],
    4.5: [(0, "logit_t", 1), (1, "ln1_stats", 0)],
    5.0: [(1, "tok", 2)],
    5.5: [(1, "tok", 3), (0, "route_scores", 1)],
    6.5: [(1, "ln1_norm", 0), (0, "route_groups", 1)],
    7.0: [(0, "y", (2, 0))],
    7.5: [(0, "y", (2, 1)), (1, "ln1_stats", 1)],
    8.0: [(1, "x1t", (0, 0)), (0, "route_pick", 1)],
    8.5: [(1, "x1t", (0, 1))],
    9.0: [(1, "pre", (0, 0)), (0, "route_weights", 1)],
    9.5: [(1, "tok", 4), (1, "ln1_norm", 1)],
    10.0: [(1, "tok", 5), (1, "ln1_stats", 2)],
    10.5: [(0, "comb_t", 1)],
    11.0: [(1, "x1t", (1, 0))],
    11.5: [(1, "x1t", (1, 1)), (1, "ln1_norm", 2)],

    12.0: [(1, "pre", (0, 1))],
    12.5: [(0, "ln2_stats", 2)],
    13.0: [(1, "x1t", (2, 0))],
    13.5: [(1, "x1t", (2, 1)), (0, "ln2_norm", 2)],
    14.0: [(1, "pre", (0, 2))],
    14.5: [(0, "x2t", (2, 0))],
    15.0: [(0, "x2t", (2, 1)), (1, "ssm_log", 0)],
    15.5: [(0, "logit", 2)],
    16.5: [(0, "logit_t", 2)],
    17.0: [(1, "ssm_decay", 0)],
    17.5: [(0, "route_scores", 2)],
    18.5: [(1, "ssm_scan", 0)],
    19.0: [(0, "route_groups", 2)],
    20.0: [(1, "carry", 0), (0, "route_pick", 2)],
    20.5: [(1, "pre", (1, 0))],
    21.0: [(1, "pre", (1, 1)), (0, "route_weights", 2)],
    21.5: [(1, "pre", (1, 2))],
    22.0: [(1, "ssm_log", 1)],
    22.5: [(0, "comb_t", 2)],
    23.5: [(1, "ssm_decay", 1)],

    24.5: [(1, "ssm_scan", 1)],
    25.5: [(1, "class_row", 0), (1, "residual", 0), (1, "residual", 1)],
    26.0: [(1, "residual", 2)],
    26.5: [(1, "y", (0, 0))],
    27.0: [(1, "y", (0, 1)), (1, "residual", 3)],
    27.5: [(1, "ln2_stats", 0)],
    28.0: [(1, "residual", 4)],
    28.5: [(1, "ln2_norm", 0), (1, "residual", 5)],
    29.5: [(1, "x2t", (0, 0))],
    30.0: [(1, "x2t", (0, 1))],
    30.5: [(1, "logit", 0)],
    31.0: [(1, "logit_t", 0)],
    32.0: [(1, "route_scores", 0)],
    33.0: [(1, "route_groups", 0)],
    34.0: [(1, "route_pick", 0)],
    35.0: [(1, "route_weights", 0)],
    35.5: [(1, "comb_t", 0)],
}

PREPARE = {
    0.0: [("fold", 0)],
    3.0: [("fold", 1), ("fold", 2), ("fold", 3), ("fold", 4)],
    3.5: [("routed", 0), ("softplus", 0)],
    4.0: [("routed", 1)],
    5.0: [("routed", 2)],
    8.0: [("shared", 0)],
    9.5: [("shared", 1)],
    10.0: [("routed", 3)],
    11.0: [("shared", 2)],
    12.0: [("shared", 3)],
    13.5: [("routed", 4)],
    14.0: [("shared", 4)],
    15.0: [("shared", 5)],
    17.0: [("routed", 5)],
    26.5: [("split", 0)],
}


def audio_tower_kernel(nc, x, tok_w, tok_b, wd, bd, wi, bi, a_log, wo, bo, ws, bs, router_w, corr_bias,
                       gate_w, up_w, down_w, sh_gate_w, sh_up_w, sh_down_w, out):
    B, C, T = x.shape
    D = tok_w.shape[0]
    N = wd.shape[2]
    E, _, H = gate_w.shape
    HS = sh_gate_w.shape[0]
    P = 128
    NP = B // 2
    TT = 500
    NT = 2 * T // TT
    TP = 125
    SUB = TT // TP
    NJ = NT * SUB
    KD = D // P
    MS = HS // P
    MR = E * H // P
    M = MS + MR
    NG, EG = 4, E // 4
    SLOTS = NT * M
    ALPHA = 0.1
    EPS = 1e-5
    BIG = 3e38
    RING = 4
    LAG = 2
    W_IN, W_FOLD = 4 + 6 + 1, 4 + 6 + 4 + 4 + 1
    assert C == P and D == 2 * P and 2 * N == P and 2 * H == P and 2 * T == NT * TT and M == 12

    with ExitStack() as ctx:
        def sb(name, shape, dt=F32):
            return ctx.enter_context(nc.sbuf_tensor(name, shape, dt))

        def ps(name, shape):
            return ctx.enter_context(nc.psum_tensor(name, shape, F32))

        def sem(name):
            return ctx.enter_context(nc.semaphore(name))

        gate_hi, gate_lo = (sb(f"gate_{s}", [P, KD, M * P], F32R) for s in ("hi", "lo"))
        up_hi, up_lo = (sb(f"up_{s}", [P, KD, M * P], F32R) for s in ("hi", "lo"))
        down_hi, down_lo = (sb(f"down_{s}", [P, M, D], F32R) for s in ("hi", "lo"))
        stage = sb("stage", [P, 2 * NJ * D])
        h_tok = stage[0:TP, 0:NJ * D].rearrange("p (j d) -> p j d", d=D)
        h2 = stage[0:TP, NJ * D:2 * NJ * D].rearrange("p (j d) -> p j d", d=D)
        x_in = sb("x_in", [P, 2, T])
        ew = sb("ew", [P, 2, T])
        ends10 = sb("ends10", [P, 2, 2])
        xn1 = sb("xn1", [TP, SUB, D])
        xn2 = sb("xn2", [TP, SUB, D])
        x1T = sb("x1T", [P, KD, TT])
        x_hi = sb("x_hi", [P, NT, KD, TT], F32R)
        x_lo = sb("x_lo", [P, NT, KD, TT], F32R)
        zt = sb("zt", [P, T])
        ut = sb("ut", [P, T])
        t1 = sb("t1", [P, T])
        t2 = sb("t2", [P, T])
        hs1 = sb("hs1", [P, T])
        blocks = sb("blocks", [P, 4, TT])
        sg, hid = blocks[:, 0:2, :], blocks[:, 2:4, :]
        hid_hi = sb("hid_hi", [P, 3, TT], F32R)
        hid_lo = sb("hid_lo", [P, 3, TT], F32R)
        cb = sb("cb", [P, RING, TT])
        comb_dram = nc.dram_tensor("comb_scratch", (NT, E, TT), F32, kind="Internal").ap()
        ident = sb("ident", [P, P])
        tokwT = sb("tokwT", [P, D])
        wdi0 = sb("wdi0", [P, 2, KD, P])
        g1 = sb("g1", [P, 2, P])
        sbd = sb("sbd", [P, 2, P])
        wo1 = sb("wo1", [P, 2, D])
        ws1 = sb("ws1", [P, 2, D])
        tokb_bc = sb("tokb_bc", [TP, D])
        brow = sb("brow", [TP, D])
        rows = sb("rows", [TP, 2, D])
        rw_hi = sb("rw_hi", [P, KD, E], F32R)
        rw_lo = sb("rw_lo", [P, KD, E], F32R)
        corr_bc = sb("corr_bc", [TP, E])
        vecs = sb("vecs", [P, 6])
        nspa = sb("nspa", [P, 2])
        spt = sb("spt", [P, 4])
        bias1 = sb("bias1", [P, 2])
        bias1s = sb("bias1s", [P, 2])
        c09 = sb("c09", [P, 1])
        mhalf = sb("mhalf", [TP, SUB])
        stats = [sb(f"stats{n}", [TP, SUB, 6]) for n in (1, 2)]
        halves = [sb(f"halves{n}", [TP, SUB, 2]) for n in (1, 2)]
        mv = [sb(f"mv{n}", [TP, SUB, 2]) for n in (1, 2)]
        rstd = [sb(f"rstd{n}", [TP, SUB]) for n in (1, 2)]
        logT = sb("logT", [P, TT])
        combT = logT[0:E, :]
        sc = sb("sc", [TP, SUB * E])
        sbias = sb("sbias", [TP, SUB * E])
        pairs6 = sb("pairs6", [TP, SUB * NG, 6])
        gs = sb("gs", [TP, SUB, NG])
        ge1 = sb("ge1", [TP, SUB, NG])
        ge2 = sb("ge2", [TP, SUB, 2])
        ge3 = sb("ge3", [TP, SUB, 1])
        winit = sb("winit", [TP, SUB, NG])
        wins = sb("wins", [TP, SUB, NG])
        gmask = sb("gmask", [TP, SUB * NG])
        gpen = sb("gpen", [TP, SUB * NG])
        masked = sbias
        top8 = sb("top8", [TP, SUB, 8])
        marks = sb("marks", [TP, SUB, 8])
        gscore = pairs6[:, :, :].rearrange("p g n -> p (g n)")[:, 0:SUB * E]
        marked = sb("marked", [TP, SUB * E])
        wsel = sb("wsel", [TP, SUB * E])
        wsum = sb("wsum", [TP, SUB])
        wraw = zt[:, 0:2 * P].rearrange("p (k c) -> p k c", k=KD)
        rraw = t2[0:E, 2 * P:4 * P]
        wos = ut[:, 0:2 * D].rearrange("p (o d) -> p o d", o=2)
        wosT = t1[:, 0:4 * P].rearrange("p (o k n) -> p o k n", o=2, k=KD)
        wdi1 = t2[:, 0:2 * P].rearrange("p (k n) -> p k n", k=KD)
        wdup = hs1[:, 0:4 * P].rearrange("p (s k n) -> p s k n", s=2, k=KD)
        bcol = sb("bcol", [P, KD, 2])
        bsum = sb("bsum", [P, KD])
        CH = E * H
        chunk = [stage[:, (NJ * D) + n * CH:(NJ * D) + (n + 1) * CH] for n in range(NT)]
        routed_parts = []
        for hi_t, lo_t in ((gate_hi, gate_lo), (up_hi, up_lo)):
            routed_parts += [(hi_t[:, k, HS:], lo_t[:, k, HS:]) for k in range(KD)]
        for m0 in (MS, MS + MR // 2):
            routed_parts.append(tuple(w[:, m0:m0 + MR // 2, :].rearrange("p m d -> p (m d)")
                                      for w in (down_hi, down_lo)))
        sh_a = blocks[:, :, :].rearrange("p a n -> p (a n)")[:, 0:MS * D]
        sh_b = cb[:, :, :].rearrange("p a n -> p (a n)")[:, 0:MS * D]
        sh_raw = [sh_a, sh_b, sh_a]

        g_ps = ps("g_ps", [P, 2, 512])
        u_ps = ps("u_ps", [P, 2, 512])
        ch_ps = ps("ch_ps", [P, 2, 512])
        d_ps = ps("d_ps", [P, SUB, D])
        fold_ps = [g_ps[:, 0, :], g_ps[:, 1, :], u_ps[:, 0, :], u_ps[:, 1, :],
                   d_ps[:, 0:2, :].rearrange("p j d -> p (j d)")]
        shared_ps = fold_ps + [d_ps[:, 2:4, :].rearrange("p j d -> p (j d)")]

        S = {name: sem(name) for name in (
            "x_in", "zeroed", "w_tok", "w_in", "w_fold", "w_routed0", "w_routed1", "w_routed2", "w_shared0",
            "w_shared1", "ident_done", "const_done", "fold_mm", "fold_ev", "rw_hi_done", "spa", "spa_dve",
            "routed_hi", "routed_lo", "shared_mm", "shared_hi", "shared_lo",
            "ends_done", "scan_done", "ew_done", "tok_mm", "tok_ev", "st1", "aggr1", "rstd1", "xn1",
            "x1t_mm", "x1t_ev", "pre_mm", "z_ev", "u_ev", "abs_done", "relu_done", "exp_done", "ln_done",
            "delta_done", "decay_done", "drive_done", "ssm_done", "carry_mm", "carry_ev",
            "row_mm", "row_ev", "res_done", "y_mm", "y_ev", "st2", "aggr2", "rstd2", "xn2", "x2t_mm",
            "xhi_done", "xlo_done", "logit_mm", "logit_ev", "logt_mm", "score_exp", "route", "comb_mm", "comb_ev",
            "comb_st", "cb0", "cb1", "cb2", "cb3", "gate_mm", "up_mm", "down_mm", "silu_done", "t_done",
            "hid_done", "hi_done", "lo_done", "fin_done", "out0", "out1", "out2")}
        OUT = [S["out0"], S["out1"], S["out2"]]

        def nth(pair, per_pair, n):
            return pair * per_pair + n

        def wait(eng, name, value):
            if not (isinstance(value, int) and value <= 0):
                eng.wait_ge(S[name], value)

        def inc(ins, name):
            return ins.then_inc(S[name], 1)

        ZU = [1, 3, 4]
        ROUTE = {"scores": 0, "groups": 10, "pick": 18, "weights": 26}
        NROUTE = 30
        NAGGR = 7

        def reads_of(step, arg, pair):
            if step == "tok":
                return [("tok_ev", nth(pair, 6, arg + 1))]
            if step == "x1t":
                return [("x1t_ev", nth(pair, 6, 2 * arg[0] + arg[1] + 1))]
            if step == "pre":
                v = nth(pair, 8, 4 * arg[0] + ZU[arg[1]])
                return [("z_ev", v), ("u_ev", v)]
            if step == "carry":
                return [("carry_ev", nth(pair, 1, 1))]
            if step == "class_row":
                return [("row_ev", nth(pair, 1, 1))]
            if step == "y":
                return [("y_ev", nth(pair, 6, 2 * arg[0] + arg[1] + 1))]
            if step == "x2t":
                return [("xlo_done", nth(pair, 6, 2 * arg[0] + arg[1] + 1))]
            if step == "logit":
                return [("logit_ev", nth(pair, 3, arg + 1))]
            if step == "logit_t":
                return [("score_exp", nth(pair, 3, arg + 1))]
            if step == "comb_t":
                return [("comb_ev", nth(pair, 3, arg + 1))]
            return None

        PE_STEPS = ("tok", "x1t", "pre", "carry", "class_row", "y", "x2t", "logit", "logit_t", "comb_t")
        in_order = [(which, step, arg) for at in sorted(CHAIN) for which, step, arg in CHAIN[at] if step in PE_STEPS]
        bank_of = {(step, arg): n % 2 for n, (_, step, arg) in enumerate(in_order)}
        last_in = [None, None]

        def ch(step, arg):
            return ch_ps[:, bank_of[step, arg], :]

        def banks_at_loop(pair):
            for which, step, arg in in_order:
                last_in[bank_of[step, arg]] = (step, arg, pair + which - 1)

        def chain_at(at, pair, have_next, have_this=True):
            for which, step, arg in CHAIN.get(at, ()):
                if which == 1 and have_next:
                    yield step, arg, pair + 1
                if which == 0 and have_this:
                    yield step, arg, pair

        def shared_part(n):
            if n < 2 * KD:
                pair_ = ((gate_hi, gate_lo), (up_hi, up_lo))[n // KD]
                return [w[:, n % KD, 0:HS].rearrange("p (m c) -> p m c", m=MS) for w in pair_]
            return [w[:, 0:MS, (n % KD) * P:(n % KD + 1) * P] for w in (down_hi, down_lo)]

        def shared_view(n):
            return shared_ps[n].rearrange("p (m c) -> p m c", m=MS)

        def pieces(s):
            got = []
            for b in range(2):
                lo, hi = max(s * TT, b * T), min((s + 1) * TT, (b + 1) * T)
                if lo < hi:
                    got.append((b, lo - b * T, hi - lo, lo - s * TT))
            return got

        def cols(j):
            return j // (NJ // 2), (j % (NJ // 2)) * TP

        block = ctx.enter_context(nc.Block())

        x_v = x.rearrange("(q b) c t -> q c b t", b=2)
        out_v = out.rearrange("(q b) t d -> q (b t) d", b=2).rearrange("q (t j p) d -> q t p j d", t=NT, p=TP)

        @block.sync
        def _(sp):
            sp.dma_start(wraw, tok_w.rearrange("(k p) c -> p k c", p=P)).then_inc(S["w_tok"], 16)
            sp.dma_start(x_in[:], x_v[0]).then_inc(S["x_in"], 16)
            for o, (a, b) in enumerate(((wd, wi), (wi, wd))):
                sp.dma_start(wdi0[:, o, :, 0:N], a[0].rearrange("(k p) n -> p k n", p=P)).then_inc(S["w_in"], 16)
                sp.dma_start(wdi0[:, o, :, N:P], b[0].rearrange("(k p) n -> p k n", p=P)).then_inc(S["w_in"], 16)
            for o, (a, b) in enumerate(((wo, ws), (ws, wo))):
                sp.dma_start(wos[0:N, o, :], a[0]).then_inc(S["w_fold"], 16)
                sp.dma_start(wos[N:P, o, :], b[0]).then_inc(S["w_fold"], 16)
            for o, a in enumerate((wd, wi)):
                a1 = a[1].rearrange("(k p) n -> p k n", p=P)
                sp.dma_start(wdi1[:, :, o * N:(o + 1) * N], a1).then_inc(S["w_fold"], 16)
                for half in range(2):
                    sp.dma_start(wdup[:, o, :, half * N:(half + 1) * N], a1).then_inc(S["w_fold"], 16)
            sp.wait_ge(S["zeroed"], 2)
            for b in range(2):
                sp.dma_start(wo1[b * N:(b + 1) * N, b, :], wo[1]).then_inc(S["w_fold"], 16)
                sp.dma_start(ws1[b * N:(b + 1) * N, b, :], ws[1]).then_inc(S["w_fold"], 16)

            def routed_chunk(n):
                sm = S[f"w_routed{n % NT}"]
                if n >= NT:
                    sp.wait_ge(S["routed_lo"], n - NT + 1)
                if n < 2 * KD:
                    src, k = (gate_w, up_w)[n // KD], n % KD
                    sp.dma_start(chunk[n % NT].rearrange("p (e h) -> p e h", e=E),
                                 src[:, k * P:(k + 1) * P, :].rearrange("e p h -> p e h")).then_inc(sm, 16)
                else:
                    m0 = (n - 2 * KD) * MR // 2
                    rows_ = down_w.rearrange("e h d -> (e h) d").rearrange("(m p) d -> p m d", p=P)
                    sp.dma_start(chunk[n % NT].rearrange("p (m d) -> p m d", d=D),
                                 rows_[:, m0:m0 + MR // 2, :]).then_inc(sm, 16)

            for n in range(NT):
                routed_chunk(n)
            for n, w in enumerate((sh_gate_w, sh_up_w)):
                sp.dma_start(sh_raw[n].rearrange("p (m c) -> p m c", m=MS),
                             w.rearrange("(m p) c -> p m c", p=P)).then_inc(S[f"w_shared{n}"], 16)
            for n in range(NT, 2 * NT):
                routed_chunk(n)
            sp.wait_ge(S["shared_mm"], KD)
            sp.dma_start(sh_raw[2].rearrange("p (k n) -> p k n", k=KD),
                         sh_down_w.rearrange("(k p) n -> p k n", p=P)).then_inc(S["w_shared0"], 16)

            def load_x(pair):
                wait(sp, "ew_done", nth(pair - 1, 2, 2))
                sp.dma_start(x_in[:], x_v[pair]).then_inc(S["x_in"], 16)

            def store(pair, t):
                wait(sp, "fin_done", nth(pair, 2 * NT, 2 * t + 2))
                sp.dma_start(out_v[pair, t], h2[:, t * SUB:(t + 1) * SUB, :]).then_inc(OUT[t], 16)

            def store_comb(t, pair):
                wait(sp, "comb_ev", nth(pair, NT, t + 1))
                sp.dma_start(comb_dram[t], combT).then_inc(S["comb_st"], 16)

            def load_comb(pair, t, m):
                if m == 0:
                    wait(sp, "comb_st", nth(pair, 16 * NT, 16 * (t + 1)))
                else:
                    wait(sp, "t_done", nth(pair, NT * MR, t * MR + m - RING + 1))
                for a in range(2):
                    sp.dma_start(cb[a * H:(a + 1) * H, m % RING, :],
                                 comb_dram[t, 2 * m + a].partition_broadcast(H)).then_inc(S[f"cb{m % RING}"], 16)

            def iteration(pair, have_next, first=False):
                if have_next:
                    load_x(pair + 1)
                for idx in range(SLOTS):
                    t, m = divmod(idx, M)
                    if m < MR:
                        load_comb(pair, t, m)
                    if m == 2 and idx > M:
                        store(pair, t - 1)
                    elif m == 2 and not first:
                        store(pair - 1, NT - 1)
                    for half in (0.0, 0.5):
                        for step, arg, of in chain_at(idx + half, pair, have_next):
                            if step == "comb_t":
                                store_comb(arg, of)

            store_comb(0, 0)
            iteration(0, True, first=True)
            with sp.Fori(1, NP - 1) as i:
                iteration(i, True)
            iteration(NP - 1, False)
            store(NP - 1, NT - 1)
            for t in range(NT):
                sp.wait_ge(OUT[t], 16 * NP)

        @block.gpsimd
        def _(pool):
            pool.memset(ident[:], 0.0).then_inc(S["ident_done"], 1)
            pool.wait_ge(S["ident_done"], 1)
            pool.affine_select(out=ident[:], in_=ident[:], compare_op=ALU.not_equal, fill=1.0, base=0,
                               pattern=[[-1, P]], channel_multiplier=1).then_inc(S["ident_done"], 1)

            def prepare(what, n):
                if what == "routed":
                    hi_p, lo_p = routed_parts[n]
                    pool.wait_ge(S["routed_hi"], n + 1)
                    inc(pool.tensor_tensor(lo_p, chunk[n % NT], hi_p.bitcast(F32), ALU.subtract), "routed_lo")

            def chain(step, arg, pair):
                if step == "ewma":
                    wait(pool, "scan_done", nth(pair, 4, 2 * arg + 2))
                    inc(pool.tensor_tensor(ew[:, arg, :], ew[:, arg, :], x_in[:, arg, :], ALU.add), "ew_done")
                elif step in ("ln1_stats", "ln2_stats"):
                    n = int(step[2]) - 1
                    wait(pool, f"aggr{n + 1}", nth(pair, NT * NAGGR, NAGGR * (arg + 1)))
                    wait(pool, f"xn{n + 1}", nth(pair, 3, arg))
                    inc(pool.tensor_tensor(rstd[n][:], mv[n][:, :, 1], mhalf[:], ALU.pow), f"rstd{n + 1}")
                elif step == "residual":
                    wait(pool, "row_ev", nth(pair, 1, 1))
                    wait(pool, "xn1", nth(pair, 3, 3))
                    hv = h_tok[:, 2 * arg:2 * arg + 2, :]
                    row = rows[:, arg // 3, :].unsqueeze(1).broadcast_to([TP, 2, D])
                    inc(pool.tensor_tensor(hv, hv, row, ALU.add), "res_done")

            def ffn(pair, idx):
                wait(pool, "hi_done", nth(pair, SLOTS, idx + 1))
                wait(pool, "down_mm", nth(pair, SLOTS, idx - 2))
                inc(pool.tensor_tensor(hid_lo[:, idx % 3, :], hid[:, idx % 2, :],
                                       hid_hi[:, idx % 3, :].bitcast(F32), ALU.subtract), "lo_done")

            def iteration(pair, have_next):
                for idx in range(SLOTS):
                    for half in (0.0, 0.5):
                        for step, arg, of in chain_at(idx + half, pair, have_next):
                            chain(step, arg, of)
                    ffn(pair, idx)

            pool.wait_ge(S["const_done"], 2)
            for at in sorted({*CHAIN, *PREPARE}):
                for what, n in PREPARE.get(at, ()):
                    prepare(what, n)
                for step, arg, of in chain_at(at, -1, True, have_this=False):
                    chain(step, arg, of)
            iteration(0, True)
            with pool.Fori(1, NP - 1) as i:
                iteration(i, True)
            iteration(NP - 1, False)

        @block.scalar
        def _(act):
            act.dma_start(tokb_bc[:], tok_b.partition_broadcast(TP)).then_inc(S["w_tok"], 16)
            for half in (vecs[0:N, :], vecs[N:P, :]):
                for n, a in enumerate((bd, bi, a_log)):
                    act.dma_start(half[:, 2 * n:2 * n + 2], a.rearrange("l n -> n l"),
                                  allow_slow_non_contiguous=True).then_inc(S["w_in"], 16)
            act.dma_start(corr_bc[:], corr_bias.partition_broadcast(TP)).then_inc(S["w_in"], 16)
            for n, (a, dst) in enumerate(((bo, brow[:]), (bs, rows[:, 0, :]))):
                act.dma_start(bcol[:, :, n:n + 1], a[0].rearrange("(k p a) -> p k a", p=P, a=1),
                              allow_slow_non_contiguous=True).then_inc(S["w_fold"], 16)
                act.dma_start(dst, a[1].partition_broadcast(TP)).then_inc(S["w_fold"], 16)
            act.dma_start(rraw, router_w[:, :]).then_inc(S["w_fold"], 16)

            def prepare(what, n):
                if what == "softplus":
                    act.wait_ge(S["w_in"], 16 * W_IN)
                    inc(act.activation(spt[:, 0:2], vecs[:, 4:6], ACT.Abs), "spa")
                    act.wait_ge(S["spa"], 1)
                    inc(act.activation(spt[:, 2:4], spt[:, 0:2], ACT.Exp, scale=-1.0), "spa")
                    act.wait_ge(S["spa"], 2)
                    inc(act.activation(spt[:, 0:2], spt[:, 2:4], ACT.Ln, bias=1.0), "spa")
                elif what == "routed":
                    act.wait_ge(S[f"w_routed{n % NT}"], 16 * (n // NT + 1))
                    inc(act.activation(routed_parts[n][0], chunk[n % NT], ACT.Copy), "routed_hi")
                elif what == "shared":
                    act.wait_ge(S["shared_mm"], n + 1)
                    inc(act.activation(shared_part(n)[0], shared_view(n), ACT.Copy), "shared_hi")

            def chain(step, arg, pair):
                if step == "x1t":
                    t, k = arg
                    wait(act, "x1t_mm", nth(pair, 6, 2 * t + k + 1))
                    if k == 0:
                        wait(act, "pre_mm", nth(pair, 6, t) if t else nth(pair - 1, 6, 3))
                    inc(act.activation(x1T[:, k, :], ch(step, arg)[:, 0:TT], ACT.Copy), "x1t_ev")
                elif step == "pre":
                    layer, s = arg
                    wait(act, "pre_mm", nth(pair, 6, 3 * layer + s + 1))
                    wait(act, "ssm_done", nth(pair, 2, layer))
                    for b, c0, n, at in pieces(s):
                        src = ch(step, arg)[0:N, at:at + n] if b == 0 else ch(step, arg)[N:P, at:at + n]
                        inc(act.activation(zt[b * N:(b + 1) * N, c0:c0 + n], src, ACT.Copy), "z_ev")
                elif step == "ssm_log":
                    bz = vecs[:, 0:1] if arg == 0 else bias1s[:, 0:1]
                    wait(act, "z_ev", nth(pair, 8, 4 * arg + 4))
                    if arg == 0:
                        wait(act, "delta_done", nth(pair - 1, 2, 2))
                    else:
                        wait(act, "pre_mm", nth(pair, 6, 6))
                        wait(act, "carry_ev", nth(pair, 1, 1))
                    inc(act.activation(t1[:], zt[:], ACT.Abs, bias=bz), "abs_done")
                    wait(act, "abs_done", nth(pair, 2, arg + 1))
                    inc(act.activation(t1[:], t1[:], ACT.Exp, scale=-1.0), "exp_done")
                    wait(act, "exp_done", nth(pair, 2, arg + 1))
                    inc(act.activation(t1[:], t1[:], ACT.Ln, bias=1.0), "ln_done")
                elif step == "ssm_decay":
                    wait(act, "delta_done", nth(pair, 2, arg + 1))
                    inc(act.activation(zt[:], t2[:], ACT.Exp, scale=nspa[:, arg:arg + 1]), "decay_done")
                elif step == "x2t":
                    t, k = arg
                    wait(act, "x2t_mm", nth(pair, 6, 2 * t + k + 1))
                    if k == 0:
                        wait(act, "up_mm", nth(pair - 1, SLOTS, M * (t + 1)))
                    inc(act.activation(x_hi[:, t, k, :], ch(step, arg)[:, 0:TT], ACT.Copy), "xhi_done")
                elif step == "logit":
                    wait(act, "logit_mm", nth(pair, 3, arg + 1))
                    wait(act, "comb_st", nth(pair, 16 * NT, 16 * arg))
                    inc(act.activation(logT[0:E, :], ch(step, arg)[0:E, 0:TT], ACT.Copy), "logit_ev")
                elif step == "logit_t":
                    wait(act, "logt_mm", nth(pair, 3, arg + 1))
                    wait(act, "route", nth(pair, 3 * NROUTE, NROUTE * arg))
                    inc(act.activation(sc[:, :].rearrange("p (j e) -> p j e", e=E),
                                       ch(step, arg)[0:TP, :].rearrange("p (j e) -> p j e", j=SUB)[:, :, 0:E],
                                       ACT.Exp, scale=-1.0), "score_exp")
                elif step == "comb_t":
                    wait(act, "comb_mm", nth(pair, 3, arg + 1))
                    inc(act.activation(combT, ch(step, arg)[0:E, 0:TT], ACT.Copy), "comb_ev")

            def ffn(pair, idx):
                wait(act, "gate_mm", nth(pair, SLOTS, idx + 1))
                wait(act, "hid_done", nth(pair, SLOTS, idx - 1))
                inc(act.activation(sg[:, idx % 2, :], g_ps[:, idx % 2, 0:TT], ACT.Silu), "silu_done")

            def ffn_hi(pair, idx):
                wait(act, "hid_done", nth(pair, SLOTS, idx + 1))
                wait(act, "down_mm", nth(pair, SLOTS, idx - 2))
                inc(act.activation(hid_hi[:, idx % 3, :], hid[:, idx % 2, :], ACT.Copy), "hi_done")

            def iteration(pair, have_next):
                for idx in range(SLOTS):
                    for step, arg, of in chain_at(idx + 0.0, pair, have_next):
                        chain(step, arg, of)
                    ffn(pair, idx)
                    for step, arg, of in chain_at(idx + 0.5, pair, have_next):
                        chain(step, arg, of)
                    ffn_hi(pair, idx)

            for at in sorted({*CHAIN, *PREPARE}):
                for what, n in PREPARE.get(at, ()):
                    prepare(what, n)
                for step, arg, of in chain_at(at, -1, True, have_this=False):
                    chain(step, arg, of)
            iteration(0, True)
            with act.Fori(1, NP - 1) as i:
                iteration(i, True)
            iteration(NP - 1, False)

        @block.vector
        def _(dve):
            inc(dve.memset(wo1[:], 0.0), "zeroed")
            inc(dve.memset(ws1[:], 0.0), "zeroed")
            inc(dve.memset(g1[:], 0.0), "zeroed")
            inc(dve.memset(sbd[:], 0.0), "zeroed")
            inc(dve.memset(ge1[:], 0.0), "zeroed")
            inc(dve.memset(logT[:], 0.0), "zeroed")
            for g in range(NG):
                dve.memset(winit[:, :, g:g + 1], float(g))
            inc(dve.memset(c09[:], 1.0 - ALPHA), "const_done")
            inc(dve.memset(mhalf[:], -0.5), "const_done")
            dve.wait_ge(S["const_done"], 2)

            def prepare(what, n):
                lo_, hi_ = slice(0, N), slice(N, P)
                if what == "fold" and n == 0:
                    dve.wait_ge(S["fold_mm"], 1)
                    inc(dve.tensor_scalar(tokwT[:], fold_ps[0][:, 0:D], 0.5 * ALPHA, None, ALU.mult), "fold_ev")
                    dve.wait_ge(S["w_tok"], 32)
                elif what == "fold" and n == 1:
                    dve.wait_ge(S["fold_mm"], 2)
                    inc(dve.tensor_copy(wosT, fold_ps[1].rearrange("p (o k n) -> p o k n", o=2, k=KD)), "fold_ev")
                    dve.wait_ge(S["w_fold"], 16 * W_FOLD)
                    inc(dve.tensor_tensor(bsum[:], bcol[:, :, 0], bcol[:, :, 1], ALU.add), "fold_ev")
                    inc(dve.tensor_tensor(brow[:], brow[:], rows[:, 0, :], ALU.add), "fold_ev")
                elif what == "fold" and n == 2:
                    dve.wait_ge(S["fold_mm"], 3)
                    dve.wait_ge(S["zeroed"], 4)
                    p0, p1 = fold_ps[2][:, 0:P], fold_ps[2][:, P:2 * P]
                    for dst, src in (
                        (g1[lo_, 0, :], p0[lo_, :]),
                        (g1[hi_, 1, lo_], p1[hi_, hi_]), (g1[hi_, 1, hi_], p1[hi_, lo_]),
                        (sbd[lo_, 0, lo_], p1[lo_, lo_]), (sbd[hi_, 0, hi_], p0[hi_, lo_]),
                        (sbd[lo_, 1, lo_], p1[lo_, hi_]), (sbd[hi_, 1, hi_], p0[hi_, hi_]),
                    ):
                        last = dve.tensor_copy(dst, src)
                    inc(last, "fold_ev")
                elif what == "fold" and n == 3:
                    dve.wait_ge(S["fold_mm"], 4)
                    dve.wait_ge(S["w_in"], 16 * W_IN)
                    for s in range(2):
                        last = dve.tensor_tensor(bias1[:, s:s + 1], fold_ps[3][:, s:s + 1],
                                                 vecs[:, 2 * s + 1:2 * s + 2], ALU.add)
                    inc(last, "fold_ev")
                elif what == "fold" and n == 4:
                    dve.wait_ge(S["fold_mm"], 5)
                    rwT_ps = fold_ps[4][:, 0:KD * E].rearrange("p (k e) -> p k e", k=KD)
                    inc(dve.tensor_copy(rw_hi[:], rwT_ps), "rw_hi_done")
                    dve.wait_ge(S["rw_hi_done"], 1)
                    inc(dve.tensor_tensor(rw_lo[:], rwT_ps, rw_hi[:, :, :].bitcast(F32), ALU.subtract), "fold_ev")
                elif what == "softplus":
                    dve.wait_ge(S["spa"], 3)
                    inc(dve.tensor_scalar(spt[:, 2:4], vecs[:, 4:6], 0.0, None, ALU.max), "spa_dve")
                    dve.wait_ge(S["spa_dve"], 1)
                    inc(dve.tensor_tensor(spt[:, 2:4], spt[:, 2:4], spt[:, 0:2], ALU.add), "spa_dve")
                    dve.wait_ge(S["spa_dve"], 2)
                    inc(dve.tensor_scalar(nspa[:], spt[:, 2:4], -1.0, None, ALU.mult), "spa_dve")
                elif what == "shared":
                    dve.wait_ge(S["shared_hi"], n + 1)
                    hi_p, lo_p = shared_part(n)
                    inc(dve.tensor_tensor(lo_p, shared_view(n), hi_p.bitcast(F32), ALU.subtract), "shared_lo")
                elif what == "split":
                    dve.wait_ge(S["routed_lo"], 2 * NT)

            def routed(ins, pair, tile, n):
                inc(ins, "route")
                wait(dve, "route", nth(pair, 3 * NROUTE, NROUTE * tile + n))

            def chain(step, arg, pair):
                if step == "ewma":
                    b = arg
                    if b == 0:
                        wait(dve, "x_in", nth(pair, 16, 16))
                        inc(dve.tensor_scalar(ends10[:], x_in[:, :, 0:T:T - 1], 1.0 / ALPHA, None, ALU.mult),
                            "ends_done")
                    wait(dve, "ends_done", nth(pair, 1, 1))
                    wait(dve, "tok_mm", nth(pair - 1, 6, 3 * (b + 1)))
                    decay = c09[:, 0:1].broadcast_to([P, T])
                    inc(dve.tensor_tensor_scan(ew[:, b, :], decay, x_in[:, b, :], ends10[:, b, 0:1],
                                               ALU.mult, ALU.add), "scan_done")
                    wait(dve, "scan_done", nth(pair, 4, 2 * b + 1))
                    inc(dve.tensor_tensor_scan(x_in[:, b, T - 1::-1], decay, x_in[:, b, T - 1::-1],
                                               ends10[:, b, 1:2], ALU.mult, ALU.add), "scan_done")
                elif step == "tok":
                    wait(dve, "tok_mm", nth(pair, 6, arg + 1))
                    wait(dve, "y_ev", nth(pair - 1, 6, arg + 1))
                    hv = h_tok[:, 2 * arg:2 * arg + 2, :]
                    inc(dve.tensor_tensor(hv, ch(step, arg)[0:TP, :].rearrange("p (j d) -> p j d", d=D),
                                          tokb_bc[:, :].unsqueeze(1).broadcast_to([TP, 2, D]), ALU.add), "tok_ev")
                    wait(dve, "tok_ev", nth(pair, 6, arg + 1))
                    for j in range(2):
                        inc(dve.bn_stats(stats[0][:, (2 * arg + j) % SUB, :], hv[:, j, :]), "st1")
                elif step in ("ln1_stats", "ln2_stats"):
                    n = int(step[2]) - 1
                    wait(dve, f"st{n + 1}", nth(pair, NJ, SUB * (arg + 1)))
                    wait(dve, f"xn{n + 1}", nth(pair, 3, arg))
                    st, sq, a = stats[n], halves[n], f"aggr{n + 1}"
                    v0 = NAGGR * arg
                    inc(dve.tensor_tensor(mv[n][:, :, 0], st[:, :, 1], st[:, :, 4], ALU.add), a)
                    inc(dve.tensor_tensor(sq[:, :, 0], st[:, :, 1], st[:, :, 4], ALU.subtract), a)
                    inc(dve.tensor_tensor(sq[:, :, 1], st[:, :, 2], st[:, :, 5], ALU.add), a)
                    wait(dve, a, nth(pair, NT * NAGGR, v0 + 3))
                    inc(dve.tensor_scalar(mv[n][:, :, 0], mv[n][:, :, 0], 0.5, None, ALU.mult), a)
                    inc(dve.scalar_tensor_tensor(sq[:, :, 0], sq[:, :, 0], 0.25, sq[:, :, 0], ALU.mult, ALU.mult), a)
                    inc(dve.tensor_scalar(sq[:, :, 1], sq[:, :, 1], 1.0 / D, EPS, ALU.mult, ALU.add), a)
                    wait(dve, a, nth(pair, NT * NAGGR, v0 + 6))
                    inc(dve.tensor_tensor(mv[n][:, :, 1], sq[:, :, 1], sq[:, :, 0], ALU.add), a)
                elif step in ("ln1_norm", "ln2_norm"):
                    n = int(step[2]) - 1
                    src, dst = (h_tok, xn1) if n == 0 else (h2, xn2)
                    wait(dve, f"rstd{n + 1}", nth(pair, 3, arg + 1))
                    wait(dve, f"x{n + 1}t_mm", nth(pair, 6, 2 * arg))
                    for j in range(SUB):
                        last = dve.tensor_scalar(dst[:, j, :], src[:, arg * SUB + j, :], mv[n][:, j, 0:1],
                                                 rstd[n][:, j:j + 1], ALU.subtract, ALU.mult)
                    inc(last, f"xn{n + 1}")
                elif step == "pre":
                    layer, s = arg
                    wait(dve, "pre_mm", nth(pair, 6, 3 * layer + s + 1))
                    wait(dve, "ssm_done", nth(pair, 2, layer))
                    if len(pieces(s)) > 1:
                        wait(dve, "z_ev", nth(pair, 8, 4 * layer + ZU[s]))
                    for b, c0, n, at in pieces(s):
                        src = ch(step, arg)[N:P, at:at + n] if b == 0 else ch(step, arg)[0:N, at:at + n]
                        inc(dve.tensor_copy(ut[b * N:(b + 1) * N, c0:c0 + n], src), "u_ev")
                elif step == "ssm_log":
                    bz = vecs[:, 0:1] if arg == 0 else bias1s[:, 0:1]
                    wait(dve, "z_ev", nth(pair, 8, 4 * arg + 4))
                    if arg == 1:
                        wait(dve, "carry_ev", nth(pair, 1, 1))
                    inc(dve.tensor_scalar(t2[:], zt[:], bz, 0.0, ALU.add, ALU.max), "relu_done")
                elif step == "ssm_decay":
                    wait(dve, "ln_done", nth(pair, 2, arg + 1))
                    wait(dve, "relu_done", nth(pair, 2, arg + 1))
                    inc(dve.tensor_tensor(t2[:], t1[:], t2[:], ALU.add), "delta_done")
                    bu = vecs[:, 2:3] if arg == 0 else bias1s[:, 1:2]
                    wait(dve, "delta_done", nth(pair, 2, arg + 1))
                    wait(dve, "u_ev", nth(pair, 8, 4 * arg + 4))
                    inc(dve.scalar_tensor_tensor(ut[:], ut[:], bu, t2[:], ALU.add, ALU.mult), "drive_done")
                elif step == "ssm_scan":
                    wait(dve, "decay_done", nth(pair, 2, arg + 1))
                    wait(dve, "drive_done", nth(pair, 2, arg + 1))
                    if arg == 1:
                        wait(dve, "y_mm", nth(pair - 1, 6, 6))
                    inc(dve.tensor_tensor_scan(t1[:] if arg == 0 else hs1[:], zt[:], ut[:], 0.0,
                                               ALU.mult, ALU.add), "ssm_done")
                elif step == "carry":
                    wait(dve, "carry_mm", nth(pair, 1, 1))
                    inc(dve.tensor_tensor(bias1s[:], ch(step, arg)[:, 0:2], bias1[:], ALU.add), "carry_ev")
                elif step == "class_row":
                    wait(dve, "row_mm", nth(pair, 1, 1))
                    wait(dve, "res_done", nth(pair - 1, 6, 6))
                    inc(dve.tensor_tensor(rows[:], ch(step, arg)[0:TP, :].rearrange("p (b d) -> p b d", b=2),
                                          brow[:, :].unsqueeze(1).broadcast_to([TP, 2, D]), ALU.add), "row_ev")
                elif step == "y":
                    t, q = arg
                    j = t * SUB + 2 * q
                    wait(dve, "y_mm", nth(pair, 6, 2 * t + q + 1))
                    wait(dve, "res_done", nth(pair, 6, 2 * t + q + 1))
                    if not (isinstance(pair, int) and pair == 0):
                        dve.wait_ge(OUT[t], nth(pair, 16, 0))
                    hv = h2[:, j:j + 2, :]
                    inc(dve.tensor_tensor(hv, ch(step, arg)[0:TP, :].rearrange("p (j d) -> p j d", d=D),
                                          h_tok[:, j:j + 2, :], ALU.add), "y_ev")
                    wait(dve, "y_ev", nth(pair, 6, 2 * t + q + 1))
                    if q == 0:
                        wait(dve, "aggr2", nth(pair, NT * NAGGR, NAGGR * t))
                    for n in range(2):
                        inc(dve.bn_stats(stats[1][:, 2 * q + n, :], hv[:, n, :]), "st2")
                elif step == "x2t":
                    t, k = arg
                    wait(dve, "xhi_done", nth(pair, 6, 2 * t + k + 1))
                    inc(dve.tensor_tensor(x_lo[:, t, k, :], ch(step, arg)[:, 0:TT], x_hi[:, t, k, :].bitcast(F32),
                                          ALU.subtract), "xlo_done")
                elif step == "route_scores":
                    base = ROUTE["scores"]
                    wait(dve, "score_exp", nth(pair, 3, arg + 1))
                    routed(dve.tensor_scalar(sc[:], sc[:], 1.0, None, ALU.add), pair, arg, base + 1)
                    routed(dve.reciprocal(sc[:], sc[:]), pair, arg, base + 2)
                    routed(dve.tensor_tensor(sbias[:, :].rearrange("p (j e) -> p j e", e=E),
                                             sc[:, :].rearrange("p (j e) -> p j e", e=E),
                                             corr_bc[:, :].unsqueeze(1).broadcast_to([TP, SUB, E]), ALU.add),
                           pair, arg, base + 3)
                    s4 = sbias[:, :].rearrange("p (g e) -> p g e", e=EG)
                    n0 = 0
                    for d in range(1, EG):
                        inc(dve.tensor_tensor(pairs6[:, :, n0:n0 + EG - d], s4[:, :, 0:EG - d], s4[:, :, d:EG],
                                              ALU.add), "route")
                        n0 += EG - d
                    wait(dve, "route", nth(pair, 3 * NROUTE, NROUTE * arg + base + 6))
                    routed(dve.tensor_reduce(gs[:, :, :].rearrange("p j g -> p (j g)"), pairs6[:], AX.X, ALU.max),
                           pair, arg, base + 7)
                    inc(dve.tensor_tensor(ge1[:, :, 0:3], gs[:, :, 0:3], gs[:, :, 1:4], ALU.is_ge), "route")
                    inc(dve.tensor_tensor(ge2[:], gs[:, :, 0:2], gs[:, :, 2:4], ALU.is_ge), "route")
                    inc(dve.tensor_tensor(ge3[:], gs[:, :, 0:1], gs[:, :, 3:4], ALU.is_ge), "route")
                elif step == "route_groups":
                    base = ROUTE["groups"]
                    wait(dve, "route", nth(pair, 3 * NROUTE, NROUTE * arg + base))
                    steps = ((slice(0, 4), winit[:], ge1[:], ALU.add),
                             (slice(1, 4), None, ge1[:, :, 0:3], ALU.subtract), (slice(0, 2), None, ge2[:], ALU.add),
                             (slice(2, 4), None, ge2[:], ALU.subtract), (slice(0, 1), None, ge3[:], ALU.add),
                             (slice(3, 4), None, ge3[:], ALU.subtract))
                    for n, (s, a, b, op) in enumerate(steps):
                        routed(dve.tensor_tensor(wins[:, :, s], wins[:, :, s] if a is None else a, b, op),
                               pair, arg, base + n + 1)
                    routed(dve.tensor_scalar(gmask[:], wins[:, :, :].rearrange("p j g -> p (j g)"), 2.0, None,
                                             ALU.is_ge), pair, arg, base + 7)
                    routed(dve.tensor_scalar(gpen[:], gmask[:], 1.0, BIG, ALU.subtract, ALU.mult),
                           pair, arg, base + 8)
                elif step == "route_pick":
                    base = ROUTE["pick"]
                    gm = gmask[:, :].unsqueeze(2).broadcast_to([TP, SUB * NG, EG])
                    gp = gpen[:, :].unsqueeze(2).broadcast_to([TP, SUB * NG, EG])
                    m4 = masked[:, :].rearrange("p (g e) -> p g e", e=EG)
                    s4 = sbias[:, :].rearrange("p (g e) -> p g e", e=EG)
                    routed(dve.tensor_tensor(m4, s4, gm, ALU.mult), pair, arg, base + 1)
                    routed(dve.tensor_tensor(m4, m4, gp, ALU.add), pair, arg, base + 2)
                    inc(dve.memset(marks[:, :, 4:8], -BIG), "route")
                    for j in range(SUB):
                        last = dve.max(top8[:, j, :], masked[:, j * E:(j + 1) * E])
                    routed(last, pair, arg, base + 4)
                    routed(dve.tensor_copy(marks[:, :, 0:4], top8[:, :, 0:4]), pair, arg, base + 5)
                    inc(dve.tensor_tensor(gscore.rearrange("p (g e) -> p g e", e=EG),
                                          sc[:, :].rearrange("p (g e) -> p g e", e=EG), gm, ALU.mult), "route")
                    for j in range(SUB):
                        last = dve.match_replace(marked[:, j * E:(j + 1) * E], marks[:, j, :],
                                                 masked[:, j * E:(j + 1) * E], BIG)
                    routed(last, pair, arg, base + 7)
                    wait(dve, "comb_mm", nth(pair, 3, arg))
                    inc(dve.scalar_tensor_tensor(wsel[:], marked[:], BIG, gscore, ALU.is_equal, ALU.mult),
                        "route")
                elif step == "route_weights":
                    base = ROUTE["weights"]
                    w3 = wsel[:, :].rearrange("p (j e) -> p j e", e=E)
                    wait(dve, "route", nth(pair, 3 * NROUTE, NROUTE * arg + base))
                    routed(dve.tensor_reduce(wsum[:], w3, AX.X, ALU.add), pair, arg, base + 1)
                    routed(dve.tensor_scalar(wsum[:], wsum[:], 1e-20, None, ALU.add), pair, arg, base + 2)
                    routed(dve.reciprocal(wsum[:], wsum[:]), pair, arg, base + 3)
                    inc(dve.tensor_tensor(w3, w3, wsum[:, :].unsqueeze(2).broadcast_to([TP, SUB, E]), ALU.mult),
                        "route")

            def ffn(pair, idx):
                t, m = divmod(idx, M)
                if m >= MS:
                    r = m - MS
                    wait(dve, f"cb{r % RING}", nth(pair, 32 * NT * MR // RING,
                                                   32 * ((t * MR + r) // RING + 1)))
                    wait(dve, "silu_done", nth(pair, SLOTS, idx + 1))
                    inc(dve.tensor_tensor(sg[:, idx % 2, :], sg[:, idx % 2, :], cb[:, r % RING, :], ALU.mult), "t_done")
                    wait(dve, "t_done", nth(pair, NT * MR, t * MR + m - MS + 1))
                else:
                    wait(dve, "silu_done", nth(pair, SLOTS, idx + 1))
                wait(dve, "up_mm", nth(pair, SLOTS, idx + 1))
                wait(dve, "lo_done", nth(pair, SLOTS, idx - 1))
                inc(dve.tensor_tensor(hid[:, idx % 2, :], sg[:, idx % 2, :], u_ps[:, idx % 2, 0:TT], ALU.mult),
                    "hid_done")

            def finish(pair, t):
                wait(dve, "down_mm", nth(pair, SLOTS, M * (t + 1)))
                for q in range(2):
                    hv = h2[:, t * SUB + 2 * q:t * SUB + 2 * q + 2, :]
                    inc(dve.tensor_tensor(hv, d_ps[0:TP, 2 * q:2 * q + 2, :], hv, ALU.add), "fin_done")

            def iteration(pair, have_next, first=False):
                for idx in range(SLOTS):
                    for half in (0.0, 0.5):
                        for step, arg, of in chain_at(idx + half, pair, have_next):
                            chain(step, arg, of)
                    ffn(pair, idx)
                    if idx % M == 1 and idx > M:
                        finish(pair, idx // M - 1)
                    elif idx == 1 and not first:
                        finish(pair - 1, NT - 1)

            for at in sorted({*CHAIN, *PREPARE}):
                for what, n in PREPARE.get(at, ()):
                    prepare(what, n)
                for step, arg, of in chain_at(at, -1, True, have_this=False):
                    chain(step, arg, of)
            iteration(0, True, first=True)
            with dve.Fori(1, NP - 1) as i:
                iteration(i, True)
            iteration(NP - 1, False)
            finish(NP - 1, NT - 1)

        @block.tensor
        def _(pe):
            pe.wait_ge(S["ident_done"], 2)

            def prepare(what, n):
                if what == "fold":
                    bank = fold_ps[n]
                    if n == 0:
                        pe.wait_ge(S["w_tok"], 32)
                        for k in range(KD):
                            last = pe.transpose(bank[:, k * P:(k + 1) * P], wraw[:, k, :], ident[:])
                    elif n == 1:
                        pe.wait_ge(S["w_fold"], 16 * W_FOLD)
                        for o in range(2):
                            for k in range(KD):
                                last = pe.transpose(bank[:, (2 * o + k) * P:(2 * o + k + 1) * P],
                                                    wos[:, o, k * P:(k + 1) * P], ident[:])
                    elif n == 2:
                        pe.wait_ge(S["fold_ev"], 2)
                        for o in range(2):
                            for k in range(KD):
                                last = pe.matmul(bank[:, o * P:(o + 1) * P], wosT[:, o, k, :], wdi1[:, k, :],
                                                 start=(k == 0), stop=(k == KD - 1))
                    elif n == 3:
                        pe.wait_ge(S["fold_ev"], 4)
                        for s in range(2):
                            for k in range(KD):
                                last = pe.matmul(bank[:, s:s + 1], wdup[:, s, k, :], bsum[:, k:k + 1],
                                                 start=(k == 0), stop=(k == KD - 1))
                    else:
                        for k in range(KD):
                            last = pe.transpose(bank[:, k * E:(k + 1) * E], rraw[:, k * P:(k + 1) * P],
                                                ident[0:E, 0:E])
                    inc(last, "fold_mm")
                elif what == "shared":
                    pe.wait_ge(S["fold_ev"], 7)
                    pe.wait_ge(S[f"w_shared{n // KD % 2}"], 16 * (n // (2 * KD) + 1))
                    raw, k = sh_raw[n // KD], n % KD
                    for m in range(MS):
                        a = (raw.rearrange("p (m c) -> p m c", m=MS)[:, m, k * P:(k + 1) * P] if n < 2 * KD
                             else raw.rearrange("p (k n) -> p k n", k=KD)[:, k, m * P:(m + 1) * P])
                        last = pe.transpose(shared_ps[n][:, m * P:(m + 1) * P], a, ident[:])
                    inc(last, "shared_mm")

            def chain(step, arg, pair):
                if step not in PE_STEPS:
                    return
                bank, ch_ps = bank_of[step, arg], ch(step, arg)
                if last_in[bank] is not None:
                    for name, value in reads_of(*last_in[bank]):
                        wait(pe, name, value)
                last_in[bank] = (step, arg, pair)
                if step == "tok":
                    if arg % 3 == 0:
                        wait(pe, "ew_done", nth(pair, 2, arg // 3 + 1))
                    for n in range(2):
                        b, c0 = cols(2 * arg + n)
                        last = pe.matmul(ch_ps[0:TP, n * D:(n + 1) * D], ew[:, b, c0:c0 + TP], tokwT[:],
                                         start=True, stop=True)
                    inc(last, "tok_mm")
                elif step in ("x1t", "x2t"):
                    t, k = arg
                    src = xn1 if step == "x1t" else xn2
                    wait(pe, f"xn{step[1]}", nth(pair, 3, t + 1))
                    for j in range(SUB):
                        last = pe.transpose(ch_ps[:, j * TP:(j + 1) * TP], src[:, j, k * P:(k + 1) * P],
                                            ident[0:TP, 0:TP])
                    inc(last, f"{step}_mm")
                elif step == "pre":
                    layer, s = arg
                    if layer == 0:
                        wait(pe, "x1t_ev", nth(pair, 6, 2 * s + 2))
                    else:
                        wait(pe, "ssm_done", nth(pair, 2, 1))
                    for b, c0, n, at in pieces(s):
                        if layer == 0:
                            for k in range(KD):
                                last = pe.matmul(ch_ps[:, at:at + n], wdi0[:, b, k, :], x1T[:, k, at:at + n],
                                                 start=(k == 0), stop=(k == KD - 1))
                        else:
                            last = pe.matmul(ch_ps[:, at:at + n], g1[:, b, :], t1[:, c0:c0 + n],
                                             start=True, stop=True)
                    inc(last, "pre_mm")
                elif step == "carry":
                    wait(pe, "ssm_done", nth(pair, 2, 1))
                    for s in range(2):
                        last = pe.matmul(ch_ps[:, s:s + 1], sbd[:, s, :], t1[:, T - 1:T], start=True, stop=True)
                    inc(last, "carry_mm")
                elif step == "class_row":
                    wait(pe, "ssm_done", nth(pair, 2, 2))
                    for b in range(2):
                        last = pe.matmul(ch_ps[0:TP, b * D:(b + 1) * D],
                                         hs1[:, T - 1:T].broadcast_to([P, TP]), ws1[:, b, :],
                                         start=True, stop=True)
                    inc(last, "row_mm")
                elif step == "y":
                    t, q = arg
                    wait(pe, "ssm_done", nth(pair, 2, 2))
                    for n in range(2):
                        b, c0 = cols(t * SUB + 2 * q + n)
                        last = pe.matmul(ch_ps[0:TP, n * D:(n + 1) * D], hs1[:, c0:c0 + TP], wo1[:, b, :],
                                         start=True, stop=True)
                    inc(last, "y_mm")
                elif step == "logit":
                    wait(pe, "xlo_done", nth(pair, 6, 2 * arg + 2))
                    parts = [(w, xx, k) for k in range(KD) for w, xx in ((rw_hi, x_hi), (rw_lo, x_hi), (rw_hi, x_lo))]
                    for n, (w, xx, k) in enumerate(parts):
                        last = pe.matmul(ch_ps[0:E, 0:TT], w[:, k, :], xx[:, arg, k, :], start=(n == 0),
                                         stop=(n == len(parts) - 1))
                    inc(last, "logit_mm")
                elif step == "logit_t":
                    wait(pe, "logit_ev", nth(pair, 3, arg + 1))
                    for j in range(SUB):
                        last = pe.transpose(ch_ps[0:TP, j * P:(j + 1) * P], logT[:, j * TP:(j + 1) * TP], ident[:])
                    inc(last, "logt_mm")
                elif step == "comb_t":
                    wait(pe, "route", nth(pair, 3 * NROUTE, NROUTE * (arg + 1)))
                    for j in range(SUB):
                        last = pe.transpose(ch_ps[0:E, j * TP:(j + 1) * TP], wsel[:, j * E:(j + 1) * E],
                                            ident[0:TP, 0:TP])
                    inc(last, "comb_mm")

            def down(pair, idx):
                t, m = divmod(idx, M)
                wait(pe, "lo_done", nth(pair, SLOTS, idx + 1))
                if m == 0:
                    wait(pe, "fin_done", nth(pair, 2 * NT, 2 * t))
                hh, hl = hid_hi[:, idx % 3, :], hid_lo[:, idx % 3, :]
                for j in range(SUB):
                    tc = slice(j * TP, (j + 1) * TP)
                    for n, (a, w) in enumerate(((hh, down_hi), (hh, down_lo), (hl, down_hi))):
                        last = pe.matmul(d_ps[0:TP, j, :], a[:, tc], w[:, m, :],
                                         start=(m == 0 and n == 0 and j % 2 == 0),
                                         stop=(m == M - 1 and n == 2), skip_group_check=True)
                inc(last, "down_mm")

            def ffn(pair, idx, before):
                t, m = divmod(idx, M)

                def product(bank, hi_w, lo_w):
                    ms = slice(m * P, (m + 1) * P)
                    for k in range(KD):
                        for n, (w, xx) in enumerate(((hi_w, x_hi), (hi_w, x_lo), (lo_w, x_hi))):
                            last = pe.matmul(bank, w[:, k, ms], xx[:, t, k, :], start=(k == 0 and n == 0),
                                             stop=(k == KD - 1 and n == 2))
                    return last

                if m == 0:
                    wait(pe, "xlo_done", nth(pair, 6, 2 * t + 2))
                wait(pe, "silu_done", nth(pair, SLOTS, idx - 1))
                inc(product(g_ps[:, idx % 2, 0:TT], gate_hi, gate_lo), "gate_mm")
                for step, arg, of in before:
                    chain(step, arg, of)
                wait(pe, "hid_done", nth(pair, SLOTS, idx - 1))
                inc(product(u_ps[:, idx % 2, 0:TT], up_hi, up_lo), "up_mm")

            def iteration(pair, have_next, first=False):
                for idx in range(SLOTS):
                    for step, arg, of in chain_at(idx + 0.0, pair, have_next):
                        chain(step, arg, of)
                    ffn(pair, idx, list(chain_at(idx + 0.5, pair, have_next)))
                    if idx >= LAG:
                        down(pair, idx - LAG)
                    elif not first:
                        down(pair - 1, SLOTS + idx - LAG)

            for at in sorted({*CHAIN, *PREPARE}):
                for what, n in PREPARE.get(at, ()):
                    prepare(what, n)
                for step, arg, of in chain_at(at, -1, True, have_this=False):
                    chain(step, arg, of)
            iteration(0, True, first=True)
            with pe.Fori(1, NP - 1) as i:
                banks_at_loop(i)
                iteration(i, True)
            banks_at_loop(NP - 1)
            iteration(NP - 1, False)
            for n in range(LAG):
                down(NP - 1, SLOTS + n - LAG)


_INS = ["x", "L0_tok_W", "L0_tok_b", "L0_attn_Wd", "L0_attn_bd", "L0_attn_Wi", "L0_attn_bi", "L0_attn_A_log",
        "L0_attn_Wo", "L0_attn_bo", "L0_attn_Ws", "L0_attn_bs", "L0_ffn_router_w", "L0_ffn_correction_bias",
        "L0_ffn_gate_w", "L0_ffn_up_w", "L0_ffn_down_w", "L0_ffn_shared_gate_w", "L0_ffn_shared_up_w",
        "L0_ffn_shared_down_w"]


def kernel(**inputs):
    import numpy as _np
    import concourse.bacc as _bacc
    from concourse import mybir as _mybir
    from concourse.bass_utils import run_bass_kernel_spmd as _run

    nc = _bacc.Bacc("TRN2", target_bir_lowering=False, num_devices=1)
    arrays, args = {}, []
    for name in _INS:
        a = _np.ascontiguousarray(inputs[name])
        arrays[f"in_{name}_dram"] = a
        args.append(nc.dram_tensor(f"in_{name}_dram", a.shape, _mybir.dt.from_np(a.dtype), kind="ExternalInput").ap())
    shape = (inputs["x"].shape[0], inputs["x"].shape[2], inputs["L0_tok_W"].shape[0])
    args.append(nc.dram_tensor("out_0_dram", shape, _mybir.dt.float32, kind="ExternalOutput").ap())
    audio_tower_kernel(nc, *args)
    r = _run(nc, [arrays], core_ids=[0])
    return r.results[0]["out_0_dram"]
```

```python
from contextlib import ExitStack

import concourse.bass as bass
from concourse import mybir

F32 = mybir.dt.float32
F32R = mybir.dt.float32r
ALU = mybir.AluOpType
ACT = mybir.ActivationFunctionType
AX = mybir.AxisListType

CHAIN = {
    0.0: [(1, "ewma", 0), (0, "y", (1, 0))],
    1.0: [(0, "y", (1, 1))],
    2.5: [(1, "load", 1)],
    3.5: [(0, "ln2_stats", 1)],
    4.0: [(1, "ewma", 1), (1, "tok", 0), (1, "tok", 1)],
    4.5: [(1, "ln1_stats", 0)],
    5.0: [(0, "ln2_norm", 1)],
    5.5: [(0, "y", (2, 0)), (1, "tok", 2)],
    6.0: [(1, "spread", 0)],
    6.5: [(1, "tok", 3)],
    7.0: [(1, "ln1_stats", 1), (0, "y", (2, 1)), (0, "x2t", (1, 0))],
    8.0: [(0, "x2t", (1, 1)), (1, "tok", 4), (1, "spread", 1)],
    8.5: [(0, "logit", 1), (1, "tok", 5)],
    9.0: [(0, "logit_t", 1), (1, "ln1_stats", 2)],
    9.5: [(0, "route_scores", 1)],
    10.0: [(0, "route_groups", 1), (1, "spread", 2)],
    10.5: [(0, "route_pick", 1)],
    11.0: [(0, "route_weights", 1)],
    11.5: [(0, "comb_store", 1)],

    12.0: [(1, "pre", (0, 0)), (1, "pre", (0, 1))],
    13.0: [(1, "pre", (0, 2)), (0, "ln2_stats", 2)],
    13.5: [(1, "ssm_log", 0)],
    14.0: [(0, "ln2_norm", 2), (1, "ssm_decay", 0)],
    15.5: [(1, "ssm_scan", 0), (0, "x2t", (2, 0))],
    16.0: [(0, "x2t", (2, 1))],
    17.0: [(1, "split", (0, 0)), (1, "split", (0, 1))],
    17.5: [(1, "carry", 0), (0, "logit", 2)],
    18.0: [(1, "pre", (1, 0)), (1, "pre", (1, 1))],
    18.5: [(0, "logit_t", 2), (1, "pre", (1, 2)), (1, "ssm_log", 1)],
    19.0: [(0, "route_scores", 2)],
    20.5: [(0, "route_groups", 2)],
    21.5: [(0, "route_pick", 2)],
    22.0: [(1, "ssm_decay", 1)],
    22.5: [(0, "route_weights", 2)],
    23.0: [(0, "comb_store", 2)],
    23.5: [(1, "ssm_scan", 1)],

    24.0: [(1, "split", (1, 0))],
    24.5: [(1, "class_row", 0), (1, "residual", 0), (1, "split", (1, 1))],
    25.0: [(1, "residual", 1)],
    25.5: [(1, "y", (0, 0)), (1, "residual", 2)],
    26.0: [(1, "y", (0, 1)), (1, "residual", 3)],
    27.0: [(1, "ln2_stats", 0), (1, "residual", 4)],
    27.5: [(1, "residual", 5)],
    28.0: [(1, "ln2_norm", 0)],
    29.5: [(1, "x2t", (0, 0)), (1, "x2t", (0, 1))],
    30.0: [(1, "logit", 0)],
    30.5: [(1, "logit_t", 0)],
    31.0: [(1, "route_scores", 0)],
    32.0: [(1, "route_groups", 0), (1, "route_pick", 0)],
    33.0: [(1, "route_weights", 0)],
    34.0: [(1, "comb_store", 0)],
}

PREPARE = {
    0.0: [("tokw", 0)],
    1.0: [("tokw", 1)],
    4.2: [("tokw", 2)],
    5.0: [("small_loads", 0)],
    10.5: [("loads", 0)],
    13.0: [("softplus", 0)],
    13.2: [("fold", 1)],
    13.8: [("fold", 2), ("shared", 0)],
    14.2: [("fold", 3), ("fold", 4), ("routed", 0), ("routed", 1)],
    15.7: [("shared", 1)],
    17.2: [("routed", 2)],
    18.7: [("shared", 2), ("shared", 3), ("routed", 3)],
    22.2: [("shared", 4), ("routed", 4), ("routed", 5)],
    23.7: [("shared", 5)],
    25.5: [("staged", 0)],
}

DEFERRED = {
    0.5: [("logit", 0)],
    1.0: [("logit_t", 0)],
    1.5: [("route_scores", 0)],
    2.0: [("route_groups", 0)],
    2.5: [("route_pick", 0)],
    3.0: [("route_weights", 0), ("comb_store", 0)],
}


def audio_tower_kernel(nc, x, tok_w, tok_b, wd, bd, wi, bi, a_log, wo, bo, ws, bs, router_w, corr_bias,
                       gate_w, up_w, down_w, sh_gate_w, sh_up_w, sh_down_w, out):
    B, C, T = x.shape
    D = tok_w.shape[0]
    N = wd.shape[2]
    E, _, H = gate_w.shape
    HS = sh_gate_w.shape[0]
    P = 128
    NP = B // 2
    TT = 500
    NT = 2 * T // TT
    TP = 125
    SUB = TT // TP
    NJ = NT * SUB
    KD = D // P
    MS = HS // P
    MR = E * H // P
    M = MS + MR
    NG, EG = 4, E // 4
    SLOTS = NT * M
    ALPHA = 0.1
    EPS = 1e-5
    BIG = 3e38
    RING = 4
    LAG = 2
    W_IN, W_FOLD = 6 + 1, 4 + 2 + 4 + 4 + 1
    assert C == P and D == 2 * P and 2 * N == P and 2 * H == P and 2 * T == NT * TT and M == 12

    with ExitStack() as ctx:
        def sb(name, shape, dt=F32):
            return ctx.enter_context(nc.sbuf_tensor(name, shape, dt))

        def ps(name, shape):
            return ctx.enter_context(nc.psum_tensor(name, shape, F32))

        def sem(name):
            return ctx.enter_context(nc.semaphore(name))

        gate_hi, gate_lo = (sb(f"gate_{s}", [P, KD, M * P], F32R) for s in ("hi", "lo"))
        up_hi, up_lo = (sb(f"up_{s}", [P, KD, M * P], F32R) for s in ("hi", "lo"))
        down_hi, down_lo = (sb(f"down_{s}", [P, M, D], F32R) for s in ("hi", "lo"))
        stage = sb("stage", [P, 2 * NJ * D])
        h_tok = stage[0:TP, 0:NJ * D].rearrange("p (j d) -> p j d", d=D)
        h2 = stage[0:TP, NJ * D:2 * NJ * D].rearrange("p (j d) -> p j d", d=D)
        x_in = sb("x_in", [P, T])
        fw = sb("fw", [P, T])
        ew_hi = sb("ew_hi", [P, 2, T], F32R)
        ew_lo = sb("ew_lo", [P, 2, T], F32R)
        ends10 = sb("ends10", [P, 2, 2])
        xn2_rows = sb("xn2", [P, SUB, D])
        xn2 = xn2_rows[0:TP]
        x_hi = sb("x_hi", [P, NT, KD, TT], F32R)
        x_lo = sb("x_lo", [P, NT, KD, TT], F32R)
        zt = sb("zt", [P, T])
        ut = sb("ut", [P, T])
        t1 = sb("t1", [P, T])
        t2 = sb("t2", [P, T])
        rb01 = sb("rb01", [P, 2, TT])
        rb = [rb01[:, 0, :], rb01[:, 1, :], t2[:, 0:TT]]
        states = sb("states", [P, 2, T], F32R)
        blocks = sb("blocks", [P, 3, TT])
        sg, hid = blocks[:, 0:2, :], blocks[:, 2, :]
        hid_hi = sb("hid_hi", [P, 3, TT], F32R)
        hid_lo = sb("hid_lo", [P, 3, TT], F32R)
        cb = sb("cb", [P, RING, TT])
        rstd_dram = nc.dram_tensor("rstd_scratch", (NT, TT), F32, kind="Internal").ap()
        comb_dram = nc.dram_tensor("comb_scratch", (NT, E, TT), F32, kind="Internal").ap()
        ident = sb("ident", [P, P])
        tw_hi = sb("tw_hi", [P, D], F32R)
        tw_lo = sb("tw_lo", [P, D], F32R)
        f_hi = sb("f_hi", [P, P], F32R)
        f_lo = sb("f_lo", [P, P], F32R)
        cb0 = sb("cb0", [P, 1])
        g_hi = sb("g_hi", [P, P], F32R)
        g_lo = sb("g_lo", [P, P], F32R)
        sbd = sb("sbd", [P, 2, P])
        wo_hi = sb("wo_hi", [P, D], F32R)
        wo_lo = sb("wo_lo", [P, D], F32R)
        ws1 = sb("ws1", [P, 2, D])
        tokb_bc = sb("tokb_bc", [TP, D])
        brow = sb("brow", [TP, D])
        rows = sb("rows", [TP, 2, D])
        LO = 2 * E
        rw = sb("rw", [P, KD, LO + E], F32R)
        corr_bc = sb("corr_bc", [TP, E])
        vecs = sb("vecs", [P, 6])
        nspa = sb("nspa", [P, 2])
        spt = sb("spt", [P, 4])
        bias1 = sb("bias1", [P, 2])
        bias1s = sb("bias1s", [P, 2])
        c09 = sb("c09", [P, 1])
        mhalf = sb("mhalf", [TP, SUB])
        stats = [sb(f"stats{n}", [TP, SUB, 6]) for n in (1, 2)]
        halves = [sb(f"halves{n}", [TP, SUB, 2]) for n in (1, 2)]
        mv = [sb(f"mv{n}", [TP, SUB, 2]) for n in (1, 2)]
        rstd = [sb(f"rstd{n}", [TP, SUB]) for n in (1, 2)]
        logT = sb("logT", [P, TT])
        sc = sb("sc", [TP, SUB * E])
        sbias = sb("sbias", [TP, SUB * E])
        pairs6 = sb("pairs6", [TP, SUB * NG, 6])
        gs = sb("gs", [TP, SUB, NG])
        ge1 = sb("ge1", [TP, SUB, NG])
        ge2 = sb("ge2", [TP, SUB, 2])
        ge3 = sb("ge3", [TP, SUB, 1])
        winit = sb("winit", [TP, SUB, NG])
        wins = sb("wins", [TP, SUB, NG])
        gmask = sb("gmask", [TP, SUB * NG])
        gpen = sb("gpen", [TP, SUB * NG])
        masked = sbias
        top8 = sb("top8", [TP, SUB, 8])
        marks = sb("marks", [TP, SUB, 8])
        gscore = pairs6[:, :, :].rearrange("p g n -> p (g n)")[:, 0:SUB * E]
        marked = sb("marked", [TP, SUB * E])
        wpad = sb("wpad", [P, SUB, 32])
        wsel = wpad[0:TP, :, 0:E]
        wT = sb("wT", [P, SUB, 32])
        wsum = sb("wsum", [TP, SUB])
        wraw = zt[:, 0:2 * P].rearrange("p (k c) -> p k c", k=KD)
        ones = zt[:, 2 * P:3 * P]
        wdi0 = ut[:, 0:2 * P].rearrange("p (k n) -> p k n", k=KD)
        xn_flat = xn2_rows[:, :, :].rearrange("p j d -> p (j d)")
        wo_raw = xn_flat[:, D:2 * D]
        spare = cb[:, :, :].rearrange("p a n -> p (a n)")[:, MS * D:]
        wos = xn_flat[:, 2 * D:4 * D].rearrange("p (o d) -> p o d", o=2)
        wdi1 = xn_flat[:, 0:D].rearrange("p (k n) -> p k n", k=KD)
        wosT = spare[:, 0:4 * P].rearrange("p (o k n) -> p o k n", o=2, k=KD)
        rraw = spare[0:E, 4 * P:4 * P + D]
        tokb_col = sb("tokb_col", [P, KD])
        bcol = sb("bcol", [P, KD, 2])
        bsum = sb("bsum", [P, KD])
        CH = E * H
        chunk = [stage[:, (NJ * D) + n * CH:(NJ * D) + (n + 1) * CH] for n in range(NT)]
        routed_parts = []
        for hi_t, lo_t in ((gate_hi, gate_lo), (up_hi, up_lo)):
            routed_parts += [(hi_t[:, k, HS:], lo_t[:, k, HS:]) for k in range(KD)]
        for m0 in (MS, MS + MR // 2):
            routed_parts.append(tuple(w[:, m0:m0 + MR // 2, :].rearrange("p m d -> p (m d)")
                                      for w in (down_hi, down_lo)))
        sh_a = blocks[:, :, :].rearrange("p a n -> p (a n)")[:, 0:MS * D]
        sh_b = cb[:, :, :].rearrange("p a n -> p (a n)")[:, 0:MS * D]
        sh_raw = [sh_a, sh_b, sh_a]

        g_ps = ps("g_ps", [P, 2, 512])
        u_ps = ps("u_ps", [P, 2, 512])
        ch_ps = ps("ch_ps", [P, 2, 512])
        d_ps = ps("d_ps", [P, SUB, D])
        fold_ps = [g_ps[:, 0, :], g_ps[:, 1, :], u_ps[:, 0, :], u_ps[:, 1, :],
                   d_ps[:, 0:2, :].rearrange("p j d -> p (j d)")]
        shared_ps = fold_ps + [d_ps[:, 2:4, :].rearrange("p j d -> p (j d)")]

        S = {name: sem(name) for name in (
            "x_in0", "x_in1", "zeroed", "zeroed_rw", "ones_done", "w_tok", "w_pre", "w_in", "w_fold", "w_routed0",
            "w_routed1", "w_routed2", "w_shared0", "w_shared1", "ident_done", "const_done", "fold_mm", "fold_ev",
            "wo_hi_done", "g_hi_done", "rw_hi_done", "spa", "spa_dve", "routed_hi", "routed_lo", "shared_mm",
            "shared_hi", "shared_lo", "ends_done", "scan_done", "ew_done", "ew_hi_done", "ew_lo_done", "tw_hi_done",
            "f_hi_done", "tok_mm", "tok_ev", "st1", "aggr1", "rstd1", "rstd_st", "rb0", "rb1", "rb2", "pre_mm",
            "z_ev", "u_ev", "abs_done", "relu_done", "exp_done", "ln_done", "delta_done", "decay_done",
            "drive_done", "ssm_done", "st_hi", "st_lo", "carry_mm", "carry_ev", "row_mm", "row_ev", "res_done",
            "y_mm", "y_ev", "st2", "aggr2", "rstd2", "xn2", "x2t_mm", "xhi_done", "xlo_done", "logit_mm",
            "logit_ev", "logt_mm", "logit_half", "logit_sum", "score_exp", "route", "comb_tr", "comb_st", "cb0",
            "cb1", "cb2", "cb3", "gate_mm", "up_mm", "down_mm", "silu_done", "t_done", "hid_done", "hi_done",
            "lo_done", "fin_done", "out0", "out1", "out2")}
        OUT = [S["out0"], S["out1"], S["out2"]]

        def nth(pair, per_pair, n):
            return pair * per_pair + n

        def wait(eng, name, value):
            if not (isinstance(value, int) and value <= 0):
                eng.wait_ge(S[name], value)

        def inc(ins, name):
            return ins.then_inc(S[name], 1)

        ZU = [1, 3, 4]
        ROUTE = {"scores": 0, "groups": 10, "pick": 18, "weights": 26}
        NROUTE = 30
        NAGGR = 7

        def reads_of(step, arg, pair):
            if step == "tok":
                return [("tok_ev", nth(pair, 6, arg + 1))]
            if step == "pre":
                v = nth(pair, 8, 4 * arg[0] + ZU[arg[1]])
                return [("z_ev", v), ("u_ev", v)]
            if step == "carry":
                return [("carry_ev", nth(pair, 1, 1))]
            if step == "class_row":
                return [("row_ev", nth(pair, 1, 1))]
            if step == "y":
                return [("y_ev", nth(pair, 6, 2 * arg[0] + arg[1] + 1))]
            if step == "x2t":
                return [("xlo_done", nth(pair, 6, 2 * arg[0] + arg[1] + 1))]
            if step == "logit":
                return [("logit_ev", nth(pair, 3, arg + 1))]
            if step == "logit_t":
                return [("logit_sum", nth(pair, 3, arg + 1))]
            return None

        PE_STEPS = ("tok", "pre", "carry", "class_row", "y", "x2t", "logit", "logit_t")
        in_order = [(which, step, arg) for at in sorted(CHAIN) for which, step, arg in CHAIN[at] if step in PE_STEPS]
        bank_of = {(step, arg): n % 2 for n, (_, step, arg) in enumerate(in_order)}
        last_in = [None, None]

        first_bank = {(step, arg): n % 2 for n, (step, arg) in
                      enumerate((step, arg) for which, step, arg in in_order if which == 1)}

        def bank(step, arg, pair):
            alone = is_first(pair) and (step, arg) in first_bank
            return (first_bank if alone else bank_of)[step, arg]

        def ch(step, arg, pair):
            return ch_ps[:, bank(step, arg, pair), :]

        def banks_at_loop(pair):
            for which, step, arg in in_order:
                last_in[bank_of[step, arg]] = (step, arg, pair + which - 1)

        deferred = [s for at in DEFERRED for s in DEFERRED[at]]

        def chain_at(at, pair, have_next, have_this=True):
            if is_first(pair):
                for step, arg in DEFERRED.get(at, ()):
                    yield step, arg, 0
            for which, step, arg in CHAIN.get(at, ()):
                if not have_this and (step, arg) in deferred:
                    continue
                if which == 1 and have_next:
                    yield step, arg, pair + 1
                if which == 0 and have_this:
                    yield step, arg, pair

        def shared_part(n):
            if n < 2 * KD:
                pair_ = ((gate_hi, gate_lo), (up_hi, up_lo))[n // KD]
                return [w[:, n % KD, 0:HS].rearrange("p (m c) -> p m c", m=MS) for w in pair_]
            return [w[:, 0:MS, (n % KD) * P:(n % KD + 1) * P] for w in (down_hi, down_lo)]

        def shared_view(n):
            return shared_ps[n].rearrange("p (m c) -> p m c", m=MS)

        def is_first(pair):
            return isinstance(pair, int) and pair == 0

        def scans_of(pair, b):
            return (t2[:], t1[:]) if is_first(pair) and b == 1 else (x_in[:], fw[:])

        def pieces(s):
            got = []
            for b in range(2):
                lo, hi = max(s * TT, b * T), min((s + 1) * TT, (b + 1) * T)
                if lo < hi:
                    got.append((b, lo - b * T, hi - lo, lo - s * TT))
            return got

        def cols(j):
            return j // (NJ // 2), (j % (NJ // 2)) * TP

        block = ctx.enter_context(nc.Block())

        x_v = x.rearrange("(q b) c t -> q c b t", b=2)
        out_v = out.rearrange("(q b) t d -> q (b t) d", b=2).rearrange("q (t j p) d -> q t p j d", t=NT, p=TP)

        @block.sync
        def _(sp):
            sp.dma_start(wraw, tok_w.rearrange("(k p) c -> p k c", p=P)).then_inc(S["w_tok"], 16)
            for b in range(2):
                sp.dma_start(scans_of(0, b)[0], x_v[0][:, b, :]).then_inc(S[f"x_in{b}"], 16)
            for o, a in enumerate((wd, wi)):
                sp.dma_start(wdi0[:, :, o * N:(o + 1) * N],
                             a[0].rearrange("(k p) n -> p k n", p=P)).then_inc(S["w_pre"], 16)
            for half in range(2):
                sp.dma_start(wo_raw[half * N:(half + 1) * N, :], wo[1]).then_inc(S["w_fold"], 16)
            for o, (a, b) in enumerate(((wo, ws), (ws, wo))):
                sp.dma_start(wos[0:N, o, :], a[0]).then_inc(S["w_fold"], 16)
                sp.dma_start(wos[N:P, o, :], b[0]).then_inc(S["w_fold"], 16)
            for o, a in enumerate((wd, wi)):
                sp.dma_start(wdi1[:, :, o * N:(o + 1) * N],
                             a[1].rearrange("(k p) n -> p k n", p=P)).then_inc(S["w_fold"], 16)
            sp.wait_ge(S["zeroed"], 1)
            for b in range(2):
                sp.dma_start(ws1[b * N:(b + 1) * N, b, :], ws[1]).then_inc(S["w_fold"], 16)

            def routed_chunk(n):
                sm = S[f"w_routed{n % NT}"]
                if n >= NT:
                    sp.wait_ge(S["routed_lo"], n - NT + 1)
                if n < 2 * KD:
                    src, k = (gate_w, up_w)[n // KD], n % KD
                    sp.dma_start(chunk[n % NT].rearrange("p (e h) -> p e h", e=E),
                                 src[:, k * P:(k + 1) * P, :].rearrange("e p h -> p e h")).then_inc(sm, 16)
                else:
                    m0 = (n - 2 * KD) * MR // 2
                    rows_ = down_w.rearrange("e h d -> (e h) d").rearrange("(m p) d -> p m d", p=P)
                    sp.dma_start(chunk[n % NT].rearrange("p (m d) -> p m d", d=D),
                                 rows_[:, m0:m0 + MR // 2, :]).then_inc(sm, 16)

            def prepare(what, n):
                if what == "loads":
                    for n, w in enumerate((sh_gate_w, sh_up_w)):
                        sp.dma_start(sh_raw[n].rearrange("p (m c) -> p m c", m=MS),
                                     w.rearrange("(m p) c -> p m c", p=P)).then_inc(S[f"w_shared{n}"], 16)
                    for n in range(NT):
                        routed_chunk(n)
                elif what == "routed" and 1 <= n <= NT:
                    routed_chunk(n - 1 + NT)
                elif what == "shared" and n == KD:
                    sp.wait_ge(S["shared_mm"], KD)
                    sp.dma_start(sh_raw[2].rearrange("p (k n) -> p k n", k=KD),
                                 sh_down_w.rearrange("(k p) n -> p k n", p=P)).then_inc(S["w_shared0"], 16)

            def load_x(pair, b):
                wait(sp, "ew_done", nth(pair, 2, b))
                sp.dma_start(x_in[:], x_v[pair][:, b, :]).then_inc(S[f"x_in{b}"], 16)

            def store(pair, t):
                wait(sp, "fin_done", nth(pair, 2 * NT, 2 * t + 2))
                sp.dma_start(out_v[pair, t], h2[:, t * SUB:(t + 1) * SUB, :]).then_inc(OUT[t], 16)

            def spread(s, pair):
                wait(sp, "rstd1", nth(pair, NT, s + 1))
                sp.dma_start(rstd_dram[s].rearrange("(j p) -> p j", p=TP), rstd[0][:],
                             allow_slow_non_contiguous=True).then_inc(S["rstd_st"], 16)
                wait(sp, "rstd_st", nth(pair, 16 * NT, 16 * (s + 1)))
                sp.dma_start(rb[s], rstd_dram[s].partition_broadcast(P)).then_inc(S[f"rb{s}"], 16)

            def store_comb(t, pair):
                wait(sp, "comb_tr", nth(pair, NT, t + 1))
                for q in range(4):
                    n = min(32, TP - 32 * q)
                    sp.dma_start(comb_dram[t].rearrange("e (j p) -> e j p", p=TP)[:, :, 32 * q:32 * q + n],
                                 wT[32 * q:32 * q + E, :, 0:n]).then_inc(S["comb_st"], 16)

            def chain(step, arg, pair):
                if step == "comb_store":
                    store_comb(arg, pair)
                elif step == "spread":
                    spread(arg, pair)
                elif step == "load" and not is_first(pair):
                    load_x(pair, arg)

            def load_comb(pair, t, m):
                if m == 0:
                    wait(sp, "comb_st", nth(pair, 64 * NT, 64 * (t + 1)))
                else:
                    wait(sp, "t_done", nth(pair, NT * MR, t * MR + m - RING + 1))
                for a in range(2):
                    sp.dma_start(cb[a * H:(a + 1) * H, m % RING, :],
                                 comb_dram[t, 2 * m + a].partition_broadcast(H)).then_inc(S[f"cb{m % RING}"], 16)

            def iteration(pair, have_next, first=False):
                if have_next:
                    load_x(pair + 1, 0)
                for idx in range(SLOTS):
                    t, m = divmod(idx, M)
                    if first and idx == RING:
                        for ahead in range(RING):
                            load_comb(pair, t, ahead)
                    if m < MR and not (first and idx < RING):
                        load_comb(pair, t, m)
                    if m == 2 and idx > M:
                        store(pair, t - 1)
                    elif m == 2 and not first:
                        store(pair - 1, NT - 1)
                    for half in (0.0, 0.5):
                        for step, arg, of in chain_at(idx + half, pair, have_next):
                            chain(step, arg, of)

            for at in sorted({*CHAIN, *PREPARE}):
                for what, n in PREPARE.get(at, ()):
                    prepare(what, n)
                for step, arg, of in chain_at(at, -1, True, have_this=False):
                    chain(step, arg, of)
            iteration(0, True, first=True)
            with sp.Fori(1, NP - 1) as i:
                iteration(i, True)
            iteration(NP - 1, False)
            store(NP - 1, NT - 1)
            for t in range(NT):
                sp.wait_ge(OUT[t], 16 * NP)

        @block.gpsimd
        def _(pool):
            pool.memset(ident[:], 0.0).then_inc(S["ident_done"], 1)
            pool.wait_ge(S["ident_done"], 1)
            pool.affine_select(out=ident[:], in_=ident[:], compare_op=ALU.not_equal, fill=1.0, base=0,
                               pattern=[[-1, P]], channel_multiplier=1).then_inc(S["ident_done"], 1)

            def prepare(what, n):
                if what == "routed":
                    hi_p, lo_p = routed_parts[n]
                    pool.wait_ge(S["routed_hi"], n + 1)
                    inc(pool.tensor_tensor(lo_p, chunk[n % NT], hi_p.bitcast(F32), ALU.subtract), "routed_lo")

            def chain(step, arg, pair):
                if step == "ewma":
                    x_b, fw_b = scans_of(pair, arg)
                    if not is_first(pair):
                        wait(pool, "scan_done", nth(pair, 4, 2 * arg + 2))
                        inc(pool.tensor_tensor(fw_b, fw_b, x_b, ALU.add), "ew_done")
                    wait(pool, "ew_hi_done", nth(pair, 2, arg + 1))
                    inc(pool.tensor_tensor(ew_lo[:, arg, :], fw_b, ew_hi[:, arg, :].bitcast(F32), ALU.subtract),
                        "ew_lo_done")
                elif step in ("ln1_stats", "ln2_stats"):
                    n = int(step[2]) - 1
                    wait(pool, f"aggr{n + 1}", nth(pair, NT * NAGGR, NAGGR * (arg + 1)))
                    if n == 0:
                        wait(pool, "rstd_st", nth(pair, 16 * NT, 16 * arg))
                    else:
                        wait(pool, "xn2", nth(pair, 3, arg))
                    inc(pool.tensor_tensor(rstd[n][:], mv[n][:, :, 1], mhalf[:], ALU.pow), f"rstd{n + 1}")
                elif step == "residual":
                    wait(pool, "row_ev", nth(pair, 1, 1))
                    hv = h_tok[:, 2 * arg:2 * arg + 2, :]
                    row = rows[:, arg // 3, :].unsqueeze(1).broadcast_to([TP, 2, D])
                    inc(pool.tensor_tensor(hv, hv, row, ALU.add), "res_done")

            def ffn(pair, idx):
                wait(pool, "hi_done", nth(pair, SLOTS, idx + 1))
                wait(pool, "down_mm", nth(pair, SLOTS, idx - 2))
                inc(pool.tensor_tensor(hid_lo[:, idx % 3, :], hid,
                                       hid_hi[:, idx % 3, :].bitcast(F32), ALU.subtract), "lo_done")

            def iteration(pair, have_next):
                for idx in range(SLOTS):
                    for half in (0.0, 0.5):
                        for step, arg, of in chain_at(idx + half, pair, have_next):
                            chain(step, arg, of)
                    ffn(pair, idx)

            inc(pool.memset(rw[:].bitcast(F32), 0.0), "zeroed_rw")
            pool.wait_ge(S["const_done"], 2)
            for at in sorted({*CHAIN, *PREPARE}):
                for what, n in PREPARE.get(at, ()):
                    prepare(what, n)
                for step, arg, of in chain_at(at, -1, True, have_this=False):
                    chain(step, arg, of)
            iteration(0, True)
            with pool.Fori(1, NP - 1) as i:
                iteration(i, True)
            iteration(NP - 1, False)

        @block.scalar
        def _(act):
            act.dma_start(tokb_bc[:], tok_b.partition_broadcast(TP)).then_inc(S["w_tok"], 16)
            act.dma_start(tokb_col[:, :].unsqueeze(2), tok_b.rearrange("(k p a) -> p k a", p=P, a=1),
                          allow_slow_non_contiguous=True).then_inc(S["w_pre"], 16)

            def prepare(what, n):
                if what == "small_loads":
                    for half in (vecs[0:N, :], vecs[N:P, :]):
                        for n, a in enumerate((bd, bi, a_log)):
                            act.dma_start(half[:, 2 * n:2 * n + 2], a.rearrange("l n -> n l"),
                                          allow_slow_non_contiguous=True).then_inc(S["w_in"], 16)
                    act.dma_start(corr_bc[:], corr_bias.partition_broadcast(TP)).then_inc(S["w_in"], 16)
                    for n, (a, dst) in enumerate(((bo, brow[:]), (bs, rows[:, 0, :]))):
                        act.dma_start(bcol[:, :, n:n + 1], a[0].rearrange("(k p a) -> p k a", p=P, a=1),
                                      allow_slow_non_contiguous=True).then_inc(S["w_fold"], 16)
                        act.dma_start(dst, a[1].partition_broadcast(TP)).then_inc(S["w_fold"], 16)
                    act.dma_start(rraw, router_w[:, :]).then_inc(S["w_fold"], 16)
                elif what == "softplus":
                    act.wait_ge(S["w_in"], 16 * W_IN)
                    inc(act.activation(spt[:, 0:2], vecs[:, 4:6], ACT.Abs), "spa")
                    act.wait_ge(S["spa"], 1)
                    inc(act.activation(spt[:, 2:4], spt[:, 0:2], ACT.Exp, scale=-1.0), "spa")
                    act.wait_ge(S["spa"], 2)
                    inc(act.activation(spt[:, 0:2], spt[:, 2:4], ACT.Ln, bias=1.0), "spa")
                elif what == "routed":
                    act.wait_ge(S[f"w_routed{n % NT}"], 16 * (n // NT + 1))
                    inc(act.activation(routed_parts[n][0], chunk[n % NT], ACT.Copy), "routed_hi")

            def chain(step, arg, pair):
                if step == "ewma":
                    wait(act, "ew_done", nth(pair, 2, arg + 1))
                    wait(act, "tok_mm", nth(pair - 1, 6, 3 * (arg + 1)))
                    wait(act, "pre_mm", nth(pair - 1, 6, 3))
                    inc(act.activation(ew_hi[:, arg, :], scans_of(pair, arg)[1], ACT.Copy), "ew_hi_done")
                elif step == "pre" and arg[0] == 1:
                    s = arg[1]
                    wait(act, "pre_mm", nth(pair, 6, 3 + s + 1))
                    wait(act, "ssm_done", nth(pair, 2, 1))
                    for b, c0, n, at in pieces(s):
                        inc(act.activation(zt[b * N:(b + 1) * N, c0:c0 + n], ch(step, arg, pair)[0:N, at:at + n],
                                           ACT.Copy), "z_ev")
                elif step == "split":
                    layer, b = arg
                    own = slice(b * N, (b + 1) * N)
                    wait(act, "ssm_done", nth(pair, 2, layer + 1))
                    if layer == 0:
                        wait(act, "y_mm", nth(pair - 1, 6, 6))
                    else:
                        wait(act, "pre_mm", nth(pair, 6, 6))
                    inc(act.activation(states[own, b, :], t1[own, :], ACT.Copy), "st_hi")
                elif step == "ssm_log":
                    bz = vecs[:, 0:1] if arg == 0 else bias1s[:, 0:1]
                    wait(act, "z_ev", nth(pair, 8, 4 * arg + 4))
                    if arg == 0:
                        wait(act, "row_mm", nth(pair - 1, 1, 1))
                        wait(act, "st_lo", nth(pair - 1, 4, 4))
                    else:
                        wait(act, "st_lo", nth(pair, 4, 2))
                        wait(act, "carry_ev", nth(pair, 1, 1))
                    inc(act.activation(t1[:], zt[:], ACT.Abs, bias=bz), "abs_done")
                    wait(act, "abs_done", nth(pair, 2, arg + 1))
                    inc(act.activation(t1[:], t1[:], ACT.Exp, scale=-1.0), "exp_done")
                    wait(act, "exp_done", nth(pair, 2, arg + 1))
                    inc(act.activation(t1[:], t1[:], ACT.Ln, bias=1.0), "ln_done")
                elif step == "ssm_decay":
                    wait(act, "delta_done", nth(pair, 2, arg + 1))
                    inc(act.activation(zt[:], t2[:], ACT.Exp, scale=nspa[:, arg:arg + 1]), "decay_done")
                elif step == "x2t":
                    t, k = arg
                    wait(act, "x2t_mm", nth(pair, 6, 2 * t + k + 1))
                    if k == 0:
                        wait(act, "up_mm", nth(pair - 1, SLOTS, M * (t + 1)))
                    inc(act.activation(x_hi[:, t, k, :], ch(step, arg, pair)[:, 0:TT], ACT.Copy), "xhi_done")
                elif step == "logit":
                    wait(act, "logit_mm", nth(pair, 3, arg + 1))
                    wait(act, "logt_mm", nth(pair, 3, arg))
                    inc(act.activation(logT[0:LO + E, :], ch(step, arg, pair)[0:LO + E, 0:TT], ACT.Copy), "logit_ev")
                elif step == "logit_t":
                    wait(act, "logit_sum", nth(pair, 3, arg + 1))
                    inc(act.activation(sc[:], sc[:], ACT.Exp, scale=-1.0), "score_exp")

            def ffn(pair, idx):
                wait(act, "gate_mm", nth(pair, SLOTS, idx + 1))
                wait(act, "hid_done", nth(pair, SLOTS, idx - 1))
                inc(act.activation(sg[:, idx % 2, :], g_ps[:, idx % 2, 0:TT], ACT.Silu), "silu_done")

            def ffn_hi(pair, idx):
                wait(act, "hid_done", nth(pair, SLOTS, idx + 1))
                wait(act, "down_mm", nth(pair, SLOTS, idx - 2))
                inc(act.activation(hid_hi[:, idx % 3, :], hid, ACT.Copy), "hi_done")

            def iteration(pair, have_next):
                for idx in range(SLOTS):
                    for step, arg, of in chain_at(idx + 0.0, pair, have_next):
                        chain(step, arg, of)
                    ffn(pair, idx)
                    for step, arg, of in chain_at(idx + 0.5, pair, have_next):
                        chain(step, arg, of)
                    ffn_hi(pair, idx)

            for at in sorted({*CHAIN, *PREPARE}):
                for what, n in PREPARE.get(at, ()):
                    prepare(what, n)
                for step, arg, of in chain_at(at, -1, True, have_this=False):
                    chain(step, arg, of)
            iteration(0, True)
            with act.Fori(1, NP - 1) as i:
                iteration(i, True)
            iteration(NP - 1, False)

        @block.vector
        def _(dve):
            for a in (ws1[:], sbd[:], ge1[:], logT[:], wpad[:]):
                inc(dve.memset(a, 0.0), "zeroed")
            inc(dve.memset(ones, 1.0 / D), "ones_done")
            for g in range(NG):
                dve.memset(winit[:, :, g:g + 1], float(g))
            inc(dve.memset(c09[:], 1.0 - ALPHA), "const_done")
            inc(dve.memset(mhalf[:], -0.5), "const_done")
            dve.wait_ge(S["const_done"], 2)

            def prepare(what, n):
                lo_, hi_ = slice(0, N), slice(N, P)
                if what == "tokw" and n == 0:
                    dve.wait_ge(S["fold_mm"], 1)
                    inc(dve.tensor_scalar(tw_hi[:], fold_ps[0][:, 0:D], 0.5 * ALPHA, None, ALU.mult), "tw_hi_done")
                    dve.wait_ge(S["tw_hi_done"], 1)
                    inc(dve.scalar_tensor_tensor(tw_lo[:], fold_ps[0][:, 0:D], 0.5 * ALPHA, tw_hi[:].bitcast(F32),
                                                 ALU.mult, ALU.subtract), "fold_ev")
                    dve.wait_ge(S["w_tok"], 32)
                elif what == "tokw" and n == 1:
                    dve.wait_ge(S["fold_mm"], 2)
                    means = fold_ps[1][:, 0:P].unsqueeze(1).broadcast_to([P, KD, P])
                    inc(dve.tensor_tensor(wdi0, wdi0, means, ALU.subtract), "fold_ev")
                elif what == "tokw" and n == 2:
                    dve.wait_ge(S["fold_mm"], 3)
                    inc(dve.tensor_scalar(f_hi[:], fold_ps[2][:, 0:P], 0.5 * ALPHA, None, ALU.mult), "f_hi_done")
                    dve.wait_ge(S["f_hi_done"], 1)
                    inc(dve.scalar_tensor_tensor(f_lo[:], fold_ps[2][:, 0:P], 0.5 * ALPHA, f_hi[:].bitcast(F32),
                                                 ALU.mult, ALU.subtract), "fold_ev")
                    inc(dve.tensor_copy(cb0[:], fold_ps[2][:, P:P + 1]), "fold_ev")
                    dve.wait_ge(S["fold_ev"], 4)
                elif what == "fold" and n == 1:
                    dve.wait_ge(S["fold_mm"], 4)
                    inc(dve.tensor_copy(wosT, fold_ps[1].rearrange("p (o k n) -> p o k n", o=2, k=KD)), "fold_ev")
                    dve.wait_ge(S["w_fold"], 16 * W_FOLD)
                    inc(dve.tensor_tensor(bsum[:], bcol[:, :, 0], bcol[:, :, 1], ALU.add), "fold_ev")
                    inc(dve.tensor_tensor(brow[:], brow[:], rows[:, 0, :], ALU.add), "fold_ev")
                    inc(dve.tensor_copy(wo_hi[:], wo_raw), "wo_hi_done")
                    dve.wait_ge(S["wo_hi_done"], 1)
                    inc(dve.tensor_tensor(wo_lo[:], wo_raw, wo_hi[:].bitcast(F32), ALU.subtract), "fold_ev")
                elif what == "fold" and n == 2:
                    dve.wait_ge(S["fold_mm"], 5)
                    dve.wait_ge(S["zeroed"], 2)
                    p0, p1 = fold_ps[2][:, 0:P], fold_ps[2][:, P:2 * P]
                    for dst, src in (
                        (sbd[lo_, 0, lo_], p1[lo_, lo_]), (sbd[hi_, 0, hi_], p0[hi_, lo_]),
                        (sbd[lo_, 1, lo_], p1[lo_, hi_]), (sbd[hi_, 1, hi_], p0[hi_, hi_]),
                        (g_hi[lo_, :], p0[lo_, :]), (g_hi[hi_, :], p1[hi_, :]),
                    ):
                        last = dve.tensor_copy(dst, src)
                    inc(last, "g_hi_done")
                    dve.wait_ge(S["g_hi_done"], 1)
                    for rows_, src in ((lo_, p0), (hi_, p1)):
                        last = dve.tensor_tensor(g_lo[rows_, :], src[rows_, :], g_hi[rows_, :].bitcast(F32),
                                                 ALU.subtract)
                    inc(last, "fold_ev")
                elif what == "fold" and n == 3:
                    dve.wait_ge(S["fold_mm"], 6)
                    dve.wait_ge(S["w_in"], 16 * W_IN)
                    for s, src in enumerate((lo_, hi_)):
                        for dst in (lo_, hi_):
                            last = dve.tensor_tensor(bias1[dst, s:s + 1], fold_ps[3][src, 0:1],
                                                     vecs[src, 2 * s + 1:2 * s + 2], ALU.add)
                    inc(last, "fold_ev")
                elif what == "fold" and n == 4:
                    dve.wait_ge(S["fold_mm"], 7)
                    dve.wait_ge(S["zeroed_rw"], 1)
                    rwT_ps = fold_ps[4][:, 0:KD * E].rearrange("p (k e) -> p k e", k=KD)
                    inc(dve.tensor_copy(rw[:, :, 0:E], rwT_ps), "rw_hi_done")
                    dve.wait_ge(S["rw_hi_done"], 1)
                    inc(dve.tensor_tensor(rw[:, :, LO:LO + E], rwT_ps, rw[:, :, 0:E].bitcast(F32), ALU.subtract),
                        "fold_ev")
                elif what == "softplus":
                    dve.wait_ge(S["spa"], 3)
                    inc(dve.tensor_scalar(spt[:, 2:4], vecs[:, 4:6], 0.0, None, ALU.max), "spa_dve")
                    dve.wait_ge(S["spa_dve"], 1)
                    inc(dve.tensor_tensor(spt[:, 2:4], spt[:, 2:4], spt[:, 0:2], ALU.add), "spa_dve")
                    dve.wait_ge(S["spa_dve"], 2)
                    inc(dve.tensor_scalar(nspa[:], spt[:, 2:4], -1.0, None, ALU.mult), "spa_dve")
                elif what == "shared":
                    hi_p, lo_p = shared_part(n)
                    dve.wait_ge(S["shared_mm"], n + 1)
                    inc(dve.tensor_copy(hi_p, shared_view(n)), "shared_hi")
                    dve.wait_ge(S["shared_hi"], n + 1)
                    inc(dve.tensor_tensor(lo_p, shared_view(n), hi_p.bitcast(F32), ALU.subtract), "shared_lo")
                elif what == "staged":
                    dve.wait_ge(S["routed_lo"], 2 * NT)

            def routed(ins, pair, tile, n):
                inc(ins, "route")
                wait(dve, "route", nth(pair, 3 * NROUTE, NROUTE * tile + n))

            def chain(step, arg, pair):
                if step == "ewma":
                    b = arg
                    x_b, fw_b = scans_of(pair, b)
                    wait(dve, f"x_in{b}", nth(pair, 16, 16))
                    inc(dve.tensor_scalar(ends10[:, b, :], x_b[:, 0:T:T - 1], 1.0 / ALPHA, None, ALU.mult),
                        "ends_done")
                    wait(dve, "ends_done", nth(pair, 2, b + 1))
                    if not is_first(pair):
                        wait(dve, "ew_lo_done", nth(pair, 2, b))
                    decay = c09[:, 0:1].broadcast_to([P, T])
                    inc(dve.tensor_tensor_scan(fw_b, decay, x_b, ends10[:, b, 0:1],
                                               ALU.mult, ALU.add), "scan_done")
                    wait(dve, "scan_done", nth(pair, 4, 2 * b + 1))
                    inc(dve.tensor_tensor_scan(x_b[:, T - 1::-1], decay, x_b[:, T - 1::-1],
                                               ends10[:, b, 1:2], ALU.mult, ALU.add), "scan_done")
                    if is_first(pair):
                        wait(dve, "scan_done", nth(pair, 4, 2 * b + 2))
                        inc(dve.tensor_tensor(fw_b, fw_b, x_b, ALU.add), "ew_done")
                elif step == "tok":
                    wait(dve, "tok_mm", nth(pair, 6, arg + 1))
                    wait(dve, "y_ev", nth(pair - 1, 6, arg + 1))
                    hv = h_tok[:, 2 * arg:2 * arg + 2, :]
                    inc(dve.tensor_tensor(hv, ch(step, arg, pair)[0:TP, :].rearrange("p (j d) -> p j d", d=D),
                                          tokb_bc[:, :].unsqueeze(1).broadcast_to([TP, 2, D]), ALU.add), "tok_ev")
                    wait(dve, "tok_ev", nth(pair, 6, arg + 1))
                    if arg % 2 == 0:
                        wait(dve, "aggr1", nth(pair, NT * NAGGR, NAGGR * (arg // 2)))
                    for j in range(2):
                        inc(dve.bn_stats(stats[0][:, (2 * arg + j) % SUB, :], hv[:, j, :]), "st1")
                elif step in ("ln1_stats", "ln2_stats"):
                    n = int(step[2]) - 1
                    wait(dve, f"st{n + 1}", nth(pair, NJ, SUB * (arg + 1)))
                    wait(dve, "rstd1" if n == 0 else "xn2", nth(pair, 3, arg))
                    st, sq, a = stats[n], halves[n], f"aggr{n + 1}"
                    v0 = NAGGR * arg
                    inc(dve.tensor_tensor(mv[n][:, :, 0], st[:, :, 1], st[:, :, 4], ALU.add), a)
                    inc(dve.tensor_tensor(sq[:, :, 0], st[:, :, 1], st[:, :, 4], ALU.subtract), a)
                    inc(dve.tensor_tensor(sq[:, :, 1], st[:, :, 2], st[:, :, 5], ALU.add), a)
                    wait(dve, a, nth(pair, NT * NAGGR, v0 + 3))
                    inc(dve.tensor_scalar(mv[n][:, :, 0], mv[n][:, :, 0], 0.5, None, ALU.mult), a)
                    inc(dve.scalar_tensor_tensor(sq[:, :, 0], sq[:, :, 0], 0.25, sq[:, :, 0], ALU.mult, ALU.mult), a)
                    inc(dve.tensor_scalar(sq[:, :, 1], sq[:, :, 1], 1.0 / D, EPS, ALU.mult, ALU.add), a)
                    wait(dve, a, nth(pair, NT * NAGGR, v0 + 6))
                    inc(dve.tensor_tensor(mv[n][:, :, 1], sq[:, :, 1], sq[:, :, 0], ALU.add), a)
                elif step == "ln2_norm":
                    wait(dve, "rstd2", nth(pair, 3, arg + 1))
                    wait(dve, "x2t_mm", nth(pair, 6, 2 * arg))
                    for j in range(SUB):
                        last = dve.tensor_scalar(xn2[:, j, :], h2[:, arg * SUB + j, :], mv[1][:, j, 0:1],
                                                 rstd[1][:, j:j + 1], ALU.subtract, ALU.mult)
                    inc(last, "xn2")
                elif step == "pre":
                    layer, s = arg
                    wait(dve, "pre_mm", nth(pair, 6, 3 * layer + s + 1))
                    wait(dve, "ssm_done", nth(pair, 2, layer))
                    if layer == 0:
                        wait(dve, f"rb{s}", nth(pair, 16, 16))
                    for b, c0, n, at in pieces(s):
                        for dst, src, name in ((zt, slice(0, N), "z_ev"), (ut, slice(N, P), "u_ev")):
                            out_, in_ = dst[b * N:(b + 1) * N, c0:c0 + n], ch(step, arg, pair)[src, at:at + n]
                            if layer == 0:
                                inc(dve.scalar_tensor_tensor(out_, in_, cb0[src, :], rb[s][src, at:at + n],
                                                             ALU.add, ALU.mult), name)
                            elif name == "u_ev":
                                inc(dve.tensor_copy(out_, in_), name)
                elif step == "ssm_log":
                    bz = vecs[:, 0:1] if arg == 0 else bias1s[:, 0:1]
                    wait(dve, "z_ev", nth(pair, 8, 4 * arg + 4))
                    if arg == 1:
                        wait(dve, "carry_ev", nth(pair, 1, 1))
                    if arg == 0:
                        wait(dve, "u_ev", nth(pair, 8, 4))
                    inc(dve.tensor_scalar(t2[:], zt[:], bz, 0.0, ALU.add, ALU.max), "relu_done")
                elif step == "ssm_decay":
                    wait(dve, "ln_done", nth(pair, 2, arg + 1))
                    wait(dve, "relu_done", nth(pair, 2, arg + 1))
                    inc(dve.tensor_tensor(t2[:], t1[:], t2[:], ALU.add), "delta_done")
                    bu = vecs[:, 2:3] if arg == 0 else bias1s[:, 1:2]
                    wait(dve, "delta_done", nth(pair, 2, arg + 1))
                    wait(dve, "u_ev", nth(pair, 8, 4 * arg + 4))
                    inc(dve.scalar_tensor_tensor(ut[:], ut[:], bu, t2[:], ALU.add, ALU.mult), "drive_done")
                elif step == "ssm_scan":
                    wait(dve, "decay_done", nth(pair, 2, arg + 1))
                    wait(dve, "drive_done", nth(pair, 2, arg + 1))
                    inc(dve.tensor_tensor_scan(t1[:], zt[:], ut[:], 0.0,
                                               ALU.mult, ALU.add), "ssm_done")
                elif step == "split":
                    layer, b = arg
                    own, other = slice(b * N, (b + 1) * N), slice((1 - b) * N, (2 - b) * N)
                    wait(dve, "st_hi", nth(pair, 4, 2 * layer + b + 1))
                    inc(dve.tensor_tensor(states[other, b, :], t1[own, :], states[own, b, :].bitcast(F32),
                                          ALU.subtract), "st_lo")
                elif step == "carry":
                    wait(dve, "carry_mm", nth(pair, 1, 1))
                    inc(dve.tensor_tensor(bias1s[:], ch(step, arg, pair)[:, 0:2], bias1[:], ALU.add), "carry_ev")
                elif step == "class_row":
                    wait(dve, "row_mm", nth(pair, 1, 1))
                    wait(dve, "res_done", nth(pair - 1, 6, 6))
                    inc(dve.tensor_tensor(rows[:], ch(step, arg, pair)[0:TP, :].rearrange("p (b d) -> p b d", b=2),
                                          brow[:, :].unsqueeze(1).broadcast_to([TP, 2, D]), ALU.add), "row_ev")
                elif step == "y":
                    t, q = arg
                    j = t * SUB + 2 * q
                    wait(dve, "y_mm", nth(pair, 6, 2 * t + q + 1))
                    wait(dve, "res_done", nth(pair, 6, 2 * t + q + 1))
                    if not is_first(pair):
                        dve.wait_ge(OUT[t], nth(pair, 16, 0))
                    hv = h2[:, j:j + 2, :]
                    inc(dve.tensor_tensor(hv, ch(step, arg, pair)[0:TP, :].rearrange("p (j d) -> p j d", d=D),
                                          h_tok[:, j:j + 2, :], ALU.add), "y_ev")
                    wait(dve, "y_ev", nth(pair, 6, 2 * t + q + 1))
                    if q == 0:
                        wait(dve, "aggr2", nth(pair, NT * NAGGR, NAGGR * t))
                    for n in range(2):
                        inc(dve.bn_stats(stats[1][:, 2 * q + n, :], hv[:, n, :]), "st2")
                elif step == "x2t":
                    t, k = arg
                    wait(dve, "xhi_done", nth(pair, 6, 2 * t + k + 1))
                    inc(dve.tensor_tensor(x_lo[:, t, k, :], ch(step, arg, pair)[:, 0:TT], x_hi[:, t, k, :].bitcast(F32),
                                          ALU.subtract), "xlo_done")
                elif step == "logit_t":
                    wait(dve, "logt_mm", nth(pair, 3, arg + 1))
                    wait(dve, "route", nth(pair, 3 * NROUTE, NROUTE * arg))
                    both = ch(step, arg, pair)[0:TP, :].rearrange("p (j e) -> p j e", j=SUB)
                    inc(dve.tensor_copy(sc[:, :].rearrange("p (j e) -> p j e", e=E), both[:, :, LO:LO + E]),
                        "logit_half")
                    wait(dve, "logit_half", nth(pair, 3, arg + 1))
                    inc(dve.tensor_tensor(sc[:, :].rearrange("p (j e) -> p j e", e=E), both[:, :, 0:E],
                                          sc[:, :].rearrange("p (j e) -> p j e", e=E), ALU.add), "logit_sum")
                elif step == "route_scores":
                    base = ROUTE["scores"]
                    wait(dve, "score_exp", nth(pair, 3, arg + 1))
                    routed(dve.tensor_scalar(sc[:], sc[:], 1.0, None, ALU.add), pair, arg, base + 1)
                    routed(dve.reciprocal(sc[:], sc[:]), pair, arg, base + 2)
                    routed(dve.tensor_tensor(sbias[:, :].rearrange("p (j e) -> p j e", e=E),
                                             sc[:, :].rearrange("p (j e) -> p j e", e=E),
                                             corr_bc[:, :].unsqueeze(1).broadcast_to([TP, SUB, E]), ALU.add),
                           pair, arg, base + 3)
                    s4 = sbias[:, :].rearrange("p (g e) -> p g e", e=EG)
                    n0 = 0
                    for d in range(1, EG):
                        inc(dve.tensor_tensor(pairs6[:, :, n0:n0 + EG - d], s4[:, :, 0:EG - d], s4[:, :, d:EG],
                                              ALU.add), "route")
                        n0 += EG - d
                    wait(dve, "route", nth(pair, 3 * NROUTE, NROUTE * arg + base + 6))
                    routed(dve.tensor_reduce(gs[:, :, :].rearrange("p j g -> p (j g)"), pairs6[:], AX.X, ALU.max),
                           pair, arg, base + 7)
                    inc(dve.tensor_tensor(ge1[:, :, 0:3], gs[:, :, 0:3], gs[:, :, 1:4], ALU.is_ge), "route")
                    inc(dve.tensor_tensor(ge2[:], gs[:, :, 0:2], gs[:, :, 2:4], ALU.is_ge), "route")
                    inc(dve.tensor_tensor(ge3[:], gs[:, :, 0:1], gs[:, :, 3:4], ALU.is_ge), "route")
                elif step == "route_groups":
                    base = ROUTE["groups"]
                    wait(dve, "route", nth(pair, 3 * NROUTE, NROUTE * arg + base))
                    steps = ((slice(0, 4), winit[:], ge1[:], ALU.add),
                             (slice(1, 4), None, ge1[:, :, 0:3], ALU.subtract), (slice(0, 2), None, ge2[:], ALU.add),
                             (slice(2, 4), None, ge2[:], ALU.subtract), (slice(0, 1), None, ge3[:], ALU.add),
                             (slice(3, 4), None, ge3[:], ALU.subtract))
                    for n, (s, a, b, op) in enumerate(steps):
                        routed(dve.tensor_tensor(wins[:, :, s], wins[:, :, s] if a is None else a, b, op),
                               pair, arg, base + n + 1)
                    routed(dve.tensor_scalar(gmask[:], wins[:, :, :].rearrange("p j g -> p (j g)"), 2.0, None,
                                             ALU.is_ge), pair, arg, base + 7)
                    routed(dve.tensor_scalar(gpen[:], gmask[:], 1.0, BIG, ALU.subtract, ALU.mult),
                           pair, arg, base + 8)
                elif step == "route_pick":
                    base = ROUTE["pick"]
                    gm = gmask[:, :].unsqueeze(2).broadcast_to([TP, SUB * NG, EG])
                    gp = gpen[:, :].unsqueeze(2).broadcast_to([TP, SUB * NG, EG])
                    m4 = masked[:, :].rearrange("p (g e) -> p g e", e=EG)
                    s4 = sbias[:, :].rearrange("p (g e) -> p g e", e=EG)
                    routed(dve.tensor_tensor(m4, s4, gm, ALU.mult), pair, arg, base + 1)
                    routed(dve.tensor_tensor(m4, m4, gp, ALU.add), pair, arg, base + 2)
                    inc(dve.memset(marks[:, :, 4:8], -BIG), "route")
                    for j in range(SUB):
                        last = dve.max(top8[:, j, :], masked[:, j * E:(j + 1) * E])
                    routed(last, pair, arg, base + 4)
                    routed(dve.tensor_copy(marks[:, :, 0:4], top8[:, :, 0:4]), pair, arg, base + 5)
                    inc(dve.tensor_tensor(gscore.rearrange("p (g e) -> p g e", e=EG),
                                          sc[:, :].rearrange("p (g e) -> p g e", e=EG), gm, ALU.mult), "route")
                    for j in range(SUB):
                        last = dve.match_replace(marked[:, j * E:(j + 1) * E], marks[:, j, :],
                                                 masked[:, j * E:(j + 1) * E], BIG)
                    routed(last, pair, arg, base + 7)
                    inc(dve.scalar_tensor_tensor(wsel, marked[:, :].rearrange("p (j e) -> p j e", e=E), BIG,
                                                 gscore.rearrange("p (j e) -> p j e", e=E), ALU.is_equal, ALU.mult),
                        "route")
                elif step == "route_weights":
                    base = ROUTE["weights"]
                    wait(dve, "route", nth(pair, 3 * NROUTE, NROUTE * arg + base))
                    routed(dve.tensor_reduce(wsum[:], wsel, AX.X, ALU.add), pair, arg, base + 1)
                    routed(dve.tensor_scalar(wsum[:], wsum[:], 1e-20, None, ALU.add), pair, arg, base + 2)
                    routed(dve.reciprocal(wsum[:], wsum[:]), pair, arg, base + 3)
                    routed(dve.tensor_tensor(wsel, wsel, wsum[:, :].unsqueeze(2).broadcast_to([TP, SUB, E]),
                                             ALU.mult), pair, arg, base + 4)
                    wait(dve, "comb_st", nth(pair, 64 * NT, 64 * arg))
                    inc(dve.transpose(wT[:, :, :].rearrange("p j e -> p (j e)"),
                                      wpad[:, :, :].rearrange("p j e -> p (j e)")), "comb_tr")

            def ffn(pair, idx):
                t, m = divmod(idx, M)
                if m >= MS:
                    r = m - MS
                    wait(dve, f"cb{r % RING}", nth(pair, 32 * NT * MR // RING,
                                                   32 * ((t * MR + r) // RING + 1)))
                    wait(dve, "silu_done", nth(pair, SLOTS, idx + 1))
                    inc(dve.tensor_tensor(sg[:, idx % 2, :], sg[:, idx % 2, :], cb[:, r % RING, :], ALU.mult), "t_done")
                    wait(dve, "t_done", nth(pair, NT * MR, t * MR + m - MS + 1))
                else:
                    wait(dve, "silu_done", nth(pair, SLOTS, idx + 1))
                wait(dve, "up_mm", nth(pair, SLOTS, idx + 1))
                wait(dve, "lo_done", nth(pair, SLOTS, idx))
                inc(dve.tensor_tensor(hid, sg[:, idx % 2, :], u_ps[:, idx % 2, 0:TT], ALU.mult),
                    "hid_done")

            def finish(pair, t):
                wait(dve, "down_mm", nth(pair, SLOTS, M * (t + 1)))
                for q in range(2):
                    hv = h2[:, t * SUB + 2 * q:t * SUB + 2 * q + 2, :]
                    inc(dve.tensor_tensor(hv, d_ps[0:TP, 2 * q:2 * q + 2, :], hv, ALU.add), "fin_done")

            def iteration(pair, have_next, first=False):
                for idx in range(SLOTS):
                    for half in (0.0, 0.5):
                        for step, arg, of in chain_at(idx + half, pair, have_next):
                            chain(step, arg, of)
                    ffn(pair, idx)
                    if idx % M == 1 and idx > M:
                        finish(pair, idx // M - 1)
                    elif idx == 1 and not first:
                        finish(pair - 1, NT - 1)

            for at in sorted({*CHAIN, *PREPARE}):
                for what, n in PREPARE.get(at, ()):
                    prepare(what, n)
                for step, arg, of in chain_at(at, -1, True, have_this=False):
                    chain(step, arg, of)
            iteration(0, True, first=True)
            with dve.Fori(1, NP - 1) as i:
                iteration(i, True)
            iteration(NP - 1, False)
            finish(NP - 1, NT - 1)

        @block.tensor
        def _(pe):
            pe.wait_ge(S["ident_done"], 2)

            def prepare(what, n):
                if what == "tokw":
                    bank = fold_ps[n]
                    if n == 0:
                        pe.wait_ge(S["w_tok"], 32)
                        for k in range(KD):
                            last = pe.transpose(bank[:, k * P:(k + 1) * P], wraw[:, k, :], ident[:])
                    elif n == 1:
                        pe.wait_ge(S["w_pre"], 48)
                        pe.wait_ge(S["ones_done"], 1)
                        for k in range(KD):
                            last = pe.matmul(bank[:, 0:P], ones, wdi0[:, k, :], start=(k == 0), stop=(k == KD - 1))
                    else:
                        pe.wait_ge(S["fold_ev"], 2)
                        for k in range(KD):
                            pe.matmul(bank[:, 0:P], wraw[:, k, :], wdi0[:, k, :], start=(k == 0), stop=(k == KD - 1))
                        for k in range(KD):
                            last = pe.matmul(bank[:, P:P + 1], wdi0[:, k, :], tokb_col[:, k:k + 1],
                                             start=(k == 0), stop=(k == KD - 1))
                    inc(last, "fold_mm")
                elif what == "fold":
                    bank = fold_ps[n]
                    if n == 1:
                        pe.wait_ge(S["w_fold"], 16 * W_FOLD)
                        pe.wait_ge(S["fold_ev"], 4)
                        for o in range(2):
                            for k in range(KD):
                                last = pe.transpose(bank[:, (2 * o + k) * P:(2 * o + k + 1) * P],
                                                    wos[:, o, k * P:(k + 1) * P], ident[:])
                    elif n == 2:
                        pe.wait_ge(S["fold_ev"], 5)
                        for o in range(2):
                            for k in range(KD):
                                last = pe.matmul(bank[:, o * P:(o + 1) * P], wosT[:, o, k, :], wdi1[:, k, :],
                                                 start=(k == 0), stop=(k == KD - 1))
                    elif n == 3:
                        pe.wait_ge(S["fold_ev"], 6)
                        for k in range(KD):
                            last = pe.matmul(bank[:, 0:1], wdi1[:, k, :], bsum[:, k:k + 1],
                                             start=(k == 0), stop=(k == KD - 1))
                    else:
                        for k in range(KD):
                            last = pe.transpose(bank[:, k * E:(k + 1) * E], rraw[:, k * P:(k + 1) * P],
                                                ident[0:E, 0:E])
                    inc(last, "fold_mm")
                elif what == "shared":
                    pe.wait_ge(S["fold_ev"], (5, 5, 9, 10, 11, 11)[n])
                    pe.wait_ge(S[f"w_shared{n // KD % 2}"], 16 * (n // (2 * KD) + 1))
                    raw, k = sh_raw[n // KD], n % KD
                    for m in range(MS):
                        a = (raw.rearrange("p (m c) -> p m c", m=MS)[:, m, k * P:(k + 1) * P] if n < 2 * KD
                             else raw.rearrange("p (k n) -> p k n", k=KD)[:, k, m * P:(m + 1) * P])
                        last = pe.transpose(shared_ps[n][:, m * P:(m + 1) * P], a, ident[:])
                    inc(last, "shared_mm")

            def chain(step, arg, pair):
                if step not in PE_STEPS:
                    return
                place, ch_ps = bank(step, arg, pair), ch(step, arg, pair)
                if last_in[place] is not None:
                    for name, value in reads_of(*last_in[place]):
                        wait(pe, name, value)
                last_in[place] = (step, arg, pair)
                if step == "tok":
                    if arg % 3 == 0:
                        wait(pe, "ew_lo_done", nth(pair, 2, arg // 3 + 1))
                    for n in range(2):
                        b, c0 = cols(2 * arg + n)
                        for m, (e, w) in enumerate(((ew_hi, tw_hi), (ew_hi, tw_lo), (ew_lo, tw_hi))):
                            last = pe.matmul(ch_ps[0:TP, n * D:(n + 1) * D], e[:, b, c0:c0 + TP], w[:],
                                             start=(m == 0), stop=(m == 2))
                    inc(last, "tok_mm")
                elif step == "x2t":
                    t, k = arg
                    wait(pe, "xn2", nth(pair, 3, t + 1))
                    for j in range(SUB):
                        last = pe.transpose(ch_ps[:, j * TP:(j + 1) * TP], xn2[:, j, k * P:(k + 1) * P],
                                            ident[0:TP, 0:TP])
                    inc(last, "x2t_mm")
                elif step == "pre":
                    layer, s = arg
                    if layer == 0:
                        wait(pe, "ew_lo_done", nth(pair, 2, 1 if s == 0 else 2))
                    else:
                        wait(pe, "st_lo", nth(pair, 4, 1 if s == 0 else 2))
                    for b, c0, n, at in pieces(s):
                        if layer == 0:
                            for m, (w, e) in enumerate(((f_hi, ew_hi), (f_lo, ew_hi), (f_hi, ew_lo))):
                                last = pe.matmul(ch_ps[:, at:at + n], w[:], e[:, b, c0:c0 + n],
                                                 start=(m == 0), stop=(m == 2))
                        else:
                            for w in (g_hi, g_lo):
                                last = pe.matmul(ch_ps[:, at:at + n], w[:], states[:, b, c0:c0 + n],
                                                 start=(w is g_hi), stop=(w is g_lo))
                    inc(last, "pre_mm")
                elif step == "carry":
                    wait(pe, "ssm_done", nth(pair, 2, 1))
                    for s in range(2):
                        last = pe.matmul(ch_ps[:, s:s + 1], sbd[:, s, :], t1[:, T - 1:T], start=True, stop=True)
                    inc(last, "carry_mm")
                elif step == "class_row":
                    wait(pe, "ssm_done", nth(pair, 2, 2))
                    for b in range(2):
                        last = pe.matmul(ch_ps[0:TP, b * D:(b + 1) * D],
                                         t1[:, T - 1:T].broadcast_to([P, TP]), ws1[:, b, :],
                                         start=True, stop=True)
                    inc(last, "row_mm")
                elif step == "y":
                    t, q = arg
                    wait(pe, "st_lo", nth(pair, 4, 3 if t == 0 else 4))
                    for n in range(2):
                        b, c0 = cols(t * SUB + 2 * q + n)
                        for w in (wo_hi, wo_lo):
                            last = pe.matmul(ch_ps[0:TP, n * D:(n + 1) * D], states[:, b, c0:c0 + TP], w[:],
                                             start=(w is wo_hi), stop=(w is wo_lo))
                    inc(last, "y_mm")
                elif step == "logit":
                    wait(pe, "xlo_done", nth(pair, 6, 2 * arg + 2))
                    parts = ((x_hi, 0, LO + E), (x_lo, 0, E), (x_lo, 1, E), (x_hi, 1, LO + E))
                    for n, (xx, k, e1) in enumerate(parts):
                        last = pe.matmul(ch_ps[0:e1, 0:TT], rw[:, k, 0:e1], xx[:, arg, k, :], start=(n == 0),
                                         stop=(n == len(parts) - 1), skip_group_check=True)
                    inc(last, "logit_mm")
                elif step == "logit_t":
                    wait(pe, "logit_ev", nth(pair, 3, arg + 1))
                    for j in range(SUB):
                        last = pe.transpose(ch_ps[0:TP, j * P:(j + 1) * P], logT[:, j * TP:(j + 1) * TP], ident[:])
                    inc(last, "logt_mm")

            def down(pair, idx):
                t, m = divmod(idx, M)
                wait(pe, "lo_done", nth(pair, SLOTS, idx + 1))
                if m == 0:
                    wait(pe, "fin_done", nth(pair, 2 * NT, 2 * t))
                hh, hl = hid_hi[:, idx % 3, :], hid_lo[:, idx % 3, :]
                for j in range(SUB):
                    tc = slice(j * TP, (j + 1) * TP)
                    for n, (a, w) in enumerate(((hh, down_hi), (hh, down_lo), (hl, down_hi))):
                        last = pe.matmul(d_ps[0:TP, j, :], a[:, tc], w[:, m, :],
                                         start=(m == 0 and n == 0 and j % 2 == 0),
                                         stop=(m == M - 1 and n == 2), skip_group_check=True)
                inc(last, "down_mm")

            def ffn(pair, idx, before):
                t, m = divmod(idx, M)

                def product(bank, hi_w, lo_w):
                    ms = slice(m * P, (m + 1) * P)
                    for k in range(KD):
                        for n, (w, xx) in enumerate(((hi_w, x_hi), (hi_w, x_lo), (lo_w, x_hi))):
                            last = pe.matmul(bank, w[:, k, ms], xx[:, t, k, :], start=(k == 0 and n == 0),
                                             stop=(k == KD - 1 and n == 2))
                    return last

                if m == 0:
                    wait(pe, "xlo_done", nth(pair, 6, 2 * t + 2))
                wait(pe, "silu_done", nth(pair, SLOTS, idx - 1))
                inc(product(g_ps[:, idx % 2, 0:TT], gate_hi, gate_lo), "gate_mm")
                for step, arg, of in before:
                    chain(step, arg, of)
                wait(pe, "hid_done", nth(pair, SLOTS, idx - 1))
                inc(product(u_ps[:, idx % 2, 0:TT], up_hi, up_lo), "up_mm")

            def iteration(pair, have_next, first=False):
                for idx in range(SLOTS):
                    for step, arg, of in chain_at(idx + 0.0, pair, have_next):
                        chain(step, arg, of)
                    ffn(pair, idx, list(chain_at(idx + 0.5, pair, have_next)))
                    if idx >= LAG:
                        down(pair, idx - LAG)
                    elif not first:
                        down(pair - 1, SLOTS + idx - LAG)

            for at in sorted({*CHAIN, *PREPARE}):
                for what, n in PREPARE.get(at, ()):
                    prepare(what, n)
                for step, arg, of in chain_at(at, -1, True, have_this=False):
                    chain(step, arg, of)
            iteration(0, True, first=True)
            with pe.Fori(1, NP - 1) as i:
                banks_at_loop(i)
                iteration(i, True)
            banks_at_loop(NP - 1)
            iteration(NP - 1, False)
            for n in range(LAG):
                down(NP - 1, SLOTS + n - LAG)


_INS = ["x", "L0_tok_W", "L0_tok_b", "L0_attn_Wd", "L0_attn_bd", "L0_attn_Wi", "L0_attn_bi", "L0_attn_A_log",
        "L0_attn_Wo", "L0_attn_bo", "L0_attn_Ws", "L0_attn_bs", "L0_ffn_router_w", "L0_ffn_correction_bias",
        "L0_ffn_gate_w", "L0_ffn_up_w", "L0_ffn_down_w", "L0_ffn_shared_gate_w", "L0_ffn_shared_up_w",
        "L0_ffn_shared_down_w"]


def kernel(**inputs):
    import numpy as _np
    import concourse.bacc as _bacc
    from concourse import mybir as _mybir
    from concourse.bass_utils import run_bass_kernel_spmd as _run

    nc = _bacc.Bacc("TRN2", target_bir_lowering=False, num_devices=1)
    arrays, args = {}, []
    for name in _INS:
        a = _np.ascontiguousarray(inputs[name])
        arrays[f"in_{name}_dram"] = a
        args.append(nc.dram_tensor(f"in_{name}_dram", a.shape, _mybir.dt.from_np(a.dtype), kind="ExternalInput").ap())
    shape = (inputs["x"].shape[0], inputs["x"].shape[2], inputs["L0_tok_W"].shape[0])
    args.append(nc.dram_tensor("out_0_dram", shape, _mybir.dt.float32, kind="ExternalOutput").ap())
    audio_tower_kernel(nc, *args)
    r = _run(nc, [arrays], core_ids=[0])
    return r.results[0]["out_0_dram"]
```
